# Optimizing a Trainium2 kernel written in Bass

```python
import numpy as np
import jax
import jax.numpy as jnp

def _softmax(x, axis=-1):
    return jax.nn.softmax(x, axis=axis)

def _gelu(x):
    return jax.nn.gelu(x, approximate=True)

def _silu(x):
    return jax.nn.silu(x)

def _sigmoid(x):
    return jax.nn.sigmoid(x)

def _layernorm(x, axis=-1, eps=1e-05):
    m = jnp.mean(x, axis=axis, keepdims=True)
    v = jnp.var(x, axis=axis, keepdims=True)
    return (x - m) / jnp.sqrt(v + eps)

def _scatter_add(tgt, idx, src, axis=0):
    return tgt.at[idx].add(src)

def _segment_sum(src, seg, n):
    return jax.ops.segment_sum(src, seg, n)
kernel_name = 'mk_early_fusion_d1_tok_img1024_r4_8daf4b'

def setup_inputs(seed: int=0):
    np.random.seed(seed)
    _w = jnp.asarray

    def _rec_inputs():
        import jax
        import jax.numpy as jnp
        _rk = jax.random.key(seed)
        x = -0.00016672 + 0.999947 * jax.random.normal(jax.random.fold_in(_rk, 1), (32, 3, 96, 96), jnp.float32)
        txt = 0.00140885 + 1.4139 * jax.random.normal(jax.random.fold_in(_rk, 2), (32, 32, 256), jnp.float32)
        return (x, txt)
    x, txt = _rec_inputs()

    def _L0_tok_setup():
        import jax, jax.numpy as jnp
        import numpy as np
        B, C, H, W = (64, 3, 96, 96)
        P = 16
        NP = H // P * (W // P)
        PD = C * P * P
        ED = 256
        NCLS = 1

        def _layernorm(x, g, b, eps=1e-05):
            mu = jnp.mean(x, axis=-1, keepdims=True)
            var = jnp.mean(jnp.square(x - mu), axis=-1, keepdims=True)
            return (x - mu) * jax.lax.rsqrt(var + eps) * g + b
        key = jax.random.key(seed)
        ks = jax.random.split(key, 8)
        x = jax.random.normal(ks[0], (B, C, H, W), dtype=jnp.float32)
        ln1_g = jnp.ones((PD,), jnp.float32)
        ln1_b = jnp.zeros((PD,), jnp.float32)
        W_proj = jax.random.normal(ks[1], (PD, ED), jnp.float32) / np.sqrt(PD)
        b_proj = jnp.zeros((ED,), jnp.float32)
        ln2_g = jnp.ones((ED,), jnp.float32)
        ln2_b = jnp.zeros((ED,), jnp.float32)
        cls_token = jax.random.normal(ks[2], (1, NCLS, ED), jnp.float32)
        pos_emb = jax.random.normal(ks[3], (1, NP + NCLS, ED), jnp.float32)
        return {'x': x, 'ln1_g': ln1_g, 'ln1_b': ln1_b, 'W_proj': W_proj, 'b_proj': b_proj, 'ln2_g': ln2_g, 'ln2_b': ln2_b, 'cls_token': cls_token, 'pos_emb': pos_emb}
    _L0_tok_all = _L0_tok_setup()
    _L0_tok_in = {k: v for k, v in _L0_tok_all.items() if k in ('ln1_g', 'ln1_b', 'W_proj', 'b_proj', 'ln2_g', 'ln2_b', 'cls_token', 'pos_emb')}
    del _L0_tok_all

    def _L0_attn_setup():
        import jax, jax.numpy as jnp
        import numpy as np
        B, S, D = (2, 512, 256)
        H, P = (16, 64)
        NUM_OUT = 256
        key = jax.random.key(seed)
        ks = jax.random.split(key, 9)
        sc = 0.05
        return {'x': jax.random.normal(ks[0], (B, S, D), jnp.float32), 'q_w': jax.random.normal(ks[1], (H, P, D), jnp.float32) * sc, 'q_b': jax.random.normal(ks[2], (H, 1, P), jnp.float32) * sc, 'k_w': jax.random.normal(ks[3], (H, P, D), jnp.float32) * sc, 'k_b': jax.random.normal(ks[4], (H, 1, P), jnp.float32) * sc, 'v_w': jax.random.normal(ks[5], (H, P, D), jnp.float32) * sc, 'v_b': jax.random.normal(ks[6], (H, 1, P), jnp.float32) * sc, 'l_w': jax.random.normal(ks[7], (NUM_OUT, P * H), jnp.float32) * sc, 'l_b': jax.random.normal(ks[8], (1, NUM_OUT), jnp.float32) * sc}
    _L0_attn_all = _L0_attn_setup()
    _L0_attn_in = {k: v for k, v in _L0_attn_all.items() if k in ('q_w', 'q_b', 'k_w', 'k_b', 'v_w', 'v_b', 'l_w', 'l_b')}
    del _L0_attn_all

    def _L0_ffn_setup():
        import jax, jax.numpy as jnp
        import numpy as np
        import math
        N_EXP = 8
        TOP_K = 2
        CAPACITY_FACTOR = 1.25

        def _capacity(num_tokens):
            cap = math.floor(TOP_K * CAPACITY_FACTOR * num_tokens / N_EXP)
            cap += cap % 2
            return int(cap)
        key = jax.random.key(seed)
        k1, k2, k3, k4 = jax.random.split(key, 4)
        B, C, d = (4, 256, 256)
        x = jax.random.normal(k1, (B, C, d), dtype=jnp.float32)
        w_g = jax.random.normal(k2, (d, N_EXP), dtype=jnp.float32) * 0.02
        c_fc = jax.random.normal(k3, (N_EXP, d, 4 * d), dtype=jnp.float32) * 0.02
        c_proj = jax.random.normal(k4, (N_EXP, 4 * d, d), dtype=jnp.float32) * 0.02
        return {'x': x, 'w_g': w_g, 'c_fc': c_fc, 'c_proj': c_proj}
    _L0_ffn_all = _L0_ffn_setup()
    _L0_ffn_in = {k: v for k, v in _L0_ffn_all.items() if k in ('w_g', 'c_fc', 'c_proj')}
    del _L0_ffn_all
    return {'x': x, 'txt': txt, 'L0_tok_ln1_g': _L0_tok_in['ln1_g'], 'L0_tok_ln1_b': _L0_tok_in['ln1_b'], 'L0_tok_W_proj': _L0_tok_in['W_proj'], 'L0_tok_b_proj': _L0_tok_in['b_proj'], 'L0_tok_ln2_g': _L0_tok_in['ln2_g'], 'L0_tok_ln2_b': _L0_tok_in['ln2_b'], 'L0_tok_cls_token': _L0_tok_in['cls_token'], 'L0_tok_pos_emb': _L0_tok_in['pos_emb'], 'L0_attn_q_w': _L0_attn_in['q_w'], 'L0_attn_q_b': _L0_attn_in['q_b'], 'L0_attn_k_w': _L0_attn_in['k_w'], 'L0_attn_k_b': _L0_attn_in['k_b'], 'L0_attn_v_w': _L0_attn_in['v_w'], 'L0_attn_v_b': _L0_attn_in['v_b'], 'L0_attn_l_w': _L0_attn_in['l_w'], 'L0_attn_l_b': _L0_attn_in['l_b'], 'L0_ffn_w_g': _L0_ffn_in['w_g'], 'L0_ffn_c_fc': _L0_ffn_in['c_fc'], 'L0_ffn_c_proj': _L0_ffn_in['c_proj']}

def reference(x, txt, L0_tok_ln1_g, L0_tok_ln1_b, L0_tok_W_proj, L0_tok_b_proj, L0_tok_ln2_g, L0_tok_ln2_b, L0_tok_cls_token, L0_tok_pos_emb, L0_attn_q_w, L0_attn_q_b, L0_attn_k_w, L0_attn_k_b, L0_attn_v_w, L0_attn_v_b, L0_attn_l_w, L0_attn_l_b, L0_ffn_w_g, L0_ffn_c_fc, L0_ffn_c_proj):
    import jax
    import jax.numpy as jnp

    def _L0_tok_ref(x, ln1_g, ln1_b, W_proj, b_proj, ln2_g, ln2_b, cls_token, pos_emb):
        import jax, jax.numpy as jnp
        import numpy as np
        B, C, H, W = (64, 3, 96, 96)
        P = 16
        NP = H // P * (W // P)
        PD = C * P * P
        ED = 256
        NCLS = 1

        def _layernorm(x, g, b, eps=1e-05):
            mu = jnp.mean(x, axis=-1, keepdims=True)
            var = jnp.mean(jnp.square(x - mu), axis=-1, keepdims=True)
            return (x - mu) * jax.lax.rsqrt(var + eps) * g + b
        b = x.shape[0]
        h, w = (H // P, W // P)
        patches = x.reshape(b, C, h, P, w, P)
        patches = patches.transpose(0, 2, 4, 3, 5, 1).reshape(b, h * w, P * P * C)
        z = _layernorm(patches, ln1_g, ln1_b)
        z = jnp.einsum('bnp,pe->bne', z, W_proj) + b_proj
        z = _layernorm(z, ln2_g, ln2_b)
        cls = jnp.broadcast_to(cls_token, (b, NCLS, ED))
        z = jnp.concatenate([cls, z], axis=1)
        z = z + pos_emb
        return z

    def _L0_attn_ref(x, q_w, q_b, k_w, k_b, v_w, v_b, l_w, l_b):
        import jax, jax.numpy as jnp
        import numpy as np
        B, S, D = (2, 512, 256)
        H, P = (16, 64)
        NUM_OUT = 256
        q = jnp.einsum('bsd,hpd->bhsp', x, q_w) + q_b
        k = jnp.einsum('bsd,hpd->bhsp', x, k_w) + k_b
        v = jnp.einsum('bsd,hpd->bhsp', x, v_w) + v_b
        scores = jnp.einsum('bhqp,bhkp->bhqk', q, k) / jnp.sqrt(jnp.float32(P))
        attn = jax.nn.softmax(scores, axis=2)
        ctx = jnp.einsum('bhqk,bhkp->bqhp', attn, v)
        concat = ctx.reshape(ctx.shape[0], ctx.shape[1], H * P)
        out = concat @ l_w.T + l_b
        return out

    def _L0_ffn_ref(x, w_g, c_fc, c_proj):
        import jax, jax.numpy as jnp
        import numpy as np
        import math
        N_EXP = 8
        TOP_K = 2
        CAPACITY_FACTOR = 1.25

        def _capacity(num_tokens):
            cap = math.floor(TOP_K * CAPACITY_FACTOR * num_tokens / N_EXP)
            cap += cap % 2
            return int(cap)
        B, C, d = x.shape
        T = B * C
        cap = _capacity(T)
        xt = x.reshape(T, d)
        logits = xt @ w_g
        top_v, top_i = jax.lax.top_k(logits, TOP_K)
        full = jnp.full_like(logits, -jnp.inf)
        full = full.at[jnp.arange(T)[:, None], top_i].set(top_v)
        probs = jax.nn.softmax(full, axis=-1)
        exp_mask = jax.nn.one_hot(top_i, N_EXP, dtype=jnp.int32)
        exp_mask = jnp.transpose(exp_mask, (1, 0, 2))
        exp_rank = jnp.cumsum(exp_mask.reshape(TOP_K * T, N_EXP), axis=0) - 1
        exp_rank = exp_rank.reshape(TOP_K, T, N_EXP)
        exp_mask = exp_mask * (exp_rank < cap).astype(jnp.int32)
        exp_rank = jnp.sum(exp_mask * exp_rank, axis=-1)
        exp_weights = exp_mask.astype(x.dtype) * probs[None]
        rank_oh = jax.nn.one_hot(exp_rank, cap, dtype=x.dtype)
        cb_weight = jnp.einsum('kte,ktc->tec', exp_weights, rank_oh)
        sec_mask = (cb_weight != 0).astype(x.dtype)
        exp_batches = jnp.einsum('tec,td->ecd', sec_mask, xt)
        h = jax.nn.gelu(jnp.einsum('ecd,edf->ecf', exp_batches, c_fc), approximate=False)
        exp_out = jnp.einsum('ecf,efd->ecd', h, c_proj)
        out = cb_weight.reshape(T, N_EXP * cap) @ exp_out.reshape(N_EXP * cap, d)
        return out.reshape(B, C, d)
    h = _L0_tok_ref(x, L0_tok_ln1_g, L0_tok_ln1_b, L0_tok_W_proj, L0_tok_b_proj, L0_tok_ln2_g, L0_tok_ln2_b, L0_tok_cls_token, L0_tok_pos_emb)
    h = jnp.concatenate([h, txt], axis=1)
    h = h + _L0_attn_ref(_layernorm(h, axis=-1), L0_attn_q_w, L0_attn_q_b, L0_attn_k_w, L0_attn_k_b, L0_attn_v_w, L0_attn_v_b, L0_attn_l_w, L0_attn_l_b)
    h = h + _L0_ffn_ref(_layernorm(h, axis=-1), L0_ffn_w_g, L0_ffn_c_fc, L0_ffn_c_proj)
    return h

_drawn_inputs = setup_inputs


def setup_inputs(seed=0):
    import zlib

    import numpy as np

    out = dict(_drawn_inputs(seed))
    spreads = {'L0_tok_ln1_g': (1.0, 0.2),
     'L0_tok_ln1_b': (0.0, 0.1),
     'L0_tok_b_proj': (0.0, 0.1),
     'L0_tok_ln2_g': (1.0, 0.2),
     'L0_tok_ln2_b': (0.0, 0.1)}
    factors = {'L0_attn_q_b': 8.0, 'L0_attn_k_b': 7.643}
    for name, (base, spread) in spreads.items():
        noise = np.random.default_rng([zlib.crc32(name.encode()), seed]).standard_normal(out[name].shape)
        drawn = base * np.exp(spread * noise) if base else spread * noise
        out[name] = jnp.asarray(drawn.astype(out[name].dtype))
    for name, factor in factors.items():
        out[name] = (out[name] * factor).astype(out[name].dtype)
    return out
```

```python
from contextlib import ExitStack

import concourse.bass as bass
from concourse import mybir

F32 = mybir.dt.float32
F32R = mybir.dt.float32r
BF16 = mybir.dt.bfloat16
I32 = mybir.dt.int32
U32 = mybir.dt.uint32
ALU = mybir.AluOpType
ACT = mybir.ActivationFunctionType
AX = mybir.AxisListType.X

BATCH, SEQ, D = 32, 69, 256
NPATCH, NTXT, PD = 36, 32, 768
HEADS, HD = 16, 64
NEXP, FF, TOPK = 8, 1024, 2
TOKENS = BATCH * SEQ
CAP = TOPK * 5 * TOKENS // (4 * NEXP)
CAP += CAP % 2
EPS = 1e-5
SCALE = HD ** -0.5
KD = D // 128
KP = PD // 128
KF = FF // 128
PAIRS = HEADS // 2

PT = BATCH * NPATCH // 128

PIECES = range(2, 8)
PIECE = 3 * HEADS * HD // len(PIECES)

BPG = 4
GROUPS = BATCH // BPG
GT = BPG * SEQ
TPG = 3
TR = GT // TPG
TILES = GROUPS * TPG
NQKV = 3 * PAIRS
START = [*range(8), *range(16, 20), *range(8, 16), *range(20, NQKV)]
UNITS = 2 * BPG
UH = HEADS // 2
UP = UH // 2

ROW = D + 1 + NEXP
NSLOT = NEXP * CAP
XR = CAP // 6
XT = CAP // XR
HALVES = ((0, CAP // 2 + CAP // 2 % 2), (CAP // 2 + CAP // 2 % 2, CAP))
ROUTED = 28
FAR = 1 << 20


def runs(first, count):
    found = []
    for b in range(BPG):
        n = 0
        while n < count:
            t, r = divmod(b * SEQ + first + n, TR)
            m = min(count - n, TR - r)
            found.append((b, n, r, t, m))
            n += m
    return found


POS_RUNS = runs(0, 1 + NPATCH)
PATCH_RUNS = runs(1, NPATCH)
TEXT_RUNS = runs(1 + NPATCH, NTXT)


class Step:

    def __init__(self, i, k=None, span=1):
        self.i, self.k, self.span = i, k, span

    def of(self, f):
        if self.k is None:
            return f(self.i)
        return self.k * (f(self.i + self.span) - f(self.i)) + f(self.i)


def sweep(eng, body, n, head, tail, span):
    for i in range(head):
        body(Step(i))
    with eng.Fori(0, (n - head - tail) // span) as k:
        for i in range(head, head + span):
            body(Step(i, k, span))
    for i in range(n - tail, n):
        body(Step(i))


def wait(eng, sem, step, f):
    assert step.k is None or f(step.i) >= 0
    if step.k is not None or f(step.i) > 0:
        eng.wait_ge(sem, step.of(f))


def wait_apart(eng, sem, step, f):
    wait(eng, sem, step, f)
    if step.k is not None:
        eng.nop(nofuse=True)


def bank_uses():
    order = [("xt", 0, c) for c in range(KD)] + [("qkv", 0, c) for c in START]
    for g in range(GROUPS + 1):
        for u in range(UNITS):
            order += group_uses(g, u)
    return {use: (n % 2, n // 2 + 1) for n, use in enumerate(order)}


def qkv_of(u):
    first = (0, 0, 5, 8, 12, 15, 19, 22, NQKV)
    return range(first[u], first[u + 1])


def group_uses(g, u):
    uses = []
    if g >= 1:
        uses += {0: [("proj", g - 1, c) for c in range(KD)],
                 2: [("ytr", g - 1, 0), ("ytr", g - 1, 1)],
                 4: [("x2t", g - 1, c) for c in range(KD)],
                 5: [("logit", g - 1, 0)]}.get(u, [])
    if g + 1 < GROUPS:
        if u == 0:
            uses += [("xt", g + 1, c) for c in range(KD)]
        uses += [("qkv", g + 1, c) for c in qkv_of(u)]
    return uses


def program(nc, patches, txt, ln1_g, ln1_b, w_proj, b_proj, ln2_g, ln2_b, cls, pos,
            w_qkv, b_qkv, w_l, b_l, w_g, c_fc, c_proj, ident_in, out):
    USE = bank_uses()
    z_dram = nc.dram_tensor("patch_rows", (PT * 128, D), F32, kind="Internal").ap()
    slots_dram = nc.dram_tensor("slot_rows", (NSLOT, ROW), F32, kind="Internal").ap()

    ctx = ExitStack()
    with ctx:
        def sb(name, shape, dt=F32, stack=ctx):
            return stack.enter_context(nc.sbuf_tensor(name, shape, dt))

        def sem(name):
            return ctx.enter_context(nc.semaphore(name))

        pair = [ctx.enter_context(nc.psum_tensor(f"pair{i}", [128, 2, 512], F32)) for i in range(2)]
        shared = [ctx.enter_context(nc.psum_tensor(f"shared{i}", [128, 512], F32)) for i in range(2)]
        vt_ps = ctx.enter_context(nc.psum_tensor("vt_ps", [128, 512], F32))
        ct_ps = ctx.enter_context(nc.psum_tensor("ct_ps", [128, 512], F32))

        ident = sb("ident", [128, 128])
        rows = sb("rows", [TR, TILES, ROW])
        xg = [sb(f"xg{i}", [XR, XT, ROW]) for i in range(2)]

        pos_sb = sb("pos_sb", [TR, TPG, D])
        logits = sb("logits", [TR, TILES, NEXP])
        tri = sb("tri", [TR, TR], BF16)
        ones = sb("ones", [TR, TR], BF16)
        half = sb("half", [128, TPG])
        expert = sb("expert", [TR, TILES, NEXP])
        base = sb("base", [TR, NEXP, TOPK * TILES])
        restart = sb("restart", [TR, NEXP, TOPK * TILES])
        slot_ix = sb("slot_ix", [TR, TOPK * TILES], I32)

        bmem = ctx.enter_context(ExitStack())
        wq_hi = sb("wq_hi", [128, KD, NQKV * 128], F32R, bmem)
        wq_lo = sb("wq_lo", [128, KD, NQKV * 128], F32R, bmem)
        wl_hi = sb("wl_hi", [128, PAIRS, D], F32R, bmem)
        wl_lo = sb("wl_lo", [128, PAIRS, D], F32R, bmem)
        qkv = [sb(f"qkv{i}", [128, NQKV, GT], F32, bmem) for i in range(2)]
        ctx_hi = sb("ctx_hi", [128, PAIRS, GT], F32R, bmem)
        ctx_lo = sb("ctx_lo", [128, PAIRS, GT], F32R, bmem)
        bq_sb = sb("bq_sb", [128, NQKV], F32, bmem)
        bl_sb = sb("bl_sb", [128, KD], F32, bmem)
        wg_sb = sb("wg_sb", [128, KD, NEXP], F32, bmem)

        z_stat = sb("z_stat", [128, 6], F32, bmem)
        z_mv = sb("z_mv", [128, 2], F32, bmem)
        z_rs = sb("z_rs", [128, 1], F32, bmem)
        z_row = [sb(f"z_row{i}", [128, D], F32, bmem) for i in range(2)]
        g2_sb = sb("g2_sb", [128, D], F32, bmem)
        b2_sb = sb("b2_sb", [128, D], F32, bmem)
        zb_sb = sb("zb_sb", [128, D], F32, bmem)
        with ExitStack() as amem:
            pT_hi = [sb(f"pT_hi{i}", [128, KP, 128], F32R, amem) for i in range(2)]
            pT_lo = [sb(f"pT_lo{i}", [128, KP, 128], F32R, amem) for i in range(2)]
            a_stat = sb("a_stat", [128, 2, 6], F32, amem)
            a_mv = sb("a_mv", [128, 2], F32, amem)
            a_rs = sb("a_rs", [128, 1], F32, amem)
            wp_g = sb("wp_g", [128, KP, D], F32, amem)
            g1_sb = sb("g1_sb", [128, KP], F32, amem)
            b1_sb = sb("b1_sb", [128, KP], F32, amem)
        flat0 = qkv[0][:, :, :].rearrange("p c n -> p (c n)")
        flat1 = qkv[1][:, :, :].rearrange("p c n -> p (c n)")
        wq_raw = flat1[:, 0:KD * NQKV * 128].rearrange("p (k n) -> p k n", k=KD)
        wl_raw = flat0[:, 0:PAIRS * D].rearrange("p (k n) -> p k n", k=PAIRS)
        at = PAIRS * D
        wp_raw = flat0[:, at:at + KP * D].rearrange("p (k n) -> p k n", k=KP)
        at += KP * D
        patch = [flat0[:, at + i * PD:at + (i + 1) * PD] for i in range(2)]
        at += 2 * PD
        b1_wide = flat0[:, at:at + KP * 128].rearrange("p (k n) -> p k n", k=KP)
        wp_hi = ctx_hi[:, :, :].rearrange("p c n -> p (c n)")[:, 0:KP * D].rearrange("p (k n) -> p k n", k=KP)
        wp_lo = ctx_lo[:, :, :].rearrange("p c n -> p (c n)")[:, 0:KP * D].rearrange("p (k n) -> p k n", k=KP)

        with ExitStack() as smem:
            xT_hi = sb("xT_hi", [128, KD, GT], F32R, smem)
            xT_lo = sb("xT_lo", [128, KD, GT], F32R, smem)
            expo = [sb(f"expo{i}", [SEQ, UH, SEQ], F32, smem) for i in range(2)]
            vals = [sb(f"vals{i}", [SEQ, UH, HD], F32, smem) for i in range(2)]
            top = sb("top", [SEQ, UH], F32, smem)
            zsum = sb("zsum", [SEQ, UH], F32, smem)
            zinv = sb("zinv", [SEQ, UH], F32, smem)
            yT = sb("yT", [128, KD, GT], F32, smem)
            x2T = sb("x2T", [128, KD, GT], F32, smem)
            xn = sb("xn", [TR, TPG, D], F32, smem)
            h2 = sb("h2", [TR, TPG, D], F32, smem)
            n_stat = sb("n_stat", [TR, TPG, 6], F32, smem)
            n_mv = sb("n_mv", [TR, TPG, 2], F32, smem)
            n_rs = sb("n_rs", [TR, TPG], F32, smem)
            m_stat = sb("m_stat", [TR, TPG, 6], F32, smem)
            m_mv = sb("m_mv", [TR, TPG, 2], F32, smem)
            m_rs = sb("m_rs", [TR, TPG], F32, smem)
        bmem.close()

        with ExitStack() as cmem:
            is_top = sb("is_top", [TR, TILES, NEXP], F32, cmem)
            cand = sb("cand", [TR, TILES, NEXP], F32, cmem)
            rest = sb("rest", [TR, TILES, NEXP], F32, cmem)
            best = sb("best", [TR, TOPK, TILES], F32, cmem)
            first = sb("first", [TR, TOPK, TILES], F32, cmem)
            gap = sb("gap", [TR, TILES], F32, cmem)
            e_gap = sb("e_gap", [TR, TILES], F32, cmem)
            denom = sb("denom", [TR, TILES], F32, cmem)
            prob = sb("prob", [TR, TOPK, TILES], F32, cmem)
            chosen = sb("chosen", [TR, NEXP, TOPK, TILES], F32, cmem)
            chosen_b = sb("chosen_b", [TR, NEXP, TOPK, TILES], BF16, cmem)
            upto = sb("upto", [TR, NEXP * TOPK * TILES], F32, cmem)
            rank = sb("rank", [TR, NEXP * TOPK * TILES], F32, cmem)
            kept = sb("kept", [TR, NEXP, TOPK, TILES], F32, cmem)
            slot = sb("slot", [TR, NEXP, TOPK * TILES], F32, cmem)
            slot_f = sb("slot_f", [TR, TOPK * TILES], F32, cmem)
            wgt = sb("wgt", [TR, NEXP, TOPK, TILES], F32, cmem)
            raw_fc = sb("raw_fc", [128, KD, FF], F32, cmem)
            raw_pj = sb("raw_pj", [128, KF, D], F32, cmem)
            fc_hi = sb("fc_hi", [128, KD, FF], F32R, cmem)
            fc_lo = sb("fc_lo", [128, KD, FF], F32R, cmem)
            pj_hi = sb("pj_hi", [128, KF, D], F32R, cmem)
            pj_lo = sb("pj_lo", [128, KF, D], F32R, cmem)
            xe_hi = sb("xe_hi", [128, KD, CAP], F32R, cmem)
            xe_lo = sb("xe_lo", [128, KD, CAP], F32R, cmem)
            act_f = [sb(f"act_f{i}", [128, CAP], F32, cmem) for i in range(2)]
            act_hi = sb("act_hi", [128, KF, CAP], F32R, cmem)
            act_lo = sb("act_lo", [128, KF, CAP], F32R, cmem)
            yrow = [sb(f"yrow{i}", [XR, XT, D], F32, cmem) for i in range(2)]

        s_const, s_wp, s_small, s_wll = (sem(n) for n in ("s_const", "s_wp", "s_small", "s_wll"))
        s_wql = [sem(f"s_wql{i}") for i in range(2)]
        s_patch = [sem(f"s_patch{i}") for i in range(2)]
        s_pos, s_ident, s_wq_lo2, s_x2c = (sem(n) for n in ("s_pos", "s_ident", "s_wq_lo2", "s_x2c"))
        s_chosen = sem("s_chosen")
        s_a_rs, s_z_rs, s_n_rs, s_m_rs, s_half = (sem(n) for n in ("s_a_rs", "s_z_rs", "s_n_rs", "s_m_rs", "s_half"))
        s_rest_rows = sem("s_rest_rows")
        s_zdma = [sem(f"s_zdma{i}") for i in range(2)]
        s_rows = [sem(f"s_rows{i}") for i in range(2)]
        s_a_ln, s_pn, s_pT, s_pT_hi, s_pT_lo, s_z, s_z1, s_zn, s_zrow, s_wp_s, s_wp_hi, s_wp_lo, s_b1w, s_bw, s_zb = (
            sem(n) for n in ("s_a_ln", "s_pn", "s_pT", "s_pT_hi", "s_pT_lo", "s_z", "s_z1", "s_zn", "s_zrow",
                             "s_wp_s", "s_wp_hi", "s_wp_lo", "s_b1w", "s_bw", "s_zb"))
        s_z_ln, s_zmul = sem("s_z_ln"), sem("s_zmul")
        s_wq_hi, s_wq_lo, s_wl_hi, s_wl_lo = (sem(n) for n in ("s_wq_hi", "s_wq_lo", "s_wl_hi", "s_wl_lo"))
        s_full = [sem(f"s_full{i}") for i in range(2)]
        s_free = [sem(f"s_free{i}") for i in range(2)]
        s_h, s_n_ln, s_xn, s_xT_hi, s_xT_lo, s_qkv = (sem(n) for n in ("s_h", "s_n_ln", "s_xn", "s_xT_hi", "s_xT_lo", "s_qkv"))
        s_vt, s_score, s_top, s_sub, s_exp, s_zs, s_zi, s_val, s_ctx, s_c_hi, s_c_lo = (
            sem(n) for n in ("s_vt", "s_score", "s_top", "s_sub", "s_exp", "s_zs", "s_zi", "s_val", "s_ctx", "s_c_hi", "s_c_lo"))
        s_yT, s_h2, s_m_ln, s_x2, s_x2T, s_logit, s_h2_out = (
            sem(n) for n in ("s_yT", "s_h2", "s_m_ln", "s_x2", "s_x2T", "s_logit", "s_h2_out"))
        s_pool, s_masks, s_route, s_gap, s_egap, s_rank_ps, s_fill, s_sent = (
            sem(n) for n in ("s_pool", "s_masks", "s_route", "s_gap", "s_egap", "s_rank_ps", "s_fill", "s_sent"))
        s_fcl, s_pjl, s_fc_hi, s_fc_lo, s_pj_hi, s_pj_lo = (
            sem(n) for n in ("s_fcl", "s_pjl", "s_fc_hi", "s_fc_lo", "s_pj_hi", "s_pj_lo"))
        s_xg = [sem(f"s_xg{i}") for i in range(2)]
        s_xe, s_xe_hi, s_xe_lo, s_mid, s_gelu, s_act_hi, s_act_lo, s_y, s_yrow, s_added = (
            sem(n) for n in ("s_xe", "s_xe_hi", "s_xe_lo", "s_mid", "s_gelu", "s_act_hi", "s_act_lo", "s_y", "s_yrow", "s_added"))

        def use(kind, step, shift, c):
            bank = USE[(kind, step.i + shift, c)][0]
            return bank, lambda i: USE[(kind, i + shift, c)][1]

        def f32(ap):
            return ap.bitcast(F32)

        def piece(st):
            c = st.of(lambda i: (i - 2) * PIECE)
            return slice(c, c + PIECE) if st.k is None else bass.ds(c, PIECE)

        block = ctx.enter_context(nc.Block())

        @block.sync
        def _(sp):
            sp.dma_start(patch[0], patches[0]).then_inc(s_patch[0], 16)
            sp.dma_start(wp_raw, w_proj.rearrange("(k p) n -> p k n", p=128)).then_inc(s_wp, 16)
            sp.dma_start(ident[:, :], ident_in).then_inc(s_ident, 16)
            sp.dma_start(g1_sb[:, :], ln1_g).then_inc(s_small, 16)
            sp.dma_start(b1_sb[:, :], ln1_b).then_inc(s_small, 16)
            sp.dma_start(g2_sb[:, :], ln2_g.broadcast_to([128, D])).then_inc(s_small, 16)
            sp.dma_start(b2_sb[:, :], ln2_b.broadcast_to([128, D])).then_inc(s_small, 16)
            sp.dma_start(zb_sb[:, :], b_proj.broadcast_to([128, D])).then_inc(s_small, 16)
            sp.dma_start(patch[1], patches[1]).then_inc(s_patch[1], 16)
            sp.dma_start(bq_sb[:, :], b_qkv).then_inc(s_const, 16)
            sp.dma_start(bl_sb[:, :], b_l).then_inc(s_const, 16)
            sp.dma_start(wg_sb[:, :, :], w_g.rearrange("(k p) n -> p k n", p=128)).then_inc(s_const, 16)
            every = rows[:, :, 0:D].rearrange("p (g t) d -> p t g d", t=TPG)
            txt_seq = txt.rearrange("(g b) s d -> b s g d", b=BPG)
            for b in range(BPG):
                t, r = divmod(b * SEQ, TR)
                sp.dma_start(every[r:r + 1, t, :, :], cls.unsqueeze(1).broadcast_to([1, GROUPS, D])).then_inc(s_rest_rows, 16)
            for b, n, r, t, m in TEXT_RUNS:
                sp.dma_start(every[r:r + m, t, :, :], txt_seq[b, n:n + m, :, :]).then_inc(s_rest_rows, 16)
            sp.dma_start(wl_raw, w_l.rearrange("(k p) n -> p k n", p=128)).then_inc(s_wll, 16)
            sp.wait_ge(s_pool, 1)
            for _, n, r, t, m in POS_RUNS:
                sp.dma_start(pos_sb[r:r + m, t, :], pos[n:n + m, :]).then_inc(s_pos, 16)

            def load_rows(st, shift):
                g = st.of(lambda i: i + shift)
                for n in range(2):
                    wait_apart(sp, s_zdma[(st.i + shift + n) % 2], st, lambda i: 16 * ((i + shift + n) // 2 + 1))
                if st.i + shift >= 2:
                    wait_apart(sp, s_rows[(st.i + shift) % 2], st, lambda i: 16 * len(PATCH_RUNS) * ((i + shift) // 2))
                for b, n, r, t, m in PATCH_RUNS:
                    sp.dma_start(rows[r:r + m, bass.ds(g * TPG + t, 1), 0:D],
                                 z_dram[bass.ds((g * BPG + b) * NPATCH + n, m), :].rearrange("(m o) d -> m o d", o=1))\
                      .then_inc(s_rows[(st.i + shift) % 2], 16)

            def stage_a(st):
                if st.i in PIECES:
                    w = piece(st)
                    sp.dma_start(wq_raw[:, :, w], w_qkv.rearrange("(k p) n -> p k n", p=128)[:, :, w])\
                      .then_inc(s_wql[st.i % 2], 16)
                if st.i + 2 < PT:
                    wait_apart(sp, s_pT, st, lambda i: i + 1)
                    j = st.of(lambda i: i + 2)
                    sp.dma_start(patch[st.i % 2], patches[bass.ds(j, 1), :, :].rearrange("o p n -> (o p) n"))\
                      .then_inc(s_patch[st.i % 2], 16)
                if PT - 2 <= st.i <= PT:
                    load_rows(Step(st.i), 2 - PT)
                if st.i >= 2:
                    j = st.of(lambda i: i - 2)
                    wait_apart(sp, s_zrow, st, lambda i: i - 1)
                    sp.dma_start(z_dram[bass.ds(j * 128, 128), :], z_row[st.i % 2][:, :]).then_inc(s_zdma[st.i % 2], 16)
            sweep(sp, stage_a, PT + 2, 3, 4, 2)

            out_tile = out.rearrange("(t p) d -> p t d", p=TR)

            def stage_b(st):
                if st.i + 3 < GROUPS:
                    load_rows(st, 3)
                g = st.of(lambda i: i)
                wait_apart(sp, s_h2, st, lambda i: i + 1)
                sp.dma_start(out_tile[:, bass.ds(g * TPG, TPG), :], h2[:, :, :]).then_inc(s_h2_out, 16)

            sweep(sp, stage_b, GROUPS, 0, 4, 2)

            def load_fc(e):
                sp.dma_start(raw_fc[:, :, :], c_fc[e].rearrange("o (k p) n -> p (o k) n", p=128)).then_inc(s_fcl, 16)

            def load_pj(e):
                sp.dma_start(raw_pj[:, :, :], c_proj[e].rearrange("o (k p) n -> p (o k) n", p=128)).then_inc(s_pjl, 16)

            def load_slots(e, p):
                sp.dma_start(xg[p][:, :, :],
                             slots_dram[bass.ds(e * CAP, CAP), :].rearrange("(t p) n -> p t n", p=XR))\
                  .then_inc(s_xg[p], 16)

            bank, n = USE[("logit", GROUPS - 1, 0)]
            sp.wait_ge(s_full[bank], n)
            sp.wait_ge(s_c_lo, UNITS * GROUPS)
            sp.wait_ge(s_free[0], USE[("logit", GROUPS - 1, 0)][1] - 1)
            load_fc(slice(0, 1))
            load_pj(slice(0, 1))
            sp.wait_ge(s_sent, 16 * TOPK * TILES)
            load_slots(0, 0)

            def stage_d(st):
                if st.i + 1 < NEXP:
                    nxt = st.of(lambda i: i + 1)
                    if st.i >= 1:
                        wait_apart(sp, s_added, st, lambda i: 16 * XT * i)
                    load_slots(nxt, (st.i + 1) % 2)
                    wait_apart(sp, s_fc_lo, st, lambda i: 4 * (i + 1))
                    load_fc(bass.ds(nxt, 1))
                    wait_apart(sp, s_pj_lo, st, lambda i: 4 * (i + 1))
                    load_pj(bass.ds(nxt, 1))

            sweep(sp, stage_d, NEXP, 1, 1, 2)
            sp.wait_ge(s_h2_out, 16 * GROUPS)
            sp.wait_ge(s_added, 16 * XT * NEXP)

        @block.gpsimd
        def _(pool):
            pool.memset(half[:, :], -0.5).then_inc(s_half, 1)
            pool.memset(pos_sb[:, :, :], 0.0).then_inc(s_pool, 1)
            pool.memset(xg[1][:, :, :], 0.0).then_inc(s_pool, 1)
            pool.wait_ge(s_pool, 2)
            pool.memset(xg[1][:, :, D:D + 1].bitcast(I32), FAR).then_inc(s_pool, 1)
            pool.memset(ones[:, :], 1.0).then_inc(s_masks, 1)
            pool.memset(tri[:, :], 1.0).then_inc(s_masks, 1)
            pool.memset(restart[:, :, :], 1.0).then_inc(s_masks, 1)
            pool.wait_ge(s_masks, 3)
            pool.affine_select(out=tri[:, :], in_=tri[:, :], compare_op=ALU.is_gt, fill=0.0, base=0,
                               pattern=[[1, TR]], channel_multiplier=-1).then_inc(s_masks, 1)
            pool.memset(restart[:, :, 0:1], 0.0).then_inc(s_masks, 1)
            pool.iota(expert[:, :, :], pattern=[[0, TILES], [1, NEXP]], base=0, channel_multiplier=0,
                      allow_small_or_imprecise_dtypes=True).then_inc(s_masks, 1)
            pool.iota(base[:, :, :], pattern=[[CAP, NEXP], [0, TOPK * TILES]], base=FAR, channel_multiplier=0,
                      allow_small_or_imprecise_dtypes=True).then_inc(s_masks, 1)

            def root(rs, st, ready, f, done):
                wait(pool, ready, st, f)
                pool.tensor_tensor(rs, rs, half[0:rs.shape[0], 0:rs.shape[1]], ALU.pow).then_inc(done, 1)

            def add_positions(st, shift):
                g = st.of(lambda i: i + shift)
                wait(pool, s_rows[(st.i + shift) % 2], st, lambda i: 16 * len(PATCH_RUNS) * ((i + shift) // 2 + 1))
                r = rows[:, g * TPG:(g + 1) * TPG, 0:D] if st.k is None else rows[:, bass.ds(g * TPG, TPG), 0:D]
                pool.tensor_tensor(r, r, pos_sb[:, :, :], ALU.add).then_inc(s_h, 1)

            def root_in(st, shift):
                root(n_rs[:, :], st, s_n_ln, lambda i: 3 * (i + shift + 1), s_n_rs)

            def stage_a(st):
                if st.i == PT - 1:
                    pool.wait_ge(s_pos, 16 * len(POS_RUNS))
                    pool.wait_ge(s_rest_rows, 16 * (BPG + len(TEXT_RUNS)))
                    add_positions(Step(0), 0)
                if st.i == PT:
                    root_in(Step(0), 0)
                if st.i + 1 < PT:
                    root(a_rs[:, :], st, s_a_ln, lambda i: 3 * (i + 2), s_a_rs)
                if st.i >= 2:
                    p = st.i % 2
                    wait(pool, s_zn, st, lambda i: i - 1)
                    pool.tensor_tensor(z_row[p][:, :], z_row[p][:, :], g2_sb[:, :], ALU.mult).then_inc(s_zmul, 1)
                    wait(pool, s_zmul, st, lambda i: i - 1)
                    pool.tensor_tensor(z_row[p][:, :], z_row[p][:, :], b2_sb[:, :], ALU.add).then_inc(s_zrow, 1)
                if 1 <= st.i <= PT:
                    root(z_rs[:, :], st, s_z_ln, lambda i: 3 * i, s_z_rs)
                if st.i in PIECES:
                    w = piece(st)
                    wait(pool, s_wq_hi, st, lambda i: i - 1)
                    pool.tensor_tensor(wq_lo[:, 0, w], wq_raw[:, 0, w], f32(wq_hi[:, 0, w]), ALU.subtract)\
                        .then_inc(s_wq_lo, 1)

            pool.wait_ge(s_half, 1)
            root(a_rs[:, :], Step(0), s_a_ln, lambda i: 3, s_a_rs)
            pool.wait_ge(s_small, 80)
            sweep(pool, stage_a, PT + 2, 3, 4, 2)
            def fill_slots(st):
                e = st.of(lambda i: i)
                if st.i == 0:
                    pool.wait_ge(s_pool, 3)
                pool.dma_start(slots_dram[bass.ds(e * CAP, CAP), :].rearrange("(t p) n -> p t n", p=XR),
                               xg[1][:, :, :]).then_inc(s_fill, 16)

            def root_mid(st, shift):
                root(m_rs[:, :], st, s_m_ln, lambda i: 3 * (i + shift + 1), s_m_rs)
                g = st.of(lambda i: i + shift)
                wait_apart(pool, s_x2, st, lambda i: i + shift + 1)
                dst = rows[:, g * TPG:(g + 1) * TPG, 0:D] if st.k is None else rows[:, bass.ds(g * TPG, TPG), 0:D]
                pool.tensor_copy(dst, xn[:, :, :]).then_inc(s_x2c, 1)

            def stage_b(st):
                if st.i + 1 < GROUPS:
                    root_in(st, 1)
                if st.i + 2 < GROUPS:
                    add_positions(st, 2)
                if st.i >= 1:
                    root_mid(st, -1)
                fill_slots(st)

            add_positions(Step(0), 1)
            sweep(pool, stage_b, GROUPS, 1, 3, 2)
            root_mid(Step(GROUPS), -1)

            pool.iota(rows[:, :, D:D + 1].bitcast(I32), pattern=[[TR, TILES], [0, 1]], base=0, channel_multiplier=1)\
                .then_inc(s_masks, 1)
            pool.wait_ge(s_masks, 8)
            pool.wait_ge(s_fill, 16 * NEXP)
            pool.wait_ge(s_x2c, GROUPS)
            pool.wait_ge(s_route, ROUTED)
            for n in range(TOPK * TILES):
                pool.indirect_dma_start(slots_dram, bass.IndirectOffsetOnAxis(ap=slot_ix[:, n:n + 1].bitcast(U32), axis=0),
                                        rows[:, n % TILES, :], None, bounds_check=NSLOT - 1, oob_is_err=False)\
                    .then_inc(s_sent, 16)

            def stage_d(st):
                p = st.i % 2
                wait(pool, s_added, st, lambda i: 16 * XT * i)
                if st.i == 0:
                    pool.wait_ge(s_h2_out, 16 * GROUPS)
                for t in range(XT):
                    wait_apart(pool, s_yrow, st, lambda i: XT * i + t + 1)
                    pool.indirect_dma_start(out, bass.IndirectOffsetOnAxis(ap=xg[p][:, t, D:D + 1].bitcast(U32), axis=0),
                                            yrow[p][:, t, :], None, bounds_check=TOKENS - 1, oob_is_err=False,
                                            compute_op=ALU.add).then_inc(s_added, 16)

            sweep(pool, stage_d, NEXP, 1, 1, 2)

        @block.scalar
        def _(act):
            act.wait_ge(s_wp_s, KP)
            act.activation(wp_hi, wp_g[:, :, :], ACT.Copy).then_inc(s_wp_hi, 1)

            def stage_a(st):
                if st.i < PT:
                    p = st.i % 2
                    wait(act, s_pT, st, lambda i: i + 1)
                    wait(act, s_z, st, lambda i: i - 1)
                    for h in range(2):
                        act.activation(pT_hi[p][:, 3 * h:3 * h + 3, :],
                                       pair[p][:, h, 0:384].rearrange("p (k n) -> p k n", k=3), ACT.Copy)\
                            .then_inc(s_pT_hi, 1)
                if st.i in PIECES:
                    w = piece(st)
                    wait(act, s_wql[st.i % 2], st, lambda i: 16 * (i // 2))
                    act.activation(wq_hi[:, :, w], wq_raw[:, :, w], ACT.Copy).then_inc(s_wq_hi, 1)
                if st.i in (PT - 1, PT):
                    act.wait_ge(s_wll, 16)
                    w = slice((st.i - PT + 1) * 4, (st.i - PT + 2) * 4)
                    act.activation(wl_hi[:, w, :], wl_raw[:, w, :], ACT.Copy).then_inc(s_wl_hi, 1)

            sweep(act, stage_a, PT + 2, 3, 4, 2)
            def put_qkv(st, shift, c):
                bank, nth = use("qkv", st, shift, c)
                wait(act, s_full[bank], st, nth)
                act.activation(qkv[(st.i + shift) % 2][:, c, :], shared[bank][:, 0:GT], ACT.Identity,
                               bias=bq_sb[:, c:c + 1]).then_inc(s_free[bank], 1)

            def put_xT(st, shift):
                for c in range(KD):
                    bank, nth = use("xt", st, shift, c)
                    wait(act, s_full[bank], st, nth)
                    act.activation(xT_hi[:, c, :], shared[bank][:, 0:GT], ACT.Copy).then_inc(s_xT_hi, 1)

            def put_exp(st, u):
                n = lambda i: UNITS * i + u + 1
                wait(act, s_sub, st, lambda i: n(i) + 1)
                e = expo[(u + 1) % 2][:, :, :]
                act.activation(e, e, ACT.Exp, scale=SCALE).then_inc(s_exp, 1)

            def put_ctx(st, u):
                wait(act, s_ctx, st, lambda i: UNITS * i + u + 1)
                act.activation(ctx_hi[:, UP * (u % 2):UP * (u % 2 + 1), SEQ * (u // 2):SEQ * (u // 2 + 1)],
                               ct_ps[:, 0:UP * SEQ].rearrange("p (k n) -> p k n", k=UP), ACT.Copy)\
                    .then_inc(s_c_hi, 1)

            def put_y(st, shift):
                for c in range(KD):
                    bank, nth = use("proj", st, shift, c)
                    wait(act, s_full[bank], st, nth)
                    act.activation(yT[:, c, :], shared[bank][:, 0:GT], ACT.Identity,
                                   bias=bl_sb[:, c:c + 1]).then_inc(s_free[bank], 1)

            def put_x2T(st, shift):
                for c in range(KD):
                    bank, nth = use("x2t", st, shift, c)
                    wait(act, s_full[bank], st, nth)
                    act.activation(x2T[:, c, :], shared[bank][:, 0:GT], ACT.Copy).then_inc(s_free[bank], 1)

            act.wait_ge(s_const, 48)
            act.wait_ge(s_wl_lo, 2)
            put_xT(Step(0), 0)
            for n, c in enumerate(START):
                put_qkv(Step(0), 0, c)
                if n == 11:
                    put_exp(Step(-1), UNITS - 1)

            def stage_b(st):
                more, before = st.i + 1 < GROUPS, st.i >= 1
                for u in range(UNITS):
                    blocks = list(qkv_of(u)) if more else []
                    if u == 4 and before:
                        put_x2T(st, -1)
                    for c in blocks[:-1][:2]:
                        put_qkv(st, 1, c)
                    if u == 0 and before:
                        put_y(st, -1)
                    if more or u + 1 < UNITS:
                        put_exp(st, u)
                    for c in blocks[:-1][2:]:
                        put_qkv(st, 1, c)
                    if u == 0 and more:
                        put_xT(st, 1)
                    put_ctx(st, u)
                    for c in blocks[-1:]:
                        put_qkv(st, 1, c)

            sweep(act, stage_b, GROUPS, 1, 1, 2)
            put_y(Step(GROUPS), -1)
            put_x2T(Step(GROUPS), -1)
            act.wait_ge(s_gap, 1)
            act.activation(e_gap[:, :], gap[:, :], ACT.Exp).then_inc(s_egap, 1)

            def split_fc(st, shift, q):
                wait(act, s_fcl, st, lambda i: 16 * (i + shift + 1))
                wait(act, s_mid, st, lambda i: KF * (i + shift))
                w = slice(q * FF // 4, (q + 1) * FF // 4)
                act.activation(fc_hi[:, :, w], raw_fc[:, :, w], ACT.Copy).then_inc(s_fc_hi, 1)

            def split_pj(st, q):
                wait(act, s_pjl, st, lambda i: 16 * (i + 1))
                wait(act, s_y, st, lambda i: XT * i)
                w = slice(q * KF // 4, (q + 1) * KF // 4)
                act.activation(pj_hi[:, w, :], raw_pj[:, w, :], ACT.Copy).then_inc(s_pj_hi, 1)

            def put_xe(st, shift):
                for n in range(2 * KD):
                    c, h = n // 2, n % 2
                    wait(act, s_xe, st, lambda i: 2 * KD * (i + shift) + n + 1)
                    bank = (vt_ps, ct_ps)[h]
                    act.activation(xe_hi[:, c, h * 3 * XR:(h + 1) * 3 * XR], bank[:, 0:3 * XR], ACT.Copy)\
                        .then_inc(s_xe_hi, 1)

            for q in range(4):
                split_fc(Step(0), 0, q)
            put_xe(Step(0), 0)

            def stage_d(st):
                for f in range(KF):
                    wait(act, s_mid, st, lambda i: KF * i + f + 1)
                    wait(act, s_act_lo, st, lambda i: KF * i + f - 1)
                    for h, (a, b) in enumerate(HALVES):
                        gelu = act.activation(act_f[f % 2][:, a:b], pair[f % 2][:, h, 0:b - a], ACT.Gelu)
                    gelu.then_inc(s_gelu, 1)
                    if f < 4:
                        split_pj(st, f)
                if st.i + 1 < NEXP:
                    for q in range(4):
                        split_fc(st, 1, q)
                    put_xe(st, 1)

            sweep(act, stage_d, NEXP, 1, 1, 2)

        @block.vector
        def _(dve):
            def norm_patches(st, shift):
                p = (st.i + shift) % 2
                wait(dve, s_patch[p], st, lambda i: 16 * ((i + shift) // 2 + 1))
                x = patch[p]
                for h in range(2):
                    stats = dve.bn_stats(a_stat[:, h, :], x[:, h * 384:(h + 1) * 384])
                stats.then_inc(s_a_ln, 1)
                wait_apart(dve, s_a_ln, st, lambda i: 3 * (i + shift) + 1)
                dve.bn_aggr(a_mv[:, :], a_stat[:, :, :].rearrange("p a b -> p (a b)")).then_inc(s_a_ln, 1)
                wait(dve, s_a_ln, st, lambda i: 3 * (i + shift) + 2)
                dve.tensor_scalar(a_rs[:, :], a_mv[:, 1:2], EPS, None, ALU.add).then_inc(s_a_ln, 1)

            def norm_patches_end(st, shift):
                p = (st.i + shift) % 2
                x = patch[p]
                wait(dve, s_a_rs, st, lambda i: i + shift + 1)
                dve.tensor_scalar(x, x, a_mv[:, 0:1], a_rs[:, 0:1], ALU.subtract, ALU.mult).then_inc(s_pn, 1)

            def low_patches(st):
                p = st.i % 2
                for h in range(2):
                    wait(dve, s_pT_hi, st, lambda i: 2 * i + h + 1)
                    dve.tensor_tensor(pT_lo[p][:, 3 * h:3 * h + 3, :],
                                      pair[p][:, h, 0:384].rearrange("p (k n) -> p k n", k=3),
                                      f32(pT_hi[p][:, 3 * h:3 * h + 3, :]), ALU.subtract).then_inc(s_pT_lo, 1)

            def norm_z(st):
                p = (st.i - 1) % 2
                z = z_row[p][:, :]
                wait(dve, s_z, st, lambda i: i)
                wait(dve, s_zdma[p], st, lambda i: 16 * ((i - 1) // 2))
                dve.tensor_tensor(z, shared[p][:, 0:D], zb_sb[:, :], ALU.add).then_inc(s_z1, 1)
                wait(dve, s_z1, st, lambda i: i)
                dve.bn_stats(z_stat[:, :], z).then_inc(s_z_ln, 1)
                wait_apart(dve, s_z_ln, st, lambda i: 3 * (i - 1) + 1)
                dve.bn_aggr(z_mv[:, :], z_stat[:, :]).then_inc(s_z_ln, 1)
                wait(dve, s_z_ln, st, lambda i: 3 * (i - 1) + 2)
                dve.tensor_scalar(z_rs[:, :], z_mv[:, 1:2], EPS, None, ALU.add).then_inc(s_z_ln, 1)

            def norm_z_end(st):
                z = z_row[st.i % 2][:, :]
                wait(dve, s_z_rs, st, lambda i: i - 1)
                dve.tensor_scalar(z, z, z_mv[:, 0:1], z_rs[:, 0:1], ALU.subtract, ALU.mult).then_inc(s_zn, 1)

            def rows_of(st, shift):
                g = st.of(lambda i: i + shift)
                if st.k is None:
                    return [rows[:, g * TPG + t, 0:D] for t in range(TPG)]
                return [rows[:, bass.ds(g * TPG + t, 1), 0:D].rearrange("p o d -> p (o d)") for t in range(TPG)]

            def norm_in(st, shift):
                src = rows_of(st, shift)
                wait(dve, s_h, st, lambda i: i + shift + 1)
                for t in range(TPG):
                    stats = dve.bn_stats(n_stat[:, t, :], src[t])
                stats.then_inc(s_n_ln, 1)
                wait_apart(dve, s_n_ln, st, lambda i: 3 * (i + shift) + 1)
                for t in range(TPG):
                    stats = dve.bn_aggr(n_mv[:, t, :], n_stat[:, t, :])
                stats.then_inc(s_n_ln, 1)
                wait(dve, s_n_ln, st, lambda i: 3 * (i + shift) + 2)
                dve.tensor_scalar(n_rs[:, :], n_mv[:, :, 1], EPS, None, ALU.add).then_inc(s_n_ln, 1)

            def norm_in_end(st, shift):
                src = rows_of(st, shift)
                wait(dve, s_n_rs, st, lambda i: i + shift + 1)
                for t in range(TPG):
                    done = dve.tensor_scalar(xn[:, t, :], src[t], n_mv[:, t, 0:1], n_rs[:, t:t + 1],
                                             ALU.subtract, ALU.mult)
                done.then_inc(s_xn, 1)

            norm_patches(Step(0), 0)
            norm_patches_end(Step(0), 0)
            dve.wait_ge(s_wp, 16)
            dve.wait_ge(s_small, 80)
            for k in range(KP):
                dve.tensor_scalar(wp_g[:, k, :], wp_raw[:, k, :], g1_sb[:, k:k + 1], None, ALU.mult).then_inc(s_wp_s, 1)
            dve.tensor_copy(b1_wide, b1_sb[:, :].unsqueeze(2).broadcast_to([128, KP, 128])).then_inc(s_b1w, 1)
            dve.wait_ge(s_wp_hi, 1)
            dve.tensor_tensor(wp_lo, wp_g[:, :, :], f32(wp_hi), ALU.subtract).then_inc(s_wp_lo, 1)
            dve.wait_ge(s_bw, 1)
            dve.tensor_tensor(zb_sb[:, :], zb_sb[:, :], vt_ps[:, 0:D], ALU.add).then_inc(s_zb, 1)
            dve.wait_ge(s_zb, 1)

            def stage_a(st):
                if st.i + 1 < PT:
                    norm_patches(st, 1)
                if st.i >= 2:
                    norm_z_end(st)
                if st.i < PT:
                    low_patches(st)
                if st.i + 1 < PT:
                    norm_patches_end(st, 1)
                if 1 <= st.i <= PT:
                    norm_z(st)
                if st.i == PT - 1:
                    norm_in(Step(0), 0)
                if st.i == PT:
                    norm_in_end(Step(0), 0)
                if st.i in PIECES:
                    w = piece(st)
                    wait(dve, s_wq_hi, st, lambda i: i - 1)
                    dve.tensor_tensor(wq_lo[:, 1, w], wq_raw[:, 1, w], f32(wq_hi[:, 1, w]), ALU.subtract)\
                        .then_inc(s_wq_lo2, 1)
                if st.i in (PT - 1, PT):
                    dve.wait_ge(s_wl_hi, st.i - PT + 2)
                    w = slice((st.i - PT + 1) * 4, (st.i - PT + 2) * 4)
                    dve.tensor_tensor(wl_lo[:, w, :], wl_raw[:, w, :], f32(wl_hi[:, w, :]), ALU.subtract)\
                        .then_inc(s_wl_lo, 1)

            sweep(dve, stage_a, PT + 2, 3, 4, 2)
            def low_xT(st, shift):
                for c in range(KD):
                    bank, nth = use("xt", st, shift, c)
                    wait(dve, s_xT_hi, st, lambda i: KD * (i + shift) + c + 1)
                    dve.tensor_tensor(xT_lo[:, c, :], shared[bank][:, 0:GT], f32(xT_hi[:, c, :]), ALU.subtract)\
                        .then_inc(s_xT_lo, 1)
                    dve.wait_ge(s_xT_lo, st.of(lambda i: KD * (i + shift) + c + 1))
                    dve.sem_inc(s_free[bank], 1)

            def take_max(st, u):
                sc = pair[u % 2][0:SEQ, :, 0:UP * SEQ].rearrange("s e (q k) -> s e q k", k=SEQ)
                tp = top[:, :].rearrange("s (e q) -> s e q", e=2)
                ex = expo[u % 2][:, :, :].rearrange("s (e q) k -> s e q k", e=2)
                wait(dve, s_score, st, lambda i: UNITS * i + u + 1)
                dve.tensor_reduce(tp, sc, AX, ALU.max).then_inc(s_top, 1)
                wait(dve, s_top, st, lambda i: UNITS * i + u + 1)
                wait(dve, s_ctx, st, lambda i: UNITS * i + u - 1)
                dve.tensor_tensor(ex, sc, tp.unsqueeze(3).broadcast_to([SEQ, 2, UP, SEQ]), ALU.subtract)\
                    .then_inc(s_sub, 1)

            def weigh_values(st, u):
                wait(dve, s_exp, st, lambda i: UNITS * i + u + 1)
                dve.tensor_reduce(zsum[:, :], expo[u % 2][:, :, :], AX, ALU.add).then_inc(s_zs, 1)
                wait(dve, s_zs, st, lambda i: UNITS * i + u + 1)
                dve.reciprocal(zinv[:, :], zsum[:, :]).then_inc(s_zi, 1)
                wait(dve, s_zi, st, lambda i: UNITS * i + u + 1)
                wait(dve, s_vt, st, lambda i: UNITS * i + u + 1)
                wait(dve, s_ctx, st, lambda i: UNITS * i + u - 1)
                zi = zinv[:, :].rearrange("s (e q) -> s q e", e=2).unsqueeze(3).broadcast_to([SEQ, UP, 2, HD])
                dve.tensor_tensor(vals[u % 2][:, :, :].rearrange("s (q e) d -> s q e d", e=2),
                                  vt_ps[0:SEQ, :].rearrange("s (q e d) -> s q e d", e=2, d=HD), zi, ALU.mult)\
                    .then_inc(s_val, 1)

            def low_ctx(st, u):
                at = (slice(None), slice(UP * (u % 2), UP * (u % 2 + 1)), slice(SEQ * (u // 2), SEQ * (u // 2 + 1)))
                wait(dve, s_c_hi, st, lambda i: UNITS * i + u + 1)
                dve.tensor_tensor(ctx_lo[at], ct_ps[:, 0:UP * SEQ].rearrange("p (k n) -> p k n", k=UP),
                                  f32(ctx_hi[at]), ALU.subtract).then_inc(s_c_lo, 1)

            def residual(st, shift):
                g = st.of(lambda i: i + shift)
                parts = ((0, 2), (2, TPG))
                for n, (a, b) in enumerate(parts):
                    bank, nth = use("ytr", st, shift, n)
                    wait(dve, s_full[bank], st, nth)
                    src = rows[:, g * TPG + a:g * TPG + b, 0:D] if st.k is None else rows[:, bass.ds(g * TPG + a, b - a), 0:D]
                    dve.tensor_tensor(h2[:, a:b, :], shared[bank][0:TR, 0:(b - a) * D].rearrange("p (t d) -> p t d", d=D),
                                      src, ALU.add).then_inc(s_free[bank], 1)

            def norm_mid(st, shift):
                for n in range(2):
                    bank, nth = use("ytr", st, shift, n)
                    wait(dve, s_free[bank], st, nth)
                dve.sem_inc(s_h2, 1)
                for t in range(TPG):
                    stats = dve.bn_stats(m_stat[:, t, :], h2[:, t, :])
                stats.then_inc(s_m_ln, 1)
                wait_apart(dve, s_m_ln, st, lambda i: 3 * (i + shift) + 1)
                for t in range(TPG):
                    stats = dve.bn_aggr(m_mv[:, t, :], m_stat[:, t, :])
                stats.then_inc(s_m_ln, 1)
                wait(dve, s_m_ln, st, lambda i: 3 * (i + shift) + 2)
                dve.tensor_scalar(m_rs[:, :], m_mv[:, :, 1], EPS, None, ALU.add).then_inc(s_m_ln, 1)

            def norm_mid_end(st, shift):
                wait(dve, s_m_rs, st, lambda i: i + shift + 1)
                for t in range(TPG):
                    done = dve.tensor_scalar(xn[:, t, :], h2[:, t, :], m_mv[:, t, 0:1], m_rs[:, t:t + 1],
                                             ALU.subtract, ALU.mult)
                done.then_inc(s_x2, 1)

            def put_logits(st, shift):
                g = st.of(lambda i: i + shift)
                bank, nth = use("logit", st, shift, 0)
                wait(dve, s_x2c, st, lambda i: i + shift + 1)
                wait(dve, s_h2_out, st, lambda i: 16 * (i + shift + 1))
                wait(dve, s_full[bank], st, nth)
                dst = logits[:, g * TPG:(g + 1) * TPG, :] if st.k is None else logits[:, bass.ds(g * TPG, TPG), :]
                dve.tensor_copy(dst, shared[bank][0:TR, 0:TPG * NEXP].rearrange("p (t e) -> p t e", e=NEXP))\
                    .then_inc(s_free[bank], 1)

            low_xT(Step(0), 0)
            take_max(Step(0), 0)

            def stage_b(st):
                more, before = st.i + 1 < GROUPS, st.i >= 1
                for u in range(UNITS):
                    if u == 0 and more:
                        norm_in(st, 1)
                    weigh_values(st, u)
                    if u == 0 and more:
                        norm_in_end(st, 1)
                    if u == 2 and before:
                        residual(st, -1)
                    if u + 1 < UNITS:
                        take_max(st, u + 1)
                    elif more:
                        take_max(Step(st.i + 1, st.k, st.span), 0)
                    if u == 2 and before:
                        norm_mid(st, -1)
                    if u == 3 and before:
                        norm_mid_end(st, -1)
                    if u == 5 and before:
                        put_logits(st, -1)
                    low_ctx(st, u)
                    if u == 0 and more:
                        low_xT(st, 1)

            sweep(dve, stage_b, GROUPS, 1, 1, 2)
            last = Step(GROUPS)
            residual(last, -1)
            norm_mid(last, -1)
            norm_mid_end(last, -1)
            put_logits(last, -1)

            links = [0]

            def link(ins):
                links[0] += 1
                ins.then_inc(s_route, 1)
                dve.wait_ge(s_route, links[0])

            bank, n = USE[("logit", GROUPS - 1, 0)]
            dve.wait_ge(s_free[bank], n)
            dve.wait_ge(s_masks, 7)

            def wide(ap):
                return ap.unsqueeze(2).broadcast_to([TR, TILES, NEXP])

            src = logits[:, :, :]
            for k in range(TOPK):
                picked = chosen[:, :, k, :].rearrange("p e t -> p t e")
                link(dve.tensor_reduce(best[:, k, :], src, AX, ALU.max))
                link(dve.tensor_tensor(is_top[:, :, :], src, wide(best[:, k, :]), ALU.is_equal))
                link(dve.scalar_tensor_tensor(cand[:, :, :], is_top[:, :, :], -float(NEXP), expert[:, :, :], ALU.mult, ALU.add))
                link(dve.tensor_reduce(first[:, k, :], cand[:, :, :], AX, ALU.min))
                link(dve.scalar_tensor_tensor(picked, expert[:, :, :], -float(NEXP), wide(first[:, k, :]), ALU.add, ALU.is_equal))
                if k == 0:
                    link(dve.scalar_tensor_tensor(rest[:, :, :], picked, -3.0e38, src, ALU.mult, ALU.add))
                    src = rest[:, :, :]
            dve.tensor_copy(chosen_b[:, :, :, :], chosen[:, :, :, :]).then_inc(s_chosen, 1)
            link(dve.tensor_tensor(gap[:, :], best[:, 1, :], best[:, 0, :], ALU.subtract))
            dve.sem_inc(s_gap, 1)
            dve.wait_ge(s_egap, 1)
            link(dve.tensor_scalar(denom[:, :], e_gap[:, :], 1.0, None, ALU.add))
            link(dve.reciprocal(prob[:, 0, :], denom[:, :]))
            link(dve.tensor_tensor(prob[:, 1, :], prob[:, 0, :], e_gap[:, :], ALU.mult))
            dve.wait_ge(s_rank_ps, 1)
            count = vt_ps[0:TR, 0:NEXP * TOPK * TILES]
            total = ct_ps[0:TR, 0:NEXP * TOPK * TILES]
            link(dve.tensor_tensor_scan(upto[:, :], restart[:, :, :].rearrange("p e j -> p (e j)"), total, 0.0,
                                        ALU.mult, ALU.add))
            link(dve.tensor_tensor(upto[:, :], upto[:, :], total, ALU.subtract))
            link(dve.tensor_tensor(rank[:, :], upto[:, :], count, ALU.add))
            every = "p e k t -> p (e k t)"
            link(dve.tensor_scalar(kept[:, :, :, :].rearrange(every), rank[:, :], float(CAP), None, ALU.is_lt))
            sl = slot[:, :, :].rearrange("p e j -> p (e j)")
            link(dve.tensor_tensor(rank[:, :], rank[:, :], base[:, :, :].rearrange("p e j -> p (e j)"), ALU.add))
            link(dve.scalar_tensor_tensor(sl, kept[:, :, :, :].rearrange(every), -float(FAR), rank[:, :], ALU.mult, ALU.add))
            link(dve.tensor_tensor(sl, sl, chosen[:, :, :, :].rearrange(every), ALU.mult))
            link(dve.tensor_reduce(slot_f[:, :], slot[:, :, :].rearrange("p e j -> p j e"), AX, ALU.add))
            link(dve.tensor_copy(slot_ix[:, :], slot_f[:, :]))
            link(dve.tensor_tensor(kept[:, :, :, :], kept[:, :, :, :], chosen[:, :, :, :], ALU.mult))
            for k in range(TOPK):
                link(dve.tensor_tensor(wgt[:, :, k, :], kept[:, :, k, :],
                                       prob[:, k, :].unsqueeze(1).broadcast_to([TR, NEXP, TILES]), ALU.mult))
            link(dve.tensor_tensor(rows[:, :, D + 1:], wgt[:, :, 0, :].rearrange("p e t -> p t e"),
                                   wgt[:, :, 1, :].rearrange("p e t -> p t e"), ALU.add))
            assert links[0] == ROUTED

            def low_fc(st, shift, q):
                wait(dve, s_fc_hi, st, lambda i: 4 * (i + shift) + q + 1)
                w = slice(q * FF // 4, (q + 1) * FF // 4)
                dve.tensor_tensor(fc_lo[:, :, w], raw_fc[:, :, w], f32(fc_hi[:, :, w]), ALU.subtract).then_inc(s_fc_lo, 1)

            def low_pj(st, q):
                wait(dve, s_pj_hi, st, lambda i: 4 * i + q + 1)
                w = slice(q * KF // 4, (q + 1) * KF // 4)
                dve.tensor_tensor(pj_lo[:, w, :], raw_pj[:, w, :], f32(pj_hi[:, w, :]), ALU.subtract).then_inc(s_pj_lo, 1)

            def low_xe(st, shift, c):
                for h in range(2):
                    n = 2 * c + h
                    w = slice(h * 3 * XR, (h + 1) * 3 * XR)
                    wait(dve, s_xe_hi, st, lambda i: 2 * KD * (i + shift) + n + 1)
                    dve.tensor_tensor(xe_lo[:, c, w], (vt_ps, ct_ps)[h][:, 0:3 * XR], f32(xe_hi[:, c, w]), ALU.subtract)\
                        .then_inc(s_xe_lo, 1)

            for q in range(4):
                low_fc(Step(0), 0, q)
            for c in range(KD):
                low_xe(Step(0), 0, c)

            def stage_d(st):
                p = st.i % 2
                col = D + 1 + st.of(lambda i: i)

                def put_y(t):
                    wait(dve, s_y, st, lambda i: XT * i + t + 1)
                    w = xg[p][:, t, col:col + 1] if st.k is None else xg[p][:, t, bass.ds(col, 1)]
                    dve.tensor_scalar(yrow[p][:, t, :], shared[t % 2][0:XR, 0:D], w, None, ALU.mult).then_inc(s_yrow, 1)

                for f in range(KF):
                    wait(dve, s_gelu, st, lambda i: KF * i + f + 1)
                    if f == 0:
                        wait(dve, s_y, st, lambda i: XT * i)
                    dve.tensor_copy(act_hi[:, f, :], act_f[f % 2][:, :]).then_inc(s_act_hi, 1)
                    wait(dve, s_act_hi, st, lambda i: KF * i + f + 1)
                    dve.tensor_tensor(act_lo[:, f, :], act_f[f % 2][:, :], f32(act_hi[:, f, :]), ALU.subtract)\
                        .then_inc(s_act_lo, 1)
                    if f < 4:
                        low_pj(st, f)
                more = st.i + 1 < NEXP
                for t in range(XT // 2):
                    if more:
                        low_fc(st, 1, t)
                    put_y(t)
                if more:
                    low_fc(st, 1, 3)
                    low_xe(st, 1, 0)
                put_y(3)
                if more:
                    low_xe(st, 1, 1)
                for t in range(4, XT):
                    put_y(t)
                wait(dve, s_added, st, lambda i: 16 * XT * i)
                if st.k is not None:
                    dve.nop(nofuse=True)

            sweep(dve, stage_d, NEXP, 1, 1, 2)

        @block.tensor
        def _(pe):
            def three(dst, terms, first=True, last=True):
                for n, (l_hi, l_lo, r_hi, r_lo) in enumerate(terms):
                    pe.matmul(dst, l_hi, r_hi, start=(first and n == 0), stop=False)
                    pe.matmul(dst, l_hi, r_lo, start=False, stop=False)
                    done = pe.matmul(dst, l_lo, r_hi, start=False, stop=(last and n == len(terms) - 1))
                return done

            def turn_patches(st, shift):
                p = (st.i + shift) % 2
                wait(pe, s_pn, st, lambda i: i + shift + 1)
                wait(pe, s_pT_lo, st, lambda i: 2 * (i + shift - 1))
                for k in range(KP):
                    done = pe.transpose(pair[p][:, k // 3, k % 3 * 128:(k % 3 + 1) * 128],
                                        patch[p][:, k * 128:(k + 1) * 128], ident[:, :])
                done.then_inc(s_pT, 1)

            def project(st):
                p = st.i % 2
                wait(pe, s_pT_lo, st, lambda i: 2 * (i + 1))
                wait(pe, s_z1, st, lambda i: i - 1)
                three(shared[p][:, 0:D], [(pT_hi[p][:, k, :], pT_lo[p][:, k, :], wp_hi[:, k, :], wp_lo[:, k, :])
                                          for k in range(KP)]).then_inc(s_z, 1)

            pe.wait_ge(s_ident, 16)
            turn_patches(Step(0), 0)
            pe.wait_ge(s_b1w, 1)
            for k in range(KP):
                done = pe.matmul(vt_ps[:, 0:D], b1_wide[:, k, :], wp_raw[:, k, :], start=(k == 0), stop=(k == KP - 1))
            done.then_inc(s_bw, 1)
            pe.wait_ge(s_wp_lo, 1)

            def stage_a(st):
                if st.i + 1 < PT:
                    turn_patches(st, 1)
                if st.i < PT:
                    project(st)

            sweep(pe, stage_a, PT + 2, 3, 4, 2)

            def free(st, kind, shift, c):
                bank, nth = use(kind, st, shift, c)
                wait(pe, s_free[bank], st, lambda i: nth(i) - 1)
                return bank

            def taken(st, kind, shift, blocks):
                for bank in range(2):
                    mine = [c for c in blocks if USE[(kind, st.i + shift, c)][0] == bank]
                    if mine:
                        wait(pe, s_free[bank], st, lambda i: USE[(kind, i + shift, mine[-1])][1])

            def ready(st, kind, nxt, shift):
                if use(kind, st, shift, KD - 1)[0] != use(nxt, st, shift, 0)[0]:
                    taken(st, kind, shift, [KD - 1])

            def turn_x(st, shift):
                wait(pe, s_xn, st, lambda i: i + shift + 1)
                for c in range(KD):
                    bank = free(st, "xt", shift, c)
                    for t in range(TPG):
                        done = pe.transpose(shared[bank][:, t * TR:(t + 1) * TR], xn[:, t, c * 128:(c + 1) * 128],
                                            ident[0:TR, 0:TR])
                    done.then_inc(s_full[bank], 1)

            def project_qkv(st, shift, c):
                if c == 0:
                    wait(pe, s_xT_lo, st, lambda i: KD * (i + shift + 1))
                bank = free(st, "qkv", shift, c)
                w = slice(c * 128, (c + 1) * 128)
                three(shared[bank][:, 0:GT], [(wq_hi[:, k, w], wq_lo[:, k, w], xT_hi[:, k, :], xT_lo[:, k, :])
                                              for k in range(KD)]).then_inc(s_full[bank], 1)

            def turn_values(st, u):
                b, h = u // 2, u % 2
                blocks = range(2 * PAIRS + UP * h, 2 * PAIRS + UP * (h + 1))
                taken(st, "qkv", 0, blocks)
                wait(pe, s_val, st, lambda i: UNITS * i + u)
                for q, c in enumerate(blocks):
                    done = pe.transpose(vt_ps[0:SEQ, q * 128:(q + 1) * 128],
                                        qkv[st.i % 2][:, c, b * SEQ:(b + 1) * SEQ], ident[:, :])
                done.then_inc(s_vt, 1)

            def score(st, u):
                b, h = u // 2, u % 2
                s = slice(b * SEQ, (b + 1) * SEQ)
                taken(st, "qkv", 0, range(2 * UP * h, 2 * UP * (h + 1)))
                wait(pe, s_sub, st, lambda i: UNITS * i + u - 1)
                for q in range(UP):
                    for e in range(2):
                        c, r = 2 * (UP * h + q), slice(HD * e, HD * (e + 1))
                        done = pe.matmul(pair[u % 2][0:SEQ, e, q * SEQ:(q + 1) * SEQ], qkv[st.i % 2][r, c + 1, s],
                                         qkv[st.i % 2][r, c, s], start=True, stop=True)
                done.then_inc(s_score, 1)

            def context(st, u):
                wait(pe, s_exp, st, lambda i: UNITS * i + u + 1)
                wait(pe, s_val, st, lambda i: UNITS * i + u + 1)
                wait(pe, s_c_lo, st, lambda i: UNITS * i + u)
                for q in range(UP):
                    for e in range(2):
                        done = pe.matmul(ct_ps[HD * e:HD * (e + 1), q * SEQ:(q + 1) * SEQ], vals[u % 2][:, 2 * q + e, :],
                                         expo[u % 2][:, UP * e + q, :], start=True, stop=True)
                done.then_inc(s_ctx, 1)

            def project_out(st, shift):
                wait(pe, s_c_lo, st, lambda i: UNITS * (i + shift + 1))
                for c in range(KD):
                    bank = free(st, "proj", shift, c)
                    w = slice(c * 128, (c + 1) * 128)
                    three(shared[bank][:, 0:GT], [(wl_hi[:, k, w], wl_lo[:, k, w], ctx_hi[:, k, :], ctx_lo[:, k, :])
                                                  for k in range(PAIRS)]).then_inc(s_full[bank], 1)

            def turn_y(st, shift):
                ready(st, "proj", "ytr", shift)
                for n, tiles in enumerate((range(2), range(2, TPG))):
                    bank = free(st, "ytr", shift, n)
                    for t in tiles:
                        for c in range(KD):
                            at = (t - tiles[0]) * D + c * 128
                            done = pe.transpose(shared[bank][0:TR, at:at + 128], yT[:, c, t * TR:(t + 1) * TR], ident[:, :])
                    done.then_inc(s_full[bank], 1)

            def turn_x2(st, shift):
                wait(pe, s_x2, st, lambda i: i + shift + 1)
                for c in range(KD):
                    bank = free(st, "x2t", shift, c)
                    for t in range(TPG):
                        done = pe.transpose(shared[bank][:, t * TR:(t + 1) * TR], xn[:, t, c * 128:(c + 1) * 128],
                                            ident[0:TR, 0:TR])
                    done.then_inc(s_full[bank], 1)

            def logit(st, shift):
                ready(st, "x2t", "logit", shift)
                bank = free(st, "logit", shift, 0)
                for t in range(TPG):
                    for c in range(KD):
                        done = pe.matmul(shared[bank][0:TR, t * NEXP:(t + 1) * NEXP], x2T[:, c, t * TR:(t + 1) * TR],
                                         wg_sb[:, c, :], start=(c == 0), stop=(c == KD - 1))
                done.then_inc(s_full[bank], 1)

            pe.wait_ge(s_z1, PT)
            pe.wait_ge(s_zb, 1)
            turn_x(Step(0), 0)
            pe.wait_ge(s_wq_lo, len(PIECES))
            pe.wait_ge(s_wq_lo2, len(PIECES))
            for n, c in enumerate(START):
                project_qkv(Step(0), 0, c)
                if n == 9:
                    score(Step(0), 0)
            pe.wait_ge(s_const, 48)
            pe.wait_ge(s_wl_lo, 2)

            def stage_b(st):
                more, before = st.i + 1 < GROUPS, st.i >= 1
                for u in range(UNITS):
                    turn_values(st, u)
                    if u + 1 < UNITS:
                        score(st, u + 1)
                    elif more:
                        score(Step(st.i + 1, st.k, st.span), 0)
                    if u == 0 and before:
                        project_out(st, -1)
                    if u == 0 and more:
                        turn_x(st, 1)
                    if u == 2 and before:
                        turn_y(st, -1)
                    if u == 4 and before:
                        turn_x2(st, -1)
                    if u == 5 and before:
                        logit(st, -1)
                    blocks = list(qkv_of(u)) if more else []
                    for c in blocks[:-1]:
                        project_qkv(st, 1, c)
                    context(st, u)
                    for c in blocks[-1:]:
                        project_qkv(st, 1, c)

            sweep(pe, stage_b, GROUPS, 1, 1, 2)
            last = Step(GROUPS)
            project_out(last, -1)
            turn_y(last, -1)
            turn_x2(last, -1)
            logit(last, -1)

            pe.wait_ge(s_masks, 4)
            pe.wait_ge(s_chosen, 1)
            pe.matmul(vt_ps[0:TR, 0:NEXP * TOPK * TILES], tri[:, :], chosen_b[:, :, :, :].rearrange("p e k t -> p (e k t)"),
                      start=True, stop=True)
            pe.matmul(ct_ps[0:TR, 0:NEXP * TOPK * TILES], ones[:, :], chosen_b[:, :, :, :].rearrange("p e k t -> p (e k t)"),
                      start=True, stop=True).then_inc(s_rank_ps, 1)

            def turn_slots(st, shift, c):
                p = (st.i + shift) % 2
                wait(pe, s_xg[p], st, lambda i: 16 * ((i + shift) // 2 + 1))
                for h in range(2):
                    n = 2 * c + h
                    wait(pe, s_xe_lo, st, lambda i: 2 * KD * (i + shift) + n - 1)
                    for t in range(3):
                        done = pe.transpose((vt_ps, ct_ps)[h][:, t * XR:(t + 1) * XR],
                                            xg[p][:, 3 * h + t, c * 128:(c + 1) * 128], ident[0:XR, 0:XR])
                    done.then_inc(s_xe, 1)

            pe.wait_ge(s_route, ROUTED)
            for c in range(KD):
                turn_slots(Step(0), 0, c)

            def multiply(st, t, blocks):
                r = slice(t * XR, (t + 1) * XR)
                return three(shared[t % 2][0:XR, 0:D],
                             [(act_hi[:, f, r], act_lo[:, f, r], pj_hi[:, f, :], pj_lo[:, f, :]) for f in blocks],
                             first=blocks[0] == 0, last=blocks[-1] == KF - 1)

            def stage_d(st):
                wait(pe, s_xe_lo, st, lambda i: 2 * KD * (i + 1))
                wait(pe, s_fc_lo, st, lambda i: 4 * (i + 1))
                for f in range(KF):
                    wait(pe, s_gelu, st, lambda i: KF * i + f - 1)
                    w = slice(f * 128, (f + 1) * 128)
                    for h, (a, b) in enumerate(HALVES):
                        done = three(pair[f % 2][:, h, 0:b - a],
                                     [(fc_hi[:, k, w], fc_lo[:, k, w], xe_hi[:, k, a:b], xe_lo[:, k, a:b]) for k in range(KD)])
                    done.then_inc(s_mid, 1)
                wait(pe, s_pj_lo, st, lambda i: 4 * (i + 1))
                for t in range(2):
                    wait(pe, s_yrow, st, lambda i: XT * i + t - 1)
                for f in range(KF):
                    wait(pe, s_act_lo, st, lambda i: KF * i + f + 1)
                    for t in range(2):
                        done = multiply(st, t, range(f, f + 1))
                        if f == KF - 1:
                            done.then_inc(s_y, 1)
                for t in range(2, XT):
                    if t in (3, 4) and st.i + 1 < NEXP:
                        turn_slots(st, 1, t - 3)
                    wait(pe, s_yrow, st, lambda i: XT * i + t - 1)
                    multiply(st, t, range(KF)).then_inc(s_y, 1)

            sweep(pe, stage_d, NEXP, 1, 1, 2)


def kernel(x, txt, L0_tok_ln1_g, L0_tok_ln1_b, L0_tok_W_proj, L0_tok_b_proj, L0_tok_ln2_g, L0_tok_ln2_b,
           L0_tok_cls_token, L0_tok_pos_emb, L0_attn_q_w, L0_attn_q_b, L0_attn_k_w, L0_attn_k_b,
           L0_attn_v_w, L0_attn_v_b, L0_attn_l_w, L0_attn_l_b, L0_ffn_w_g, L0_ffn_c_fc, L0_ffn_c_proj):
    import numpy as np
    import concourse.bacc as bacc
    from concourse.bass_utils import run_bass_kernel_spmd

    def blocks(w):
        return np.asarray(w).reshape(PAIRS, 128, -1)

    side = 96 // 16
    p = np.asarray(x).reshape(BATCH, 3, side, 16, side, 16).transpose(0, 2, 4, 3, 5, 1)
    p = p.reshape(PT, 128, PD)
    q, k, v = blocks(L0_attn_q_w), blocks(L0_attn_k_w), blocks(L0_attn_v_w)
    w_qkv = np.concatenate([np.stack([q, k], 1).reshape(2 * PAIRS, 128, D), v]).transpose(2, 0, 1).reshape(D, NQKV * 128)
    q, k, v = blocks(L0_attn_q_b), blocks(L0_attn_k_b), blocks(L0_attn_v_b)
    b_qkv = np.concatenate([np.stack([q, k], 1).reshape(2 * PAIRS, 128), v.reshape(PAIRS, 128)]).T
    inputs = dict(
        patches=p, txt=txt, ln1_g=np.asarray(L0_tok_ln1_g).reshape(KP, 128).T,
        ln1_b=np.asarray(L0_tok_ln1_b).reshape(KP, 128).T, w_proj=L0_tok_W_proj,
        b_proj=np.asarray(L0_tok_b_proj).reshape(1, D), ln2_g=np.asarray(L0_tok_ln2_g).reshape(1, D),
        ln2_b=np.asarray(L0_tok_ln2_b).reshape(1, D), cls=np.asarray(L0_tok_cls_token).reshape(1, D),
        pos=np.asarray(L0_tok_pos_emb).reshape(NPATCH + 1, D), w_qkv=w_qkv, b_qkv=b_qkv,
        w_l=np.asarray(L0_attn_l_w).T, b_l=np.asarray(L0_attn_l_b).reshape(KD, 128).T, w_g=L0_ffn_w_g,
        c_fc=L0_ffn_c_fc, c_proj=L0_ffn_c_proj, ident_in=np.eye(128, dtype=np.float32))
    nc = bacc.Bacc("TRN2", target_bir_lowering=False, num_devices=1)
    arrays, args = {}, {}
    for name, a in inputs.items():
        arrays[name] = np.ascontiguousarray(a)
        args[name] = nc.dram_tensor(name, arrays[name].shape, mybir.dt.from_np(arrays[name].dtype), kind="ExternalInput").ap()
    out = nc.dram_tensor("out", (TOKENS, D), F32, kind="ExternalOutput").ap()
    program(nc, **args, out=out)
    r = run_bass_kernel_spmd(nc, [arrays], core_ids=[0])
    return r.results[0]["out"].reshape(BATCH, SEQ, D)
```

```python
from contextlib import ExitStack

import concourse.bass as bass
from concourse import mybir

F32 = mybir.dt.float32
F32R = mybir.dt.float32r
BF16 = mybir.dt.bfloat16
I32 = mybir.dt.int32
U32 = mybir.dt.uint32
ALU = mybir.AluOpType
ACT = mybir.ActivationFunctionType
AX = mybir.AxisListType.X

BATCH, SEQ, D = 32, 69, 256
NPATCH, NTXT, PD = 36, 32, 768
HEADS, HD = 16, 64
NEXP, FF, TOPK = 8, 1024, 2
TOKENS = BATCH * SEQ
CAP = TOPK * 5 * TOKENS // (4 * NEXP)
CAP += CAP % 2
EPS = 1e-5
SCALE = HD ** -0.5
KD = D // 128
KP = PD // 128
KF = FF // 128
PAIRS = HEADS // 2

PT = BATCH * NPATCH // 128

PIECES = range(2, 8)
PIECE = 3 * HEADS * HD // len(PIECES)

BPG = 4
GROUPS = BATCH // BPG
GT = BPG * SEQ
TPG = 3
TR = GT // TPG
TILES = GROUPS * TPG
NQKV = 3 * PAIRS
START = [*range(8), *range(16, 20), *range(8, 16), *range(20, NQKV)]
UNITS = 2 * BPG
UH = HEADS // 2
UP = UH // 2

ROW = D + 1 + NEXP
NSLOT = NEXP * CAP
XR = CAP // 6
XT = CAP // XR
HALVES = ((0, CAP // 2 + CAP // 2 % 2), (CAP // 2 + CAP // 2 % 2, CAP))
CHOICES = TOPK * NEXP
PICKS = 11
PLACED = 5
ROUTED = 6
FAR = 1 << 20


def runs(first, count):
    found = []
    for b in range(BPG):
        n = 0
        while n < count:
            t, r = divmod(b * SEQ + first + n, TR)
            m = min(count - n, TR - r)
            found.append((b, n, r, t, m))
            n += m
    return found


POS_RUNS = runs(0, 1 + NPATCH)
PATCH_RUNS = runs(1, NPATCH)
TEXT_RUNS = runs(1 + NPATCH, NTXT)


class Step:

    def __init__(self, i, k=None, span=1):
        self.i, self.k, self.span = i, k, span

    def of(self, f):
        if self.k is None:
            return f(self.i)
        return self.k * (f(self.i + self.span) - f(self.i)) + f(self.i)


def sweep(eng, body, n, head, tail, span):
    for i in range(head):
        body(Step(i))
    with eng.Fori(0, (n - head - tail) // span) as k:
        for i in range(head, head + span):
            body(Step(i, k, span))
    for i in range(n - tail, n):
        body(Step(i))


def wait(eng, sem, step, f):
    assert step.k is None or f(step.i) >= 0
    if step.k is not None or f(step.i) > 0:
        eng.wait_ge(sem, step.of(f))


def wait_apart(eng, sem, step, f):
    wait(eng, sem, step, f)
    if step.k is not None:
        eng.nop(nofuse=True)


def bank_uses():
    order = [("xt", 0, c) for c in range(KD)] + [("qkv", 0, c) for c in START]
    for g in range(GROUPS + 1):
        for u in range(UNITS):
            order += group_uses(g, u)
    return {use: (n % 2, n // 2 + 1) for n, use in enumerate(order)}


def qkv_of(u):
    first = (0, 0, 5, 8, 12, 15, 19, 22, NQKV)
    return range(first[u], first[u + 1])


def group_uses(g, u):
    uses = []
    if g >= 1:
        uses += {0: [("proj", g - 1, c) for c in range(KD)],
                 2: [("ytr", g - 1, 0), ("ytr", g - 1, 1)],
                 4: [("x2t", g - 1, c) for c in range(KD)],
                 5: [("logit", g - 1, 0)],
                 7: [("rank", g - 1, 0)]}.get(u, [])
    if g + 1 < GROUPS:
        if u == 0:
            uses += [("xt", g + 1, c) for c in range(KD)]
        uses += [("qkv", g + 1, c) for c in qkv_of(u)]
    return uses


def program(nc, patches, txt, ln1_g, ln1_b, w_proj, b_proj, ln2_g, ln2_b, cls, pos,
            w_qkv, b_qkv, w_l, b_l, w_g, c_fc, c_proj, ident_in, out):
    USE = bank_uses()
    z_dram = nc.dram_tensor("patch_rows", (PT * 128, D), F32, kind="Internal").ap()
    slots_dram = nc.dram_tensor("slot_rows", (NSLOT, ROW), F32, kind="Internal").ap()

    ctx = ExitStack()
    with ctx:
        def sb(name, shape, dt=F32, stack=ctx):
            return stack.enter_context(nc.sbuf_tensor(name, shape, dt))

        def sem(name):
            return ctx.enter_context(nc.semaphore(name))

        pair = [ctx.enter_context(nc.psum_tensor(f"pair{i}", [128, 2, 512], F32)) for i in range(2)]
        shared = [ctx.enter_context(nc.psum_tensor(f"shared{i}", [128, 512], F32)) for i in range(2)]
        vt_ps = ctx.enter_context(nc.psum_tensor("vt_ps", [128, 512], F32))
        ct_ps = ctx.enter_context(nc.psum_tensor("ct_ps", [128, 512], F32))

        ident = sb("ident", [128, 128])
        rows = sb("rows", [TR, TILES, ROW])
        xg1 = sb("xg1", [XR, XT, ROW])

        pos_sb = sb("pos_sb", [TR, TPG, D])
        tri = sb("tri", [TR, TR], BF16)
        ones = sb("ones", [TR, TR], BF16)
        half = sb("half", [128, TPG])
        minus1 = sb("minus1", [TR, TPG])
        expert = sb("expert", [TR, TPG, NEXP])
        limit = sb("limit", [TR, TPG, NEXP])
        sent = sb("sent", [TR, TPG, ROW])
        logits = sb("logits", [TR, TPG, NEXP])
        is_top = sb("is_top", [TR, TPG, NEXP])
        cand = sb("cand", [TR, TPG, NEXP])
        rest = sb("rest", [TR, TPG, NEXP])
        best = sb("best", [TR, TOPK, TPG])
        first = sb("first", [TR, TOPK, TPG])
        gap = sb("gap", [TR, TPG])
        e_gap = sb("e_gap", [TR, TPG])
        denom = sb("denom", [TR, TPG])
        prob = sb("prob", [TR, TOPK, TPG])
        part = sb("part", [TR, TOPK, TPG, NEXP])
        chosen = sb("chosen", [TR, TILES, TOPK, NEXP])
        chosen_b = sb("chosen_b", [TR, TPG, CHOICES], BF16)
        rank = sb("rank", [TR, TILES, TOPK, NEXP])
        carry = sb("carry", [TR, CHOICES])
        over = sb("over", [TR, TPG, NEXP])
        slot_f = sb("slot_f", [TR, TPG])
        slot_ix = sb("slot_ix", [TR, TPG], I32)
        slot2_f = sb("slot2_f", [TR, TILES])
        slot2_ix = sb("slot2_ix", [TR, TILES], I32)

        bmem = ctx.enter_context(ExitStack())
        wq_hi = sb("wq_hi", [128, KD, NQKV * 128], F32R, bmem)
        wq_lo = sb("wq_lo", [128, KD, NQKV * 128], F32R, bmem)
        wl_hi = sb("wl_hi", [128, PAIRS, D], F32R, bmem)
        wl_lo = sb("wl_lo", [128, PAIRS, D], F32R, bmem)
        qkv = [sb(f"qkv{i}", [128, NQKV, GT], F32, bmem) for i in range(2)]
        ctx_hi = sb("ctx_hi", [128, PAIRS, GT], F32R, bmem)
        ctx_lo = sb("ctx_lo", [128, PAIRS, GT], F32R, bmem)
        bq_sb = sb("bq_sb", [128, NQKV], F32, bmem)
        bl_sb = sb("bl_sb", [128, KD], F32, bmem)
        wg_sb = sb("wg_sb", [128, KD, NEXP], F32, bmem)

        z_stat = sb("z_stat", [128, 6], F32, bmem)
        z_mv = sb("z_mv", [128, 2], F32, bmem)
        z_rs = sb("z_rs", [128, 1], F32, bmem)
        z_row = [sb(f"z_row{i}", [128, D], F32, bmem) for i in range(2)]
        g2_sb = sb("g2_sb", [128, D], F32, bmem)
        b2_sb = sb("b2_sb", [128, D], F32, bmem)
        zb_sb = sb("zb_sb", [128, D], F32, bmem)
        with ExitStack() as amem:
            pT_hi = [sb(f"pT_hi{i}", [128, KP, 128], F32R, amem) for i in range(2)]
            pT_lo = [sb(f"pT_lo{i}", [128, KP, 128], F32R, amem) for i in range(2)]
            a_stat = sb("a_stat", [128, 2, 6], F32, amem)
            a_mv = sb("a_mv", [128, 2], F32, amem)
            a_rs = sb("a_rs", [128, 1], F32, amem)
            wp_g = sb("wp_g", [128, KP, D], F32, amem)
            g1_sb = sb("g1_sb", [128, KP], F32, amem)
            b1_sb = sb("b1_sb", [128, KP], F32, amem)
        flat0 = qkv[0][:, :, :].rearrange("p c n -> p (c n)")
        flat1 = qkv[1][:, :, :].rearrange("p c n -> p (c n)")
        wq_raw = flat1[:, 0:KD * NQKV * 128].rearrange("p (k n) -> p k n", k=KD)
        wl_raw = flat0[:, 0:PAIRS * D].rearrange("p (k n) -> p k n", k=PAIRS)
        at = PAIRS * D
        wp_raw = flat0[:, at:at + KP * D].rearrange("p (k n) -> p k n", k=KP)
        at += KP * D
        patch = [flat0[:, at + i * PD:at + (i + 1) * PD] for i in range(2)]
        at += 2 * PD
        b1_wide = flat0[:, at:at + KP * 128].rearrange("p (k n) -> p k n", k=KP)
        wp_hi = ctx_hi[:, :, :].rearrange("p c n -> p (c n)")[:, 0:KP * D].rearrange("p (k n) -> p k n", k=KP)
        wp_lo = ctx_lo[:, :, :].rearrange("p c n -> p (c n)")[:, 0:KP * D].rearrange("p (k n) -> p k n", k=KP)

        with ExitStack() as smem:
            xT_hi = sb("xT_hi", [128, KD, GT], F32R, smem)
            xT_lo = sb("xT_lo", [128, KD, GT], F32R, smem)
            expo = [sb(f"expo{i}", [SEQ, UH, SEQ], F32, smem) for i in range(2)]
            vals = [sb(f"vals{i}", [SEQ, UH, HD], F32, smem) for i in range(2)]
            top = sb("top", [SEQ, UH], F32, smem)
            zsum = sb("zsum", [SEQ, UH], F32, smem)
            zinv = sb("zinv", [SEQ, UH], F32, smem)
            yT = sb("yT", [128, KD, GT], F32, smem)
            x2T = sb("x2T", [128, KD, GT], F32, smem)
            xn = sb("xn", [TR, TPG, D], F32, smem)
            h2 = sb("h2", [TR, TPG, D], F32, smem)
            n_stat = sb("n_stat", [TR, TPG, 6], F32, smem)
            n_mv = sb("n_mv", [TR, TPG, 2], F32, smem)
            n_rs = sb("n_rs", [TR, TPG], F32, smem)
            m_stat = sb("m_stat", [TR, TPG, 6], F32, smem)
            m_mv = sb("m_mv", [TR, TPG, 2], F32, smem)
            m_rs = sb("m_rs", [TR, TPG], F32, smem)
        bmem.close()

        with ExitStack() as cmem:
            over2 = sb("over2", [TR, TILES, NEXP], F32, cmem)
            slot2 = sb("slot2", [TR, TILES, NEXP], F32, cmem)
            raw_fc = sb("raw_fc", [128, KD, FF], F32, cmem)
            raw_pj = sb("raw_pj", [128, KF, D], F32, cmem)
            fc_hi = sb("fc_hi", [128, KD, FF], F32R, cmem)
            fc_lo = sb("fc_lo", [128, KD, FF], F32R, cmem)
            pj_hi = sb("pj_hi", [128, KF, D], F32R, cmem)
            pj_lo = sb("pj_lo", [128, KF, D], F32R, cmem)
            xe_hi = sb("xe_hi", [128, KD, CAP], F32R, cmem)
            xe_lo = sb("xe_lo", [128, KD, CAP], F32R, cmem)
            act_f = [sb(f"act_f{i}", [128, CAP], F32, cmem) for i in range(2)]
            act_hi = sb("act_hi", [128, KF, CAP], F32R, cmem)
            act_lo = sb("act_lo", [128, KF, CAP], F32R, cmem)
            xg = [sb("xg0", [XR, XT, ROW], F32, cmem), xg1]
            yrow = [sb(f"yrow{i}", [XR, XT, D], F32, cmem) for i in range(2)]

        s_const, s_wp, s_small, s_wll = (sem(n) for n in ("s_const", "s_wp", "s_small", "s_wll"))
        s_wql = [sem(f"s_wql{i}") for i in range(2)]
        s_patch = [sem(f"s_patch{i}") for i in range(2)]
        s_pos, s_ident, s_wq_lo2, s_x2c = (sem(n) for n in ("s_pos", "s_ident", "s_wq_lo2", "s_x2c"))
        s_a_rs, s_z_rs, s_n_rs, s_m_rs, s_half = (sem(n) for n in ("s_a_rs", "s_z_rs", "s_n_rs", "s_m_rs", "s_half"))
        s_rest_rows = sem("s_rest_rows")
        s_zdma = [sem(f"s_zdma{i}") for i in range(2)]
        s_rows = [sem(f"s_rows{i}") for i in range(2)]
        s_a_ln, s_pn, s_pT, s_pT_hi, s_pT_lo, s_z, s_z1, s_zn, s_zrow, s_wp_s, s_wp_hi, s_wp_lo, s_b1w, s_bw, s_zb = (
            sem(n) for n in ("s_a_ln", "s_pn", "s_pT", "s_pT_hi", "s_pT_lo", "s_z", "s_z1", "s_zn", "s_zrow",
                             "s_wp_s", "s_wp_hi", "s_wp_lo", "s_b1w", "s_bw", "s_zb"))
        s_z_ln, s_zmul = sem("s_z_ln"), sem("s_zmul")
        s_wq_hi, s_wq_lo, s_wl_hi, s_wl_lo = (sem(n) for n in ("s_wq_hi", "s_wq_lo", "s_wl_hi", "s_wl_lo"))
        s_full = [sem(f"s_full{i}") for i in range(2)]
        s_free = [sem(f"s_free{i}") for i in range(2)]
        s_h, s_n_ln, s_xn, s_xT_hi, s_xT_lo, s_qkv = (sem(n) for n in ("s_h", "s_n_ln", "s_xn", "s_xT_hi", "s_xT_lo", "s_qkv"))
        s_vt, s_score, s_top, s_sub, s_exp, s_zs, s_zi, s_val, s_ctx, s_c_hi, s_c_lo = (
            sem(n) for n in ("s_vt", "s_score", "s_top", "s_sub", "s_exp", "s_zs", "s_zi", "s_val", "s_ctx", "s_c_hi", "s_c_lo"))
        s_yT, s_h2, s_m_ln, s_x2, s_x2T, s_logit, s_h2_out = (
            sem(n) for n in ("s_yT", "s_h2", "s_m_ln", "s_x2", "s_x2T", "s_logit", "s_h2_out"))
        s_masks, s_pick, s_place, s_route, s_chosen, s_rank, s_gap, s_egap, s_prob, s_weights, s_fill, s_first, s_sent = (
            sem(n) for n in ("s_masks", "s_pick", "s_place", "s_route", "s_chosen", "s_rank", "s_gap", "s_egap",
                             "s_prob", "s_weights", "s_fill", "s_first", "s_sent"))
        s_pool = sem("s_pool")
        s_fcl, s_pjl, s_fc_hi, s_fc_lo, s_pj_hi, s_pj_lo = (
            sem(n) for n in ("s_fcl", "s_pjl", "s_fc_hi", "s_fc_lo", "s_pj_hi", "s_pj_lo"))
        s_xg = [sem(f"s_xg{i}") for i in range(2)]
        s_xe, s_xe_hi, s_xe_lo, s_mid, s_gelu, s_act_hi, s_act_lo, s_y, s_yrow, s_added = (
            sem(n) for n in ("s_xe", "s_xe_hi", "s_xe_lo", "s_mid", "s_gelu", "s_act_hi", "s_act_lo", "s_y", "s_yrow", "s_added"))

        def use(kind, step, shift, c):
            bank = USE[(kind, step.i + shift, c)][0]
            return bank, lambda i: USE[(kind, i + shift, c)][1]

        def f32(ap):
            return ap.bitcast(F32)

        def piece(st):
            c = st.of(lambda i: (i - 2) * PIECE)
            return slice(c, c + PIECE) if st.k is None else bass.ds(c, PIECE)

        block = ctx.enter_context(nc.Block())

        @block.sync
        def _(sp):
            sp.dma_start(patch[0], patches[0]).then_inc(s_patch[0], 16)
            sp.dma_start(wp_raw, w_proj.rearrange("(k p) n -> p k n", p=128)).then_inc(s_wp, 16)
            sp.dma_start(ident[:, :], ident_in).then_inc(s_ident, 16)
            sp.dma_start(g1_sb[:, :], ln1_g).then_inc(s_small, 16)
            sp.dma_start(b1_sb[:, :], ln1_b).then_inc(s_small, 16)
            sp.dma_start(g2_sb[:, :], ln2_g.broadcast_to([128, D])).then_inc(s_small, 16)
            sp.dma_start(b2_sb[:, :], ln2_b.broadcast_to([128, D])).then_inc(s_small, 16)
            sp.dma_start(zb_sb[:, :], b_proj.broadcast_to([128, D])).then_inc(s_small, 16)
            sp.dma_start(patch[1], patches[1]).then_inc(s_patch[1], 16)
            sp.dma_start(bq_sb[:, :], b_qkv).then_inc(s_const, 16)
            sp.dma_start(bl_sb[:, :], b_l).then_inc(s_const, 16)
            sp.dma_start(wg_sb[:, :, :], w_g.rearrange("(k p) n -> p k n", p=128)).then_inc(s_const, 16)
            every = rows[:, :, 0:D].rearrange("p (g t) d -> p t g d", t=TPG)
            txt_seq = txt.rearrange("(g b) s d -> b s g d", b=BPG)
            for b in range(BPG):
                t, r = divmod(b * SEQ, TR)
                sp.dma_start(every[r:r + 1, t, :, :], cls.unsqueeze(1).broadcast_to([1, GROUPS, D])).then_inc(s_rest_rows, 16)
            for b, n, r, t, m in TEXT_RUNS:
                sp.dma_start(every[r:r + m, t, :, :], txt_seq[b, n:n + m, :, :]).then_inc(s_rest_rows, 16)
            sp.dma_start(wl_raw, w_l.rearrange("(k p) n -> p k n", p=128)).then_inc(s_wll, 16)
            sp.wait_ge(s_pool, 1)
            for _, n, r, t, m in POS_RUNS:
                sp.dma_start(pos_sb[r:r + m, t, :], pos[n:n + m, :]).then_inc(s_pos, 16)

            def load_rows(st, shift):
                g = st.of(lambda i: i + shift)
                for n in range(2):
                    wait_apart(sp, s_zdma[(st.i + shift + n) % 2], st, lambda i: 16 * ((i + shift + n) // 2 + 1))
                if st.i + shift >= 2:
                    wait_apart(sp, s_rows[(st.i + shift) % 2], st, lambda i: 16 * len(PATCH_RUNS) * ((i + shift) // 2))
                for b, n, r, t, m in PATCH_RUNS:
                    sp.dma_start(rows[r:r + m, bass.ds(g * TPG + t, 1), 0:D],
                                 z_dram[bass.ds((g * BPG + b) * NPATCH + n, m), :].rearrange("(m o) d -> m o d", o=1))\
                      .then_inc(s_rows[(st.i + shift) % 2], 16)

            def stage_a(st):
                if st.i in PIECES:
                    w = piece(st)
                    sp.dma_start(wq_raw[:, :, w], w_qkv.rearrange("(k p) n -> p k n", p=128)[:, :, w])\
                      .then_inc(s_wql[st.i % 2], 16)
                if st.i + 2 < PT:
                    wait_apart(sp, s_pT, st, lambda i: i + 1)
                    j = st.of(lambda i: i + 2)
                    sp.dma_start(patch[st.i % 2], patches[bass.ds(j, 1), :, :].rearrange("o p n -> (o p) n"))\
                      .then_inc(s_patch[st.i % 2], 16)
                if PT - 2 <= st.i <= PT:
                    load_rows(Step(st.i), 2 - PT)
                if st.i >= 2:
                    j = st.of(lambda i: i - 2)
                    wait_apart(sp, s_zrow, st, lambda i: i - 1)
                    sp.dma_start(z_dram[bass.ds(j * 128, 128), :], z_row[st.i % 2][:, :]).then_inc(s_zdma[st.i % 2], 16)
            sweep(sp, stage_a, PT + 2, 3, 4, 2)

            sp.wait_ge(s_pool, 3)
            for e in range(NEXP):
                sp.dma_start(slots_dram[e * CAP:(e + 1) * CAP, :].rearrange("(t p) n -> p t n", p=XR),
                             xg[1][:, :, :]).then_inc(s_fill, 16)

            out_tile = out.rearrange("(t p) d -> p t d", p=TR)

            def stage_b(st):
                if st.i + 3 < GROUPS:
                    load_rows(st, 3)
                g = st.of(lambda i: i)
                wait_apart(sp, s_h2, st, lambda i: i + 1)
                sp.dma_start(out_tile[:, bass.ds(g * TPG, TPG), :], h2[:, :, :]).then_inc(s_h2_out, 16)

            sweep(sp, stage_b, GROUPS, 0, 4, 2)

            def load_fc(e):
                sp.dma_start(raw_fc[:, :, :], c_fc[e].rearrange("o (k p) n -> p (o k) n", p=128)).then_inc(s_fcl, 16)

            def load_pj(e):
                sp.dma_start(raw_pj[:, :, :], c_proj[e].rearrange("o (k p) n -> p (o k) n", p=128)).then_inc(s_pjl, 16)

            def load_slots(e, p):
                sp.dma_start(xg[p][:, :, :],
                             slots_dram[bass.ds(e * CAP, CAP), :].rearrange("(t p) n -> p t n", p=XR))\
                  .then_inc(s_xg[p], 16)

            bank, n = USE[("logit", GROUPS - 1, 0)]
            sp.wait_ge(s_full[bank], n)
            sp.wait_ge(s_c_lo, UNITS * GROUPS)
            sp.wait_ge(s_free[0], USE[("logit", GROUPS - 1, 0)][1] - 1)
            load_fc(slice(0, 1))
            load_pj(slice(0, 1))
            sp.wait_ge(s_first, 16 * TILES)
            sp.wait_ge(s_sent, 16 * TILES)
            load_slots(0, 0)

            def stage_d(st):
                if st.i + 1 < NEXP:
                    nxt = st.of(lambda i: i + 1)
                    if st.i >= 1:
                        wait_apart(sp, s_added, st, lambda i: 16 * XT * i)
                    load_slots(nxt, (st.i + 1) % 2)
                    wait_apart(sp, s_fc_lo, st, lambda i: 4 * (i + 1))
                    load_fc(bass.ds(nxt, 1))
                    wait_apart(sp, s_pj_lo, st, lambda i: 4 * (i + 1))
                    load_pj(bass.ds(nxt, 1))

            sweep(sp, stage_d, NEXP, 1, 1, 2)
            sp.wait_ge(s_h2_out, 16 * GROUPS)
            sp.wait_ge(s_added, 16 * XT * NEXP)

        @block.gpsimd
        def _(pool):
            pool.memset(half[:, :], -0.5).then_inc(s_half, 1)
            pool.memset(pos_sb[:, :, :], 0.0).then_inc(s_pool, 1)
            pool.memset(xg[1][:, :, :], 0.0).then_inc(s_pool, 1)
            pool.wait_ge(s_pool, 2)
            pool.memset(xg[1][:, :, D:D + 1].bitcast(I32), FAR).then_inc(s_pool, 1)
            pool.memset(ones[:, :], 1.0).then_inc(s_masks, 1)
            pool.memset(tri[:, :], 1.0).then_inc(s_masks, 1)
            pool.memset(minus1[:, :], -1.0).then_inc(s_masks, 1)
            pool.memset(carry[:, :], 0.0).then_inc(s_masks, 1)
            pool.wait_ge(s_masks, 4)
            pool.affine_select(out=tri[:, :], in_=tri[:, :], compare_op=ALU.is_gt, fill=0.0, base=0,
                               pattern=[[1, TR]], channel_multiplier=-1).then_inc(s_masks, 1)
            pool.iota(carry[:, 0:NEXP], pattern=[[CAP, NEXP]], base=0, channel_multiplier=0,
                      allow_small_or_imprecise_dtypes=True).then_inc(s_masks, 1)
            pool.iota(expert[:, :, :], pattern=[[0, TPG], [1, NEXP]], base=0, channel_multiplier=0,
                      allow_small_or_imprecise_dtypes=True).then_inc(s_masks, 1)
            pool.iota(limit[:, :, :], pattern=[[0, TPG], [CAP, NEXP]], base=CAP, channel_multiplier=0,
                      allow_small_or_imprecise_dtypes=True).then_inc(s_masks, 1)
            pool.iota(rows[:, :, D:D + 1].bitcast(I32), pattern=[[TR, TILES], [0, 1]], base=0, channel_multiplier=1)\
                .then_inc(s_masks, 1)

            def root(rs, st, ready, f, done):
                wait(pool, ready, st, f)
                pool.tensor_tensor(rs, rs, half[0:rs.shape[0], 0:rs.shape[1]], ALU.pow).then_inc(done, 1)

            def add_positions(st, shift):
                g = st.of(lambda i: i + shift)
                wait(pool, s_rows[(st.i + shift) % 2], st, lambda i: 16 * len(PATCH_RUNS) * ((i + shift) // 2 + 1))
                r = rows[:, g * TPG:(g + 1) * TPG, 0:D] if st.k is None else rows[:, bass.ds(g * TPG, TPG), 0:D]
                pool.tensor_tensor(r, r, pos_sb[:, :, :], ALU.add).then_inc(s_h, 1)

            def root_in(st, shift):
                root(n_rs[:, :], st, s_n_ln, lambda i: 3 * (i + shift + 1), s_n_rs)

            def stage_a(st):
                if st.i == PT - 1:
                    pool.wait_ge(s_pos, 16 * len(POS_RUNS))
                    pool.wait_ge(s_rest_rows, 16 * (BPG + len(TEXT_RUNS)))
                    add_positions(Step(0), 0)
                if st.i == PT:
                    root_in(Step(0), 0)
                if st.i + 1 < PT:
                    root(a_rs[:, :], st, s_a_ln, lambda i: 3 * (i + 2), s_a_rs)
                if st.i >= 2:
                    p = st.i % 2
                    wait(pool, s_zn, st, lambda i: i - 1)
                    pool.tensor_tensor(z_row[p][:, :], z_row[p][:, :], g2_sb[:, :], ALU.mult).then_inc(s_zmul, 1)
                    wait(pool, s_zmul, st, lambda i: i - 1)
                    pool.tensor_tensor(z_row[p][:, :], z_row[p][:, :], b2_sb[:, :], ALU.add).then_inc(s_zrow, 1)
                if 1 <= st.i <= PT:
                    root(z_rs[:, :], st, s_z_ln, lambda i: 3 * i, s_z_rs)
                if st.i in PIECES:
                    w = piece(st)
                    wait(pool, s_wq_hi, st, lambda i: i - 1)
                    pool.tensor_tensor(wq_lo[:, 0, w], wq_raw[:, 0, w], f32(wq_hi[:, 0, w]), ALU.subtract)\
                        .then_inc(s_wq_lo, 1)

            pool.wait_ge(s_half, 1)
            root(a_rs[:, :], Step(0), s_a_ln, lambda i: 3, s_a_rs)
            pool.wait_ge(s_small, 80)
            sweep(pool, stage_a, PT + 2, 3, 4, 2)

            def root_mid(st, shift):
                if st.i + shift >= 1:
                    wait_apart(pool, s_first, st, lambda i: 16 * TPG * (i + shift))
                root(m_rs[:, :], st, s_m_ln, lambda i: 3 * (i + shift + 1), s_m_rs)
                g = st.of(lambda i: i + shift)
                wait_apart(pool, s_x2, st, lambda i: i + shift + 1)
                t = slice(g * TPG, (g + 1) * TPG) if st.k is None else bass.ds(g * TPG, TPG)
                pool.tensor_copy(sent[:, :, D:D + 1].bitcast(I32), rows[:, t, D:D + 1].bitcast(I32)).then_inc(s_x2c, 1)
                pool.tensor_copy(rows[:, t, 0:D], sent[:, :, 0:D]).then_inc(s_x2c, 1)

            def weigh(st, shift):
                g = st.of(lambda i: i + shift)
                t = slice(g * TPG, (g + 1) * TPG) if st.k is None else bass.ds(g * TPG, TPG)

                def before(n):
                    wait(pool, s_prob, st, lambda i: 6 * (i + shift) + n)

                wait(pool, s_pick, st, lambda i: PICKS * (i + shift + 1))
                pool.tensor_tensor(gap[:, :], best[:, 1, :], best[:, 0, :], ALU.subtract).then_inc(s_gap, 1)
                wait(pool, s_egap, st, lambda i: i + shift + 1)
                pool.tensor_tensor(denom[:, :], e_gap[:, :], minus1[:, :], ALU.subtract).then_inc(s_prob, 1)
                before(1)
                pool.tensor_tensor(prob[:, 0, :], denom[:, :], minus1[:, :], ALU.pow).then_inc(s_prob, 1)
                before(2)
                pool.tensor_tensor(prob[:, 1, :], prob[:, 0, :], e_gap[:, :], ALU.mult).then_inc(s_prob, 1)
                before(3)
                for k in range(TOPK):
                    pool.tensor_tensor(part[:, k, :, :], chosen[:, t, k, :],
                                       prob[:, k, :].unsqueeze(2).broadcast_to([TR, TPG, NEXP]), ALU.mult).then_inc(s_prob, 1)
                before(5)
                pool.tensor_tensor(sent[:, :, D + 1:], part[:, 0, :, :], part[:, 1, :, :], ALU.add).then_inc(s_prob, 1)
                pool.tensor_tensor(rows[:, t, D + 1:], part[:, 0, :, :], part[:, 1, :, :], ALU.add).then_inc(s_weights, 1)

            def send_first(st, shift):
                wait(pool, s_prob, st, lambda i: 6 * (i + shift + 1))
                wait(pool, s_place, st, lambda i: PLACED * (i + shift + 1))
                wait(pool, s_x2c, st, lambda i: 2 * (i + shift + 1))
                if st.k is not None:
                    pool.nop(nofuse=True)
                for t in range(TPG):
                    pool.indirect_dma_start(slots_dram, bass.IndirectOffsetOnAxis(ap=slot_ix[:, t:t + 1].bitcast(U32), axis=0),
                                            sent[:, t, :], None, bounds_check=NSLOT - 1, oob_is_err=False)\
                        .then_inc(s_first, 16)

            def stage_b(st):
                if st.i + 1 < GROUPS:
                    root_in(st, 1)
                if st.i >= 2:
                    send_first(st, -2)
                if st.i + 2 < GROUPS:
                    add_positions(st, 2)
                if st.i >= 1:
                    root_mid(st, -1)
                    weigh(st, -1)
                if st.i == 0:
                    pool.wait_ge(s_masks, 9)
                    pool.wait_ge(s_fill, 16 * NEXP)

            add_positions(Step(0), 1)
            sweep(pool, stage_b, GROUPS, 2, 2, 2)
            send_first(Step(GROUPS), -2)
            root_mid(Step(GROUPS), -1)
            weigh(Step(GROUPS), -1)
            send_first(Step(GROUPS), -1)

            pool.wait_ge(s_x2c, 2 * GROUPS)
            pool.wait_ge(s_weights, GROUPS)
            pool.wait_ge(s_route, ROUTED)
            for n in range(TILES):
                pool.indirect_dma_start(slots_dram, bass.IndirectOffsetOnAxis(ap=slot2_ix[:, n:n + 1].bitcast(U32), axis=0),
                                        rows[:, n, :], None, bounds_check=NSLOT - 1, oob_is_err=False)\
                    .then_inc(s_sent, 16)

            def stage_d(st):
                p = st.i % 2
                wait(pool, s_added, st, lambda i: 16 * XT * i)
                if st.i == 0:
                    pool.wait_ge(s_h2_out, 16 * GROUPS)
                for t in range(XT):
                    wait_apart(pool, s_yrow, st, lambda i: XT * i + t + 1)
                    pool.indirect_dma_start(out, bass.IndirectOffsetOnAxis(ap=xg[p][:, t, D:D + 1].bitcast(U32), axis=0),
                                            yrow[p][:, t, :], None, bounds_check=TOKENS - 1, oob_is_err=False,
                                            compute_op=ALU.add).then_inc(s_added, 16)

            sweep(pool, stage_d, NEXP, 1, 1, 2)

        @block.scalar
        def _(act):
            act.wait_ge(s_wp_s, KP)
            act.activation(wp_hi, wp_g[:, :, :], ACT.Copy).then_inc(s_wp_hi, 1)

            def stage_a(st):
                if st.i < PT:
                    p = st.i % 2
                    wait(act, s_pT, st, lambda i: i + 1)
                    wait(act, s_z, st, lambda i: i - 1)
                    for h in range(2):
                        act.activation(pT_hi[p][:, 3 * h:3 * h + 3, :],
                                       pair[p][:, h, 0:384].rearrange("p (k n) -> p k n", k=3), ACT.Copy)\
                            .then_inc(s_pT_hi, 1)
                if st.i in PIECES:
                    w = piece(st)
                    wait(act, s_wql[st.i % 2], st, lambda i: 16 * (i // 2))
                    act.activation(wq_hi[:, :, w], wq_raw[:, :, w], ACT.Copy).then_inc(s_wq_hi, 1)
                if st.i in (PT - 1, PT):
                    act.wait_ge(s_wll, 16)
                    w = slice((st.i - PT + 1) * 4, (st.i - PT + 2) * 4)
                    act.activation(wl_hi[:, w, :], wl_raw[:, w, :], ACT.Copy).then_inc(s_wl_hi, 1)

            sweep(act, stage_a, PT + 2, 3, 4, 2)
            def put_qkv(st, shift, c):
                bank, nth = use("qkv", st, shift, c)
                wait(act, s_full[bank], st, nth)
                act.activation(qkv[(st.i + shift) % 2][:, c, :], shared[bank][:, 0:GT], ACT.Identity,
                               bias=bq_sb[:, c:c + 1]).then_inc(s_free[bank], 1)

            def put_xT(st, shift):
                for c in range(KD):
                    bank, nth = use("xt", st, shift, c)
                    wait(act, s_full[bank], st, nth)
                    act.activation(xT_hi[:, c, :], shared[bank][:, 0:GT], ACT.Copy).then_inc(s_xT_hi, 1)

            def put_exp(st, u):
                n = lambda i: UNITS * i + u + 1
                wait(act, s_sub, st, lambda i: n(i) + 1)
                e = expo[(u + 1) % 2][:, :, :]
                act.activation(e, e, ACT.Exp, scale=SCALE).then_inc(s_exp, 1)

            def put_ctx(st, u):
                wait(act, s_ctx, st, lambda i: UNITS * i + u + 1)
                act.activation(ctx_hi[:, UP * (u % 2):UP * (u % 2 + 1), SEQ * (u // 2):SEQ * (u // 2 + 1)],
                               ct_ps[:, 0:UP * SEQ].rearrange("p (k n) -> p k n", k=UP), ACT.Copy)\
                    .then_inc(s_c_hi, 1)

            def put_y(st, shift):
                for c in range(KD):
                    bank, nth = use("proj", st, shift, c)
                    wait(act, s_full[bank], st, nth)
                    act.activation(yT[:, c, :], shared[bank][:, 0:GT], ACT.Identity,
                                   bias=bl_sb[:, c:c + 1]).then_inc(s_free[bank], 1)

            def put_gap(st, shift):
                wait(act, s_gap, st, lambda i: i + shift + 1)
                act.activation(e_gap[:, :], gap[:, :], ACT.Exp).then_inc(s_egap, 1)

            def put_x2T(st, shift):
                for c in range(KD):
                    bank, nth = use("x2t", st, shift, c)
                    wait(act, s_full[bank], st, nth)
                    act.activation(x2T[:, c, :], shared[bank][:, 0:GT], ACT.Copy).then_inc(s_free[bank], 1)

            act.wait_ge(s_const, 48)
            act.wait_ge(s_wl_lo, 2)
            put_xT(Step(0), 0)
            for n, c in enumerate(START):
                put_qkv(Step(0), 0, c)
                if n == 11:
                    put_exp(Step(-1), UNITS - 1)

            def stage_b(st):
                more, before = st.i + 1 < GROUPS, st.i >= 1
                for u in range(UNITS):
                    blocks = list(qkv_of(u)) if more else []
                    if u == 4 and before:
                        put_x2T(st, -1)
                    for c in blocks[:-1][:2]:
                        put_qkv(st, 1, c)
                    if u == 0 and before:
                        put_y(st, -1)
                    if more or u + 1 < UNITS:
                        put_exp(st, u)
                    for c in blocks[:-1][2:]:
                        put_qkv(st, 1, c)
                    if u == 0 and more:
                        put_xT(st, 1)
                    put_ctx(st, u)
                    for c in blocks[-1:]:
                        put_qkv(st, 1, c)
                    if u == 7 and before:
                        put_gap(st, -1)

            sweep(act, stage_b, GROUPS, 1, 1, 2)
            put_y(Step(GROUPS), -1)
            put_x2T(Step(GROUPS), -1)
            put_gap(Step(GROUPS), -1)

            def split_fc(st, shift, q):
                wait(act, s_fcl, st, lambda i: 16 * (i + shift + 1))
                wait(act, s_mid, st, lambda i: KF * (i + shift))
                w = slice(q * FF // 4, (q + 1) * FF // 4)
                act.activation(fc_hi[:, :, w], raw_fc[:, :, w], ACT.Copy).then_inc(s_fc_hi, 1)

            def split_pj(st, q):
                wait(act, s_pjl, st, lambda i: 16 * (i + 1))
                wait(act, s_y, st, lambda i: XT * i)
                w = slice(q * KF // 4, (q + 1) * KF // 4)
                act.activation(pj_hi[:, w, :], raw_pj[:, w, :], ACT.Copy).then_inc(s_pj_hi, 1)

            def put_xe(st, shift):
                for n in range(2 * KD):
                    c, h = n // 2, n % 2
                    wait(act, s_xe, st, lambda i: 2 * KD * (i + shift) + n + 1)
                    bank = (vt_ps, ct_ps)[h]
                    act.activation(xe_hi[:, c, h * 3 * XR:(h + 1) * 3 * XR], bank[:, 0:3 * XR], ACT.Copy)\
                        .then_inc(s_xe_hi, 1)

            for q in range(4):
                split_fc(Step(0), 0, q)
            put_xe(Step(0), 0)

            def stage_d(st):
                for f in range(KF):
                    wait(act, s_mid, st, lambda i: KF * i + f + 1)
                    wait(act, s_act_lo, st, lambda i: KF * i + f - 1)
                    for h, (a, b) in enumerate(HALVES):
                        gelu = act.activation(act_f[f % 2][:, a:b], pair[f % 2][:, h, 0:b - a], ACT.Gelu)
                    gelu.then_inc(s_gelu, 1)
                    if f < 4:
                        split_pj(st, f)
                if st.i + 1 < NEXP:
                    for q in range(4):
                        split_fc(st, 1, q)
                    put_xe(st, 1)

            sweep(act, stage_d, NEXP, 1, 1, 2)

        @block.vector
        def _(dve):
            def norm_patches(st, shift):
                p = (st.i + shift) % 2
                wait(dve, s_patch[p], st, lambda i: 16 * ((i + shift) // 2 + 1))
                x = patch[p]
                for h in range(2):
                    stats = dve.bn_stats(a_stat[:, h, :], x[:, h * 384:(h + 1) * 384])
                stats.then_inc(s_a_ln, 1)
                wait_apart(dve, s_a_ln, st, lambda i: 3 * (i + shift) + 1)
                dve.bn_aggr(a_mv[:, :], a_stat[:, :, :].rearrange("p a b -> p (a b)")).then_inc(s_a_ln, 1)
                wait(dve, s_a_ln, st, lambda i: 3 * (i + shift) + 2)
                dve.tensor_scalar(a_rs[:, :], a_mv[:, 1:2], EPS, None, ALU.add).then_inc(s_a_ln, 1)

            def norm_patches_end(st, shift):
                p = (st.i + shift) % 2
                x = patch[p]
                wait(dve, s_a_rs, st, lambda i: i + shift + 1)
                dve.tensor_scalar(x, x, a_mv[:, 0:1], a_rs[:, 0:1], ALU.subtract, ALU.mult).then_inc(s_pn, 1)

            def low_patches(st):
                p = st.i % 2
                for h in range(2):
                    wait(dve, s_pT_hi, st, lambda i: 2 * i + h + 1)
                    dve.tensor_tensor(pT_lo[p][:, 3 * h:3 * h + 3, :],
                                      pair[p][:, h, 0:384].rearrange("p (k n) -> p k n", k=3),
                                      f32(pT_hi[p][:, 3 * h:3 * h + 3, :]), ALU.subtract).then_inc(s_pT_lo, 1)

            def norm_z(st):
                p = (st.i - 1) % 2
                z = z_row[p][:, :]
                wait(dve, s_z, st, lambda i: i)
                wait(dve, s_zdma[p], st, lambda i: 16 * ((i - 1) // 2))
                dve.tensor_tensor(z, shared[p][:, 0:D], zb_sb[:, :], ALU.add).then_inc(s_z1, 1)
                wait(dve, s_z1, st, lambda i: i)
                dve.bn_stats(z_stat[:, :], z).then_inc(s_z_ln, 1)
                wait_apart(dve, s_z_ln, st, lambda i: 3 * (i - 1) + 1)
                dve.bn_aggr(z_mv[:, :], z_stat[:, :]).then_inc(s_z_ln, 1)
                wait(dve, s_z_ln, st, lambda i: 3 * (i - 1) + 2)
                dve.tensor_scalar(z_rs[:, :], z_mv[:, 1:2], EPS, None, ALU.add).then_inc(s_z_ln, 1)

            def norm_z_end(st):
                z = z_row[st.i % 2][:, :]
                wait(dve, s_z_rs, st, lambda i: i - 1)
                dve.tensor_scalar(z, z, z_mv[:, 0:1], z_rs[:, 0:1], ALU.subtract, ALU.mult).then_inc(s_zn, 1)

            def rows_of(st, shift):
                g = st.of(lambda i: i + shift)
                if st.k is None:
                    return [rows[:, g * TPG + t, 0:D] for t in range(TPG)]
                return [rows[:, bass.ds(g * TPG + t, 1), 0:D].rearrange("p o d -> p (o d)") for t in range(TPG)]

            def norm_in(st, shift):
                src = rows_of(st, shift)
                wait(dve, s_h, st, lambda i: i + shift + 1)
                for t in range(TPG):
                    stats = dve.bn_stats(n_stat[:, t, :], src[t])
                stats.then_inc(s_n_ln, 1)
                wait_apart(dve, s_n_ln, st, lambda i: 3 * (i + shift) + 1)
                for t in range(TPG):
                    stats = dve.bn_aggr(n_mv[:, t, :], n_stat[:, t, :])
                stats.then_inc(s_n_ln, 1)
                wait(dve, s_n_ln, st, lambda i: 3 * (i + shift) + 2)
                dve.tensor_scalar(n_rs[:, :], n_mv[:, :, 1], EPS, None, ALU.add).then_inc(s_n_ln, 1)

            def norm_in_end(st, shift):
                src = rows_of(st, shift)
                wait(dve, s_n_rs, st, lambda i: i + shift + 1)
                for t in range(TPG):
                    done = dve.tensor_scalar(xn[:, t, :], src[t], n_mv[:, t, 0:1], n_rs[:, t:t + 1],
                                             ALU.subtract, ALU.mult)
                done.then_inc(s_xn, 1)

            norm_patches(Step(0), 0)
            norm_patches_end(Step(0), 0)
            dve.wait_ge(s_wp, 16)
            dve.wait_ge(s_small, 80)
            for k in range(KP):
                dve.tensor_scalar(wp_g[:, k, :], wp_raw[:, k, :], g1_sb[:, k:k + 1], None, ALU.mult).then_inc(s_wp_s, 1)
            dve.tensor_copy(b1_wide, b1_sb[:, :].unsqueeze(2).broadcast_to([128, KP, 128])).then_inc(s_b1w, 1)
            dve.wait_ge(s_wp_hi, 1)
            dve.tensor_tensor(wp_lo, wp_g[:, :, :], f32(wp_hi), ALU.subtract).then_inc(s_wp_lo, 1)
            dve.wait_ge(s_bw, 1)
            dve.tensor_tensor(zb_sb[:, :], zb_sb[:, :], vt_ps[:, 0:D], ALU.add).then_inc(s_zb, 1)
            dve.wait_ge(s_zb, 1)

            def stage_a(st):
                if st.i + 1 < PT:
                    norm_patches(st, 1)
                if st.i >= 2:
                    norm_z_end(st)
                if st.i < PT:
                    low_patches(st)
                if st.i + 1 < PT:
                    norm_patches_end(st, 1)
                if 1 <= st.i <= PT:
                    norm_z(st)
                if st.i == PT - 1:
                    norm_in(Step(0), 0)
                if st.i == PT:
                    norm_in_end(Step(0), 0)
                if st.i in PIECES:
                    w = piece(st)
                    wait(dve, s_wq_hi, st, lambda i: i - 1)
                    dve.tensor_tensor(wq_lo[:, 1, w], wq_raw[:, 1, w], f32(wq_hi[:, 1, w]), ALU.subtract)\
                        .then_inc(s_wq_lo2, 1)
                if st.i in (PT - 1, PT):
                    dve.wait_ge(s_wl_hi, st.i - PT + 2)
                    w = slice((st.i - PT + 1) * 4, (st.i - PT + 2) * 4)
                    dve.tensor_tensor(wl_lo[:, w, :], wl_raw[:, w, :], f32(wl_hi[:, w, :]), ALU.subtract)\
                        .then_inc(s_wl_lo, 1)

            sweep(dve, stage_a, PT + 2, 3, 4, 2)
            def low_xT(st, shift):
                for c in range(KD):
                    bank, nth = use("xt", st, shift, c)
                    wait(dve, s_xT_hi, st, lambda i: KD * (i + shift) + c + 1)
                    dve.tensor_tensor(xT_lo[:, c, :], shared[bank][:, 0:GT], f32(xT_hi[:, c, :]), ALU.subtract)\
                        .then_inc(s_xT_lo, 1)
                    dve.wait_ge(s_xT_lo, st.of(lambda i: KD * (i + shift) + c + 1))
                    dve.sem_inc(s_free[bank], 1)

            def take_max(st, u):
                sc = pair[u % 2][0:SEQ, :, 0:UP * SEQ].rearrange("s e (q k) -> s e q k", k=SEQ)
                tp = top[:, :].rearrange("s (e q) -> s e q", e=2)
                ex = expo[u % 2][:, :, :].rearrange("s (e q) k -> s e q k", e=2)
                wait(dve, s_score, st, lambda i: UNITS * i + u + 1)
                dve.tensor_reduce(tp, sc, AX, ALU.max).then_inc(s_top, 1)
                wait(dve, s_top, st, lambda i: UNITS * i + u + 1)
                wait(dve, s_ctx, st, lambda i: UNITS * i + u - 1)
                dve.tensor_tensor(ex, sc, tp.unsqueeze(3).broadcast_to([SEQ, 2, UP, SEQ]), ALU.subtract)\
                    .then_inc(s_sub, 1)

            def weigh_values(st, u):
                wait(dve, s_exp, st, lambda i: UNITS * i + u + 1)
                dve.tensor_reduce(zsum[:, :], expo[u % 2][:, :, :], AX, ALU.add).then_inc(s_zs, 1)
                wait(dve, s_zs, st, lambda i: UNITS * i + u + 1)
                dve.reciprocal(zinv[:, :], zsum[:, :]).then_inc(s_zi, 1)
                wait(dve, s_zi, st, lambda i: UNITS * i + u + 1)
                wait(dve, s_vt, st, lambda i: UNITS * i + u + 1)
                wait(dve, s_ctx, st, lambda i: UNITS * i + u - 1)
                zi = zinv[:, :].rearrange("s (e q) -> s q e", e=2).unsqueeze(3).broadcast_to([SEQ, UP, 2, HD])
                dve.tensor_tensor(vals[u % 2][:, :, :].rearrange("s (q e) d -> s q e d", e=2),
                                  vt_ps[0:SEQ, :].rearrange("s (q e d) -> s q e d", e=2, d=HD), zi, ALU.mult)\
                    .then_inc(s_val, 1)

            def low_ctx(st, u):
                at = (slice(None), slice(UP * (u % 2), UP * (u % 2 + 1)), slice(SEQ * (u // 2), SEQ * (u // 2 + 1)))
                wait(dve, s_c_hi, st, lambda i: UNITS * i + u + 1)
                dve.tensor_tensor(ctx_lo[at], ct_ps[:, 0:UP * SEQ].rearrange("p (k n) -> p k n", k=UP),
                                  f32(ctx_hi[at]), ALU.subtract).then_inc(s_c_lo, 1)

            def residual(st, shift):
                g = st.of(lambda i: i + shift)
                parts = ((0, 2), (2, TPG))
                for n, (a, b) in enumerate(parts):
                    bank, nth = use("ytr", st, shift, n)
                    wait(dve, s_full[bank], st, nth)
                    src = rows[:, g * TPG + a:g * TPG + b, 0:D] if st.k is None else rows[:, bass.ds(g * TPG + a, b - a), 0:D]
                    dve.tensor_tensor(h2[:, a:b, :], shared[bank][0:TR, 0:(b - a) * D].rearrange("p (t d) -> p t d", d=D),
                                      src, ALU.add).then_inc(s_free[bank], 1)

            def norm_mid(st, shift):
                for n in range(2):
                    bank, nth = use("ytr", st, shift, n)
                    wait(dve, s_free[bank], st, nth)
                dve.sem_inc(s_h2, 1)
                for t in range(TPG):
                    stats = dve.bn_stats(m_stat[:, t, :], h2[:, t, :])
                stats.then_inc(s_m_ln, 1)
                wait_apart(dve, s_m_ln, st, lambda i: 3 * (i + shift) + 1)
                for t in range(TPG):
                    stats = dve.bn_aggr(m_mv[:, t, :], m_stat[:, t, :])
                stats.then_inc(s_m_ln, 1)
                wait(dve, s_m_ln, st, lambda i: 3 * (i + shift) + 2)
                dve.tensor_scalar(m_rs[:, :], m_mv[:, :, 1], EPS, None, ALU.add).then_inc(s_m_ln, 1)

            def norm_mid_end(st, shift):
                wait(dve, s_m_rs, st, lambda i: i + shift + 1)
                for t in range(TPG):
                    done = dve.tensor_scalar(sent[:, t, 0:D], h2[:, t, :], m_mv[:, t, 0:1], m_rs[:, t:t + 1],
                                             ALU.subtract, ALU.mult)
                done.then_inc(s_x2, 1)

            def put_logits(st, shift):
                bank, nth = use("logit", st, shift, 0)
                wait(dve, s_h2_out, st, lambda i: 16 * (i + shift + 1))
                wait(dve, s_full[bank], st, nth)
                dve.tensor_copy(logits[:, :, :], shared[bank][0:TR, 0:TPG * NEXP].rearrange("p (t e) -> p t e", e=NEXP))\
                    .then_inc(s_free[bank], 1)

            def tiles_of(st, shift):
                g = st.of(lambda i: i + shift)
                return slice(g * TPG, (g + 1) * TPG) if st.k is None else bass.ds(g * TPG, TPG)

            def pick(st, shift, k):
                at, t = 6 * k, tiles_of(st, shift)
                src = (logits, rest)[k][:, :, :]

                def before(n):
                    wait(dve, s_pick, st, lambda i: PICKS * (i + shift) + n)

                def wide(ap):
                    return ap.unsqueeze(2).broadcast_to([TR, TPG, NEXP])

                if k == 0:
                    bank, nth = use("logit", st, shift, 0)
                    wait(dve, s_free[bank], st, nth)
                else:
                    before(at)
                dve.tensor_reduce(best[:, k, :], src, AX, ALU.max).then_inc(s_pick, 1)
                before(at + 1)
                dve.tensor_tensor(is_top[:, :, :], src, wide(best[:, k, :]), ALU.is_equal).then_inc(s_pick, 1)
                before(at + 2)
                dve.scalar_tensor_tensor(cand[:, :, :], is_top[:, :, :], -float(NEXP), expert[:, :, :], ALU.mult, ALU.add)\
                    .then_inc(s_pick, 1)
                before(at + 3)
                dve.tensor_reduce(first[:, k, :], cand[:, :, :], AX, ALU.min).then_inc(s_pick, 1)
                before(at + 4)
                dve.scalar_tensor_tensor(chosen[:, t, k, :], expert[:, :, :], -float(NEXP), wide(first[:, k, :]),
                                         ALU.add, ALU.is_equal).then_inc(s_pick, 1)
                before(at + 5)
                if k == 1 and st.k is not None:
                    dve.nop(nofuse=True)
                if k == 0:
                    dve.scalar_tensor_tensor(rest[:, :, :], chosen[:, t, 0, :], -3.0e38, logits[:, :, :], ALU.mult, ALU.add)\
                        .then_inc(s_pick, 1)
                else:
                    dve.tensor_copy(chosen_b[:, :, :], chosen[:, t, :, :].rearrange("p t k e -> p t (k e)"))\
                        .then_inc(s_chosen, 1)

            def place(st, shift):
                t = tiles_of(st, shift)
                bank, nth = use("rank", st, shift, 0)
                ranks = rank[:, t, :, :].rearrange("p t k e -> p t (k e)")

                def before(n):
                    wait(dve, s_place, st, lambda i: PLACED * (i + shift) + n)

                wait(dve, s_full[bank], st, nth)
                dve.tensor_tensor(ranks, shared[bank][0:TR, 0:TPG * CHOICES].rearrange("p (t c) -> p t c", c=CHOICES),
                                  carry[:, :].unsqueeze(1).broadcast_to([TR, TPG, CHOICES]), ALU.add).then_inc(s_rank, 1)
                wait(dve, s_rank, st, lambda i: i + shift + 1)
                dve.tensor_tensor(carry[:, :], carry[:, :], shared[bank][0:TR, TPG * CHOICES:(TPG + 1) * CHOICES], ALU.add)\
                    .then_inc(s_free[bank], 1)
                dve.tensor_tensor(over[:, :, :], rank[:, t, 0, :], limit[:, :, :], ALU.is_ge).then_inc(s_place, 1)
                before(1)
                dve.scalar_tensor_tensor(over[:, :, :], over[:, :, :], float(FAR), rank[:, t, 0, :], ALU.mult, ALU.add)\
                    .then_inc(s_place, 1)
                before(2)
                dve.tensor_tensor(over[:, :, :], over[:, :, :], chosen[:, t, 0, :], ALU.mult).then_inc(s_place, 1)
                before(3)
                dve.tensor_reduce(slot_f[:, :], over[:, :, :], AX, ALU.add).then_inc(s_place, 1)
                before(4)
                wait(dve, s_x2c, st, lambda i: 2 * (i + shift + 1))
                dve.tensor_copy(slot_ix[:, :], slot_f[:, :]).then_inc(s_place, 1)
                wait(dve, s_free[bank], st, nth)

            low_xT(Step(0), 0)
            take_max(Step(0), 0)

            def stage_b(st):
                more, before = st.i + 1 < GROUPS, st.i >= 1
                for u in range(UNITS):
                    if u == 0 and st.i == 0:
                        dve.wait_ge(s_masks, 9)
                    if u == 0 and more:
                        norm_in(st, 1)
                    weigh_values(st, u)
                    if u == 0 and more:
                        norm_in_end(st, 1)
                    if u == 2 and before:
                        residual(st, -1)
                    if u + 1 < UNITS:
                        take_max(st, u + 1)
                    elif more:
                        take_max(Step(st.i + 1, st.k, st.span), 0)
                    if u == 2 and before:
                        norm_mid(st, -1)
                    if u == 3 and before:
                        norm_mid_end(st, -1)
                    if u == 5 and before:
                        put_logits(st, -1)
                        pick(st, -1, 0)
                    if u == 6 and before:
                        pick(st, -1, 1)
                    if u == 7 and before:
                        place(st, -1)
                    low_ctx(st, u)
                    if u == 0 and more:
                        low_xT(st, 1)

            sweep(dve, stage_b, GROUPS, 1, 1, 2)
            last = Step(GROUPS)
            residual(last, -1)
            norm_mid(last, -1)
            norm_mid_end(last, -1)
            put_logits(last, -1)
            pick(last, -1, 0)
            pick(last, -1, 1)
            place(last, -1)

            links = [0]

            def link(ins):
                links[0] += 1
                ins.then_inc(s_route, 1)
                dve.wait_ge(s_route, links[0])

            link(dve.tensor_tensor(slot2[:, :, :], rank[:, :, 1, :],
                                   carry[:, 0:NEXP].unsqueeze(1).broadcast_to([TR, TILES, NEXP]), ALU.add))
            link(dve.tensor_tensor(over2[:, :, :], slot2[:, :, :],
                                   limit[:, 0, :].unsqueeze(1).broadcast_to([TR, TILES, NEXP]), ALU.is_ge))
            link(dve.scalar_tensor_tensor(slot2[:, :, :], over2[:, :, :], float(FAR), slot2[:, :, :], ALU.mult, ALU.add))
            link(dve.tensor_tensor(slot2[:, :, :], slot2[:, :, :], chosen[:, :, 1, :], ALU.mult))
            link(dve.tensor_reduce(slot2_f[:, :], slot2[:, :, :], AX, ALU.add))
            link(dve.tensor_copy(slot2_ix[:, :], slot2_f[:, :]))
            assert links[0] == ROUTED

            def low_fc(st, shift, q):
                wait(dve, s_fc_hi, st, lambda i: 4 * (i + shift) + q + 1)
                w = slice(q * FF // 4, (q + 1) * FF // 4)
                dve.tensor_tensor(fc_lo[:, :, w], raw_fc[:, :, w], f32(fc_hi[:, :, w]), ALU.subtract).then_inc(s_fc_lo, 1)

            def low_pj(st, q):
                wait(dve, s_pj_hi, st, lambda i: 4 * i + q + 1)
                w = slice(q * KF // 4, (q + 1) * KF // 4)
                dve.tensor_tensor(pj_lo[:, w, :], raw_pj[:, w, :], f32(pj_hi[:, w, :]), ALU.subtract).then_inc(s_pj_lo, 1)

            def low_xe(st, shift, c):
                for h in range(2):
                    n = 2 * c + h
                    w = slice(h * 3 * XR, (h + 1) * 3 * XR)
                    wait(dve, s_xe_hi, st, lambda i: 2 * KD * (i + shift) + n + 1)
                    dve.tensor_tensor(xe_lo[:, c, w], (vt_ps, ct_ps)[h][:, 0:3 * XR], f32(xe_hi[:, c, w]), ALU.subtract)\
                        .then_inc(s_xe_lo, 1)

            for q in range(4):
                low_fc(Step(0), 0, q)
            for c in range(KD):
                low_xe(Step(0), 0, c)

            def stage_d(st):
                p = st.i % 2
                col = D + 1 + st.of(lambda i: i)

                def put_y(t):
                    wait(dve, s_y, st, lambda i: XT * i + t + 1)
                    w = xg[p][:, t, col:col + 1] if st.k is None else xg[p][:, t, bass.ds(col, 1)]
                    dve.tensor_scalar(yrow[p][:, t, :], shared[t % 2][0:XR, 0:D], w, None, ALU.mult).then_inc(s_yrow, 1)

                for f in range(KF):
                    wait(dve, s_gelu, st, lambda i: KF * i + f + 1)
                    if f == 0:
                        wait(dve, s_y, st, lambda i: XT * i)
                    dve.tensor_copy(act_hi[:, f, :], act_f[f % 2][:, :]).then_inc(s_act_hi, 1)
                    wait(dve, s_act_hi, st, lambda i: KF * i + f + 1)
                    dve.tensor_tensor(act_lo[:, f, :], act_f[f % 2][:, :], f32(act_hi[:, f, :]), ALU.subtract)\
                        .then_inc(s_act_lo, 1)
                    if f < 4:
                        low_pj(st, f)
                more = st.i + 1 < NEXP
                for t in range(XT // 2):
                    if more:
                        low_fc(st, 1, t)
                    put_y(t)
                if more:
                    low_fc(st, 1, 3)
                    low_xe(st, 1, 0)
                put_y(3)
                if more:
                    low_xe(st, 1, 1)
                for t in range(4, XT):
                    put_y(t)
                wait(dve, s_added, st, lambda i: 16 * XT * i)
                if st.k is not None:
                    dve.nop(nofuse=True)

            sweep(dve, stage_d, NEXP, 1, 1, 2)

        @block.tensor
        def _(pe):
            def three(dst, terms, first=True, last=True):
                for n, (l_hi, l_lo, r_hi, r_lo) in enumerate(terms):
                    pe.matmul(dst, l_hi, r_hi, start=(first and n == 0), stop=False)
                    pe.matmul(dst, l_hi, r_lo, start=False, stop=False)
                    done = pe.matmul(dst, l_lo, r_hi, start=False, stop=(last and n == len(terms) - 1))
                return done

            def turn_patches(st, shift):
                p = (st.i + shift) % 2
                wait(pe, s_pn, st, lambda i: i + shift + 1)
                wait(pe, s_pT_lo, st, lambda i: 2 * (i + shift - 1))
                for k in range(KP):
                    done = pe.transpose(pair[p][:, k // 3, k % 3 * 128:(k % 3 + 1) * 128],
                                        patch[p][:, k * 128:(k + 1) * 128], ident[:, :])
                done.then_inc(s_pT, 1)

            def project(st):
                p = st.i % 2
                wait(pe, s_pT_lo, st, lambda i: 2 * (i + 1))
                wait(pe, s_z1, st, lambda i: i - 1)
                three(shared[p][:, 0:D], [(pT_hi[p][:, k, :], pT_lo[p][:, k, :], wp_hi[:, k, :], wp_lo[:, k, :])
                                          for k in range(KP)]).then_inc(s_z, 1)

            pe.wait_ge(s_ident, 16)
            turn_patches(Step(0), 0)
            pe.wait_ge(s_b1w, 1)
            for k in range(KP):
                done = pe.matmul(vt_ps[:, 0:D], b1_wide[:, k, :], wp_raw[:, k, :], start=(k == 0), stop=(k == KP - 1))
            done.then_inc(s_bw, 1)
            pe.wait_ge(s_wp_lo, 1)

            def stage_a(st):
                if st.i + 1 < PT:
                    turn_patches(st, 1)
                if st.i < PT:
                    project(st)

            sweep(pe, stage_a, PT + 2, 3, 4, 2)

            def free(st, kind, shift, c):
                bank, nth = use(kind, st, shift, c)
                wait(pe, s_free[bank], st, lambda i: nth(i) - 1)
                return bank

            def taken(st, kind, shift, blocks):
                for bank in range(2):
                    mine = [c for c in blocks if USE[(kind, st.i + shift, c)][0] == bank]
                    if mine:
                        wait(pe, s_free[bank], st, lambda i: USE[(kind, i + shift, mine[-1])][1])

            def ready(st, kind, nxt, shift):
                if use(kind, st, shift, KD - 1)[0] != use(nxt, st, shift, 0)[0]:
                    taken(st, kind, shift, [KD - 1])

            def turn_x(st, shift):
                wait(pe, s_xn, st, lambda i: i + shift + 1)
                for c in range(KD):
                    bank = free(st, "xt", shift, c)
                    for t in range(TPG):
                        done = pe.transpose(shared[bank][:, t * TR:(t + 1) * TR], xn[:, t, c * 128:(c + 1) * 128],
                                            ident[0:TR, 0:TR])
                    done.then_inc(s_full[bank], 1)

            def project_qkv(st, shift, c):
                if c == 0:
                    wait(pe, s_xT_lo, st, lambda i: KD * (i + shift + 1))
                bank = free(st, "qkv", shift, c)
                w = slice(c * 128, (c + 1) * 128)
                three(shared[bank][:, 0:GT], [(wq_hi[:, k, w], wq_lo[:, k, w], xT_hi[:, k, :], xT_lo[:, k, :])
                                              for k in range(KD)]).then_inc(s_full[bank], 1)

            def turn_values(st, u):
                b, h = u // 2, u % 2
                blocks = range(2 * PAIRS + UP * h, 2 * PAIRS + UP * (h + 1))
                taken(st, "qkv", 0, blocks)
                wait(pe, s_val, st, lambda i: UNITS * i + u)
                for q, c in enumerate(blocks):
                    done = pe.transpose(vt_ps[0:SEQ, q * 128:(q + 1) * 128],
                                        qkv[st.i % 2][:, c, b * SEQ:(b + 1) * SEQ], ident[:, :])
                done.then_inc(s_vt, 1)

            def score(st, u):
                b, h = u // 2, u % 2
                s = slice(b * SEQ, (b + 1) * SEQ)
                taken(st, "qkv", 0, range(2 * UP * h, 2 * UP * (h + 1)))
                wait(pe, s_sub, st, lambda i: UNITS * i + u - 1)
                for q in range(UP):
                    for e in range(2):
                        c, r = 2 * (UP * h + q), slice(HD * e, HD * (e + 1))
                        done = pe.matmul(pair[u % 2][0:SEQ, e, q * SEQ:(q + 1) * SEQ], qkv[st.i % 2][r, c + 1, s],
                                         qkv[st.i % 2][r, c, s], start=True, stop=True)
                done.then_inc(s_score, 1)

            def context(st, u):
                wait(pe, s_exp, st, lambda i: UNITS * i + u + 1)
                wait(pe, s_val, st, lambda i: UNITS * i + u + 1)
                wait(pe, s_c_lo, st, lambda i: UNITS * i + u)
                for q in range(UP):
                    for e in range(2):
                        done = pe.matmul(ct_ps[HD * e:HD * (e + 1), q * SEQ:(q + 1) * SEQ], vals[u % 2][:, 2 * q + e, :],
                                         expo[u % 2][:, UP * e + q, :], start=True, stop=True)
                done.then_inc(s_ctx, 1)

            def project_out(st, shift):
                wait(pe, s_c_lo, st, lambda i: UNITS * (i + shift + 1))
                for c in range(KD):
                    bank = free(st, "proj", shift, c)
                    w = slice(c * 128, (c + 1) * 128)
                    three(shared[bank][:, 0:GT], [(wl_hi[:, k, w], wl_lo[:, k, w], ctx_hi[:, k, :], ctx_lo[:, k, :])
                                                  for k in range(PAIRS)]).then_inc(s_full[bank], 1)

            def turn_y(st, shift):
                ready(st, "proj", "ytr", shift)
                for n, tiles in enumerate((range(2), range(2, TPG))):
                    bank = free(st, "ytr", shift, n)
                    for t in tiles:
                        for c in range(KD):
                            at = (t - tiles[0]) * D + c * 128
                            done = pe.transpose(shared[bank][0:TR, at:at + 128], yT[:, c, t * TR:(t + 1) * TR], ident[:, :])
                    done.then_inc(s_full[bank], 1)

            def turn_x2(st, shift):
                wait(pe, s_x2, st, lambda i: i + shift + 1)
                for c in range(KD):
                    bank = free(st, "x2t", shift, c)
                    for t in range(TPG):
                        done = pe.transpose(shared[bank][:, t * TR:(t + 1) * TR], sent[:, t, c * 128:(c + 1) * 128],
                                            ident[0:TR, 0:TR])
                    done.then_inc(s_full[bank], 1)

            def logit(st, shift):
                ready(st, "x2t", "logit", shift)
                bank = free(st, "logit", shift, 0)
                for t in range(TPG):
                    for c in range(KD):
                        done = pe.matmul(shared[bank][0:TR, t * NEXP:(t + 1) * NEXP], x2T[:, c, t * TR:(t + 1) * TR],
                                         wg_sb[:, c, :], start=(c == 0), stop=(c == KD - 1))
                done.then_inc(s_full[bank], 1)

            def count(st, shift):
                wait(pe, s_chosen, st, lambda i: i + shift + 1)
                bank = free(st, "rank", shift, 0)
                for t in range(TPG + 1):
                    for b in range(min(t + 1, TPG)):
                        done = pe.matmul(shared[bank][0:TR, t * CHOICES:(t + 1) * CHOICES], (tri if b == t else ones)[:, :],
                                         chosen_b[:, b, :], start=(b == 0), stop=(b == min(t, TPG - 1)))
                done.then_inc(s_full[bank], 1)

            pe.wait_ge(s_z1, PT)
            pe.wait_ge(s_zb, 1)
            turn_x(Step(0), 0)
            pe.wait_ge(s_wq_lo, len(PIECES))
            pe.wait_ge(s_wq_lo2, len(PIECES))
            for n, c in enumerate(START):
                project_qkv(Step(0), 0, c)
                if n == 9:
                    score(Step(0), 0)
            pe.wait_ge(s_const, 48)
            pe.wait_ge(s_wl_lo, 2)
            pe.wait_ge(s_masks, 5)

            def stage_b(st):
                more, before = st.i + 1 < GROUPS, st.i >= 1
                for u in range(UNITS):
                    turn_values(st, u)
                    if u + 1 < UNITS:
                        score(st, u + 1)
                    elif more:
                        score(Step(st.i + 1, st.k, st.span), 0)
                    if u == 0 and before:
                        project_out(st, -1)
                    if u == 0 and more:
                        turn_x(st, 1)
                    if u == 2 and before:
                        turn_y(st, -1)
                    if u == 4 and before:
                        turn_x2(st, -1)
                    if u == 5 and before:
                        logit(st, -1)
                    if u == 7 and before:
                        count(st, -1)
                    blocks = list(qkv_of(u)) if more else []
                    for c in blocks[:-1]:
                        project_qkv(st, 1, c)
                    context(st, u)
                    for c in blocks[-1:]:
                        project_qkv(st, 1, c)

            sweep(pe, stage_b, GROUPS, 1, 1, 2)
            last = Step(GROUPS)
            project_out(last, -1)
            turn_y(last, -1)
            turn_x2(last, -1)
            logit(last, -1)

            count(last, -1)

            def turn_slots(st, shift, c):
                p = (st.i + shift) % 2
                wait(pe, s_xg[p], st, lambda i: 16 * ((i + shift) // 2 + 1))
                for h in range(2):
                    n = 2 * c + h
                    wait(pe, s_xe_lo, st, lambda i: 2 * KD * (i + shift) + n - 1)
                    for t in range(3):
                        done = pe.transpose((vt_ps, ct_ps)[h][:, t * XR:(t + 1) * XR],
                                            xg[p][:, 3 * h + t, c * 128:(c + 1) * 128], ident[0:XR, 0:XR])
                    done.then_inc(s_xe, 1)

            for c in range(KD):
                turn_slots(Step(0), 0, c)

            def multiply(st, t, blocks):
                r = slice(t * XR, (t + 1) * XR)
                return three(shared[t % 2][0:XR, 0:D],
                             [(act_hi[:, f, r], act_lo[:, f, r], pj_hi[:, f, :], pj_lo[:, f, :]) for f in blocks],
                             first=blocks[0] == 0, last=blocks[-1] == KF - 1)

            def stage_d(st):
                wait(pe, s_xe_lo, st, lambda i: 2 * KD * (i + 1))
                wait(pe, s_fc_lo, st, lambda i: 4 * (i + 1))
                for f in range(KF):
                    wait(pe, s_gelu, st, lambda i: KF * i + f - 1)
                    w = slice(f * 128, (f + 1) * 128)
                    for h, (a, b) in enumerate(HALVES):
                        done = three(pair[f % 2][:, h, 0:b - a],
                                     [(fc_hi[:, k, w], fc_lo[:, k, w], xe_hi[:, k, a:b], xe_lo[:, k, a:b]) for k in range(KD)])
                    done.then_inc(s_mid, 1)
                wait(pe, s_pj_lo, st, lambda i: 4 * (i + 1))
                for t in range(2):
                    wait(pe, s_yrow, st, lambda i: XT * i + t - 1)
                for f in range(KF):
                    wait(pe, s_act_lo, st, lambda i: KF * i + f + 1)
                    for t in range(2):
                        done = multiply(st, t, range(f, f + 1))
                        if f == KF - 1:
                            done.then_inc(s_y, 1)
                for t in range(2, XT):
                    if t in (3, 4) and st.i + 1 < NEXP:
                        turn_slots(st, 1, t - 3)
                    wait(pe, s_yrow, st, lambda i: XT * i + t - 1)
                    multiply(st, t, range(KF)).then_inc(s_y, 1)

            sweep(pe, stage_d, NEXP, 1, 1, 2)


def kernel(x, txt, L0_tok_ln1_g, L0_tok_ln1_b, L0_tok_W_proj, L0_tok_b_proj, L0_tok_ln2_g, L0_tok_ln2_b,
           L0_tok_cls_token, L0_tok_pos_emb, L0_attn_q_w, L0_attn_q_b, L0_attn_k_w, L0_attn_k_b,
           L0_attn_v_w, L0_attn_v_b, L0_attn_l_w, L0_attn_l_b, L0_ffn_w_g, L0_ffn_c_fc, L0_ffn_c_proj):
    import numpy as np
    import concourse.bacc as bacc
    from concourse.bass_utils import run_bass_kernel_spmd

    def blocks(w):
        return np.asarray(w).reshape(PAIRS, 128, -1)

    side = 96 // 16
    p = np.asarray(x).reshape(BATCH, 3, side, 16, side, 16).transpose(0, 2, 4, 3, 5, 1)
    p = p.reshape(PT, 128, PD)
    q, k, v = blocks(L0_attn_q_w), blocks(L0_attn_k_w), blocks(L0_attn_v_w)
    w_qkv = np.concatenate([np.stack([q, k], 1).reshape(2 * PAIRS, 128, D), v]).transpose(2, 0, 1).reshape(D, NQKV * 128)
    q, k, v = blocks(L0_attn_q_b), blocks(L0_attn_k_b), blocks(L0_attn_v_b)
    b_qkv = np.concatenate([np.stack([q, k], 1).reshape(2 * PAIRS, 128), v.reshape(PAIRS, 128)]).T
    inputs = dict(
        patches=p, txt=txt, ln1_g=np.asarray(L0_tok_ln1_g).reshape(KP, 128).T,
        ln1_b=np.asarray(L0_tok_ln1_b).reshape(KP, 128).T, w_proj=L0_tok_W_proj,
        b_proj=np.asarray(L0_tok_b_proj).reshape(1, D), ln2_g=np.asarray(L0_tok_ln2_g).reshape(1, D),
        ln2_b=np.asarray(L0_tok_ln2_b).reshape(1, D), cls=np.asarray(L0_tok_cls_token).reshape(1, D),
        pos=np.asarray(L0_tok_pos_emb).reshape(NPATCH + 1, D), w_qkv=w_qkv, b_qkv=b_qkv,
        w_l=np.asarray(L0_attn_l_w).T, b_l=np.asarray(L0_attn_l_b).reshape(KD, 128).T, w_g=L0_ffn_w_g,
        c_fc=L0_ffn_c_fc, c_proj=L0_ffn_c_proj, ident_in=np.eye(128, dtype=np.float32))
    nc = bacc.Bacc("TRN2", target_bir_lowering=False, num_devices=1)
    arrays, args = {}, {}
    for name, a in inputs.items():
        arrays[name] = np.ascontiguousarray(a)
        args[name] = nc.dram_tensor(name, arrays[name].shape, mybir.dt.from_np(arrays[name].dtype), kind="ExternalInput").ap()
    out = nc.dram_tensor("out", (TOKENS, D), F32, kind="ExternalOutput").ap()
    program(nc, **args, out=out)
    r = run_bass_kernel_spmd(nc, [arrays], core_ids=[0])
    return r.results[0]["out"].reshape(BATCH, SEQ, D)
```

```python
from contextlib import ExitStack

import concourse.bass as bass
from concourse import mybir

F32 = mybir.dt.float32
F32R = mybir.dt.float32r
BF16 = mybir.dt.bfloat16
I32 = mybir.dt.int32
U32 = mybir.dt.uint32
ALU = mybir.AluOpType
ACT = mybir.ActivationFunctionType
AX = mybir.AxisListType.X

BATCH, SEQ, D = 32, 69, 256
NPATCH, NTXT, PD = 36, 32, 768
HEADS, HD = 16, 64
NEXP, FF, TOPK = 8, 1024, 2
TOKENS = BATCH * SEQ
CAP = TOPK * 5 * TOKENS // (4 * NEXP)
CAP += CAP % 2
EPS = 1e-5
SCALE = HD ** -0.5
KD = D // 128
KP = PD // 128
KF = FF // 128
PAIRS = HEADS // 2

PT = BATCH * NPATCH // 128

PIECES = range(2, 8)
PIECE = 3 * HEADS * HD // len(PIECES)

BPG = 4
GROUPS = BATCH // BPG
GT = BPG * SEQ
TPG = 3
TR = GT // TPG
TILES = GROUPS * TPG
NQKV = 3 * PAIRS
START = [*range(8), *range(16, 20), *range(8, 16), *range(20, NQKV)]
UNITS = 2 * BPG
UH = HEADS // 2
UP = UH // 2

ROW = D + 1 + NEXP
NSLOT = NEXP * CAP
XR = CAP // 6
XT = CAP // XR
HALVES = ((0, CAP // 2 + CAP // 2 % 2), (CAP // 2 + CAP // 2 % 2, CAP))
CHOICES = TOPK * NEXP
PICKS = 11
PLACED = 5
FOUND = 4
FAR = 1 << 20


def runs(first, count):
    found = []
    for b in range(BPG):
        n = 0
        while n < count:
            t, r = divmod(b * SEQ + first + n, TR)
            m = min(count - n, TR - r)
            found.append((b, n, r, t, m))
            n += m
    return found


POS_RUNS = runs(0, 1 + NPATCH)
PATCH_RUNS = runs(1, NPATCH)
TEXT_RUNS = runs(1 + NPATCH, NTXT)


class Step:

    def __init__(self, i, k=None, span=1):
        self.i, self.k, self.span = i, k, span

    def of(self, f):
        if self.k is None:
            return f(self.i)
        return self.k * (f(self.i + self.span) - f(self.i)) + f(self.i)


def sweep(eng, body, n, head, tail, span):
    for i in range(head):
        body(Step(i))
    with eng.Fori(0, (n - head - tail) // span) as k:
        for i in range(head, head + span):
            body(Step(i, k, span))
    for i in range(n - tail, n):
        body(Step(i))


def wait(eng, sem, step, f):
    assert step.k is None or f(step.i) >= 0
    if step.k is not None or f(step.i) > 0:
        eng.wait_ge(sem, step.of(f))


def wait_apart(eng, sem, step, f):
    wait(eng, sem, step, f)
    if step.k is not None:
        eng.nop(nofuse=True)


def bank_uses():
    order = [("xt", 0, c) for c in range(KD)] + [("qkv", 0, c) for c in START]
    for g in range(GROUPS + 1):
        for u in range(UNITS):
            order += group_uses(g, u)
    return {use: (n % 2, n // 2 + 1) for n, use in enumerate(order)}


def qkv_of(u):
    first = (0, 0, 5, 8, 12, 15, 19, 22, NQKV)
    return range(first[u], first[u + 1])


def group_uses(g, u):
    uses = []
    if g >= 1:
        uses += {0: [("proj", g - 1, c) for c in range(KD)],
                 2: [("ytr", g - 1, 0), ("ytr", g - 1, 1)],
                 4: [("x2t", g - 1, c) for c in range(KD)],
                 5: [("logit", g - 1, 0)],
                 7: [("rank", g - 1, 0)]}.get(u, [])
    if g + 1 < GROUPS:
        if u == 0:
            uses += [("xt", g + 1, c) for c in range(KD)]
        uses += [("qkv", g + 1, c) for c in qkv_of(u)]
    return uses


def program(nc, patches, txt, ln1_g, ln1_b, w_proj, b_proj, ln2_g, ln2_b, cls, pos,
            w_qkv, b_qkv, w_l, b_l, w_g, c_fc, c_proj, ident_in, out):
    USE = bank_uses()
    z_dram = nc.dram_tensor("patch_rows", (PT * 128, D), F32, kind="Internal").ap()
    slots_dram = nc.dram_tensor("slot_rows", (TOPK * NSLOT, ROW), F32, kind="Internal").ap()

    ctx = ExitStack()
    with ctx:
        def sb(name, shape, dt=F32, stack=ctx):
            return stack.enter_context(nc.sbuf_tensor(name, shape, dt))

        def sem(name):
            return ctx.enter_context(nc.semaphore(name))

        pair = [ctx.enter_context(nc.psum_tensor(f"pair{i}", [128, 2, 512], F32)) for i in range(2)]
        shared = [ctx.enter_context(nc.psum_tensor(f"shared{i}", [128, 512], F32)) for i in range(2)]
        vt_ps = ctx.enter_context(nc.psum_tensor("vt_ps", [128, 512], F32))
        ct_ps = ctx.enter_context(nc.psum_tensor("ct_ps", [128, 512], F32))

        ident = sb("ident", [128, 128])
        rows = sb("rows", [TR, TILES, D])
        ids = sb("ids", [TR, TILES, 1], I32)
        xg1 = sb("xg1", [XR, XT, ROW])
        pos_sb = sb("pos_sb", [TR, TPG, D])
        tri = sb("tri", [TR, TR], BF16)
        ones = sb("ones", [TR, XR], BF16)
        half = sb("half", [128, TPG])
        minus1 = sb("minus1", [128, TPG])
        expert = sb("expert", [TR, TPG, NEXP])
        limit = sb("limit", [XR, TPG, TOPK, NEXP])
        place_of = sb("place_of", [XR, NEXP, XT])
        sent = sb("sent", [TR, TPG, ROW])
        logits = sb("logits", [TR, TPG, NEXP])
        is_top = sb("is_top", [TR, TPG, NEXP])
        cand = sb("cand", [TR, TPG, NEXP])
        rest = sb("rest", [TR, TPG, NEXP])
        best = sb("best", [TR, TOPK, TPG])
        first = sb("first", [TR, TOPK, TPG])
        gap = sb("gap", [TR, TPG])
        e_gap = sb("e_gap", [TR, TPG])
        denom = sb("denom", [TR, TPG])
        prob = sb("prob", [TR, TOPK, TPG])
        part = sb("part", [TR, TOPK, TPG, NEXP])
        chosen = sb("chosen", [TR, TPG, TOPK, NEXP])
        chosen_b = sb("chosen_b", [TR, TPG, CHOICES], BF16)
        rank = sb("rank", [TR, TPG, CHOICES])
        carry = sb("carry", [XR, CHOICES])
        over = sb("over", [TR, TPG, CHOICES])
        slot_f = sb("slot_f", [TR, TPG, TOPK])
        slot_ix = sb("slot_ix", [TR, TPG, TOPK], I32)
        shift_by = sb("shift_by", [XR, NEXP])
        second = sb("second", [XR, NEXP, XT])
        found = sb("found", [XR, NEXP, XT])
        found_ix = [sb(f"found_ix{i}", [XR, XT], I32) for i in range(2)]

        bmem = ctx.enter_context(ExitStack())
        wq_hi = sb("wq_hi", [128, KD, NQKV * 128], F32R, bmem)
        wq_lo = sb("wq_lo", [128, KD, NQKV * 128], F32R, bmem)
        wl_hi = sb("wl_hi", [128, PAIRS, D], F32R, bmem)
        wl_lo = sb("wl_lo", [128, PAIRS, D], F32R, bmem)
        qkv = [sb(f"qkv{i}", [128, NQKV, GT], F32, bmem) for i in range(2)]
        ctx_hi = sb("ctx_hi", [128, PAIRS, GT], F32R, bmem)
        ctx_lo = sb("ctx_lo", [128, PAIRS, GT], F32R, bmem)
        bq_sb = sb("bq_sb", [128, NQKV], F32, bmem)
        bl_sb = sb("bl_sb", [128, KD], F32, bmem)
        wg_sb = sb("wg_sb", [128, KD, NEXP], F32, bmem)

        z_stat = sb("z_stat", [128, 6], F32, bmem)
        z_mv = sb("z_mv", [128, 2], F32, bmem)
        z_rs = sb("z_rs", [128, 1], F32, bmem)
        z_row = [sb(f"z_row{i}", [128, D], F32, bmem) for i in range(2)]
        g2_sb = sb("g2_sb", [128, D], F32, bmem)
        b2_sb = sb("b2_sb", [128, D], F32, bmem)
        zb_sb = sb("zb_sb", [128, D], F32, bmem)
        with ExitStack() as amem:
            pT_hi = [sb(f"pT_hi{i}", [128, KP, 128], F32R, amem) for i in range(2)]
            pT_lo = [sb(f"pT_lo{i}", [128, KP, 128], F32R, amem) for i in range(2)]
            a_stat = sb("a_stat", [128, 2, 6], F32, amem)
            a_mv = sb("a_mv", [128, 2], F32, amem)
            a_rs = sb("a_rs", [128, 1], F32, amem)
            a_nb = sb("a_nb", [128, 1], F32, amem)
            g1_sb = sb("g1_sb", [128, KP], F32, amem)
            b1_sb = sb("b1_sb", [128, KP], F32, amem)
        flat0 = qkv[0][:, :, :].rearrange("p c n -> p (c n)")
        flat1 = qkv[1][:, :, :].rearrange("p c n -> p (c n)")
        wq_raw = flat1[:, 0:KD * NQKV * 128].rearrange("p (k n) -> p k n", k=KD)
        wl_raw = flat0[:, 0:PAIRS * D].rearrange("p (k n) -> p k n", k=PAIRS)
        at = PAIRS * D
        wp_raw = flat0[:, at:at + KP * D].rearrange("p (k n) -> p k n", k=KP)
        at += KP * D
        patch = [flat0[:, at + i * PD:at + (i + 1) * PD] for i in range(2)]
        at += 2 * PD
        b1_wide = flat0[:, at:at + KP * 128].rearrange("p (k n) -> p k n", k=KP)
        wp_hi = ctx_hi[:, :, :].rearrange("p c n -> p (c n)")[:, 0:KP * D].rearrange("p (k n) -> p k n", k=KP)
        wp_lo = ctx_lo[:, :, :].rearrange("p c n -> p (c n)")[:, 0:KP * D].rearrange("p (k n) -> p k n", k=KP)

        with ExitStack() as smem:
            xT_hi = sb("xT_hi", [128, KD, GT], F32R, smem)
            xT_lo = sb("xT_lo", [128, KD, GT], F32R, smem)
            expo = [sb(f"expo{i}", [SEQ, UH, SEQ], F32, smem) for i in range(2)]
            vals = [sb(f"vals{i}", [SEQ, UH, HD], F32, smem) for i in range(2)]
            top = sb("top", [SEQ, UH], F32, smem)
            zsum = sb("zsum", [SEQ, UH], F32, smem)
            zinv = sb("zinv", [SEQ, UH], F32, smem)
            yT = sb("yT", [128, KD, GT], F32, smem)
            x2T = sb("x2T", [128, KD, GT], F32, smem)
            xn = sb("xn", [TR, TPG, D], F32, smem)
            h2 = sb("h2", [TR, TPG, D], F32, smem)
            n_stat = sb("n_stat", [TR, TPG, 6], F32, smem)
            n_mv = sb("n_mv", [TR, TPG, 2], F32, smem)
            n_rs = sb("n_rs", [TR, TPG], F32, smem)
            m_stat = sb("m_stat", [TR, TPG, 6], F32, smem)
            m_mv = sb("m_mv", [TR, TPG, 2], F32, smem)
            m_rs = sb("m_rs", [TR, TPG], F32, smem)
        bmem.close()

        with ExitStack() as cmem:
            raw_fc = sb("raw_fc", [128, KD, FF], F32, cmem)
            raw_pj = sb("raw_pj", [128, KF, D], F32, cmem)
            fc_hi = sb("fc_hi", [128, KD, FF], F32R, cmem)
            fc_lo = sb("fc_lo", [128, KD, FF], F32R, cmem)
            pj_hi = sb("pj_hi", [128, KF, D], F32R, cmem)
            pj_lo = sb("pj_lo", [128, KF, D], F32R, cmem)
            xe_hi = sb("xe_hi", [128, KD, CAP], F32R, cmem)
            xe_lo = sb("xe_lo", [128, KD, CAP], F32R, cmem)
            act_f = [sb(f"act_f{i}", [128, CAP], F32, cmem) for i in range(2)]
            act_hi = sb("act_hi", [128, KF, CAP], F32R, cmem)
            act_lo = sb("act_lo", [128, KF, CAP], F32R, cmem)
            xg = [sb("xg0", [XR, XT, ROW], F32, cmem), xg1]
            yrow = [sb(f"yrow{i}", [XR, XT, D], F32, cmem) for i in range(2)]

        s_const, s_wp, s_gain, s_small, s_wll, s_pos, s_ident, s_class, s_text = (
            sem(n) for n in ("s_const", "s_wp", "s_gain", "s_small", "s_wll", "s_pos", "s_ident", "s_class", "s_text"))
        s_wql = [sem(f"s_wql{i}") for i in range(2)]
        s_patch = [sem(f"s_patch{i}") for i in range(2)]
        s_zdma = [sem(f"s_zdma{i}") for i in range(2)]
        s_rows = [sem(f"s_rows{i}") for i in range(2)]
        s_zeros, s_half, s_masks, s_a_rs, s_a_nb, s_z_rs, s_n_rs, s_m_rs = (
            sem(n) for n in ("s_zeros", "s_half", "s_masks", "s_a_rs", "s_a_nb", "s_z_rs", "s_n_rs", "s_m_rs"))
        s_a_ln, s_pn, s_pT, s_pT_hi, s_pT_lo, s_z, s_z1, s_z_ln, s_zn, s_zmul, s_zrow = (
            sem(n) for n in ("s_a_ln", "s_pn", "s_pT", "s_pT_hi", "s_pT_lo", "s_z", "s_z1", "s_z_ln", "s_zn", "s_zmul", "s_zrow"))
        s_wp_hi, s_wp_lo, s_wq_hi, s_wq_lo, s_wq_lo2, s_wl_hi, s_wl_lo, s_b1w, s_bw, s_zb = (
            sem(n) for n in ("s_wp_hi", "s_wp_lo", "s_wq_hi", "s_wq_lo", "s_wq_lo2", "s_wl_hi", "s_wl_lo", "s_b1w", "s_bw", "s_zb"))
        s_full = [sem(f"s_full{i}") for i in range(2)]
        s_free = [sem(f"s_free{i}") for i in range(2)]
        s_h, s_n_ln, s_xn, s_xT_hi, s_xT_lo = (sem(n) for n in ("s_h", "s_n_ln", "s_xn", "s_xT_hi", "s_xT_lo"))
        s_vt, s_score, s_top, s_sub, s_exp, s_zs, s_zi, s_val, s_ctx, s_c_hi, s_c_lo = (
            sem(n) for n in ("s_vt", "s_score", "s_top", "s_sub", "s_exp", "s_zs", "s_zi", "s_val", "s_ctx", "s_c_hi", "s_c_lo"))
        s_h2, s_h2_out, s_m_ln, s_x2 = (sem(n) for n in ("s_h2", "s_h2_out", "s_m_ln", "s_x2"))
        s_pick, s_place, s_found, s_found_ix, s_chosen, s_rank, s_gap, s_egap, s_prob, s_ids, s_fill, s_sent = (
            sem(n) for n in ("s_pick", "s_place", "s_found", "s_found_ix", "s_chosen", "s_rank", "s_gap", "s_egap",
                             "s_prob", "s_ids", "s_fill", "s_sent"))
        s_fcl, s_pjl, s_fc_hi, s_fc_lo, s_pj_hi, s_pj_lo = (
            sem(n) for n in ("s_fcl", "s_pjl", "s_fc_hi", "s_fc_lo", "s_pj_hi", "s_pj_lo"))
        s_xg = [sem(f"s_xg{i}") for i in range(2)]
        s_xe, s_xe_hi, s_xe_lo, s_mid, s_gelu, s_act_hi, s_act_lo, s_y, s_yrow, s_added = (
            sem(n) for n in ("s_xe", "s_xe_hi", "s_xe_lo", "s_mid", "s_gelu", "s_act_hi", "s_act_lo", "s_y", "s_yrow", "s_added"))

        y_banks = [shared[0], shared[1], pair[0][:, 0, :], pair[0][:, 1, :], shared[0], shared[1]]

        def use(kind, step, shift, c):
            bank = USE[(kind, step.i + shift, c)][0]
            return bank, lambda i: USE[(kind, i + shift, c)][1]

        def f32(ap):
            return ap.bitcast(F32)

        def piece(st, shift=0):
            c = st.of(lambda i: (i + shift - 2) * PIECE)
            return slice(c, c + PIECE) if st.k is None else bass.ds(c, PIECE)

        every = rows[:, :, :].rearrange("p (g t) d -> p t g d", t=TPG)

        block = ctx.enter_context(nc.Block())

        @block.sync
        def _(sp):
            sp.dma_start(patch[0], patches[0]).then_inc(s_patch[0], 16)
            sp.dma_start(g1_sb[:, :], ln1_g).then_inc(s_gain, 16)
            sp.dma_start(b1_sb[:, :], ln1_b).then_inc(s_gain, 16)
            sp.dma_start(wp_raw, w_proj.rearrange("(k p) n -> p k n", p=128)).then_inc(s_wp, 16)
            sp.dma_start(ident[:, :], ident_in).then_inc(s_ident, 16)
            sp.dma_start(patch[1], patches[1]).then_inc(s_patch[1], 16)
            sp.dma_start(g2_sb[:, :], ln2_g.broadcast_to([128, D])).then_inc(s_small, 16)
            sp.dma_start(b2_sb[:, :], ln2_b.broadcast_to([128, D])).then_inc(s_small, 16)
            sp.dma_start(zb_sb[:, :], b_proj.broadcast_to([128, D])).then_inc(s_small, 16)
            sp.dma_start(bq_sb[:, :], b_qkv).then_inc(s_const, 16)
            sp.dma_start(bl_sb[:, :], b_l).then_inc(s_const, 16)
            sp.dma_start(wg_sb[:, :, :], w_g.rearrange("(k p) n -> p k n", p=128)).then_inc(s_const, 16)
            txt_seq = txt.rearrange("(g b) s d -> b s g d", b=BPG)

            def load_rows(st, shift):
                g = st.of(lambda i: i + shift)
                for n in range(2):
                    wait_apart(sp, s_zdma[(st.i + shift + n) % 2], st, lambda i: 16 * ((i + shift + n) // 2 + 1))
                if st.i + shift >= 2:
                    wait_apart(sp, s_rows[(st.i + shift) % 2], st, lambda i: 16 * len(PATCH_RUNS) * ((i + shift) // 2))
                for b, n, r, t, m in PATCH_RUNS:
                    sp.dma_start(rows[r:r + m, bass.ds(g * TPG + t, 1), 0:D],
                                 z_dram[bass.ds((g * BPG + b) * NPATCH + n, m), :].rearrange("(m o) d -> m o d", o=1))\
                      .then_inc(s_rows[(st.i + shift) % 2], 16)

            def stage_a(st):
                if st.i + 1 in PIECES:
                    wait_apart(sp, s_wq_hi, st, lambda i: i - 2)
                    w = piece(st, 1)
                    sp.dma_start(wq_raw[:, :, w], w_qkv.rearrange("(k p) n -> p k n", p=128)[:, :, w])\
                      .then_inc(s_wql[(st.i + 1) % 2], 16)
                if st.i + 2 < PT:
                    wait_apart(sp, s_pT, st, lambda i: i + 1)
                    j = st.of(lambda i: i + 2)
                    sp.dma_start(patch[st.i % 2], patches[bass.ds(j, 1), :, :].rearrange("o p n -> (o p) n"))\
                      .then_inc(s_patch[st.i % 2], 16)
                if st.i == 0:
                    sp.dma_start(wl_raw, w_l.rearrange("(k p) n -> p k n", p=128)).then_inc(s_wll, 16)
                if st.i == 1:
                    for b in range(BPG):
                        t, r = divmod(b * SEQ, TR)
                        sp.dma_start(every[r:r + 1, t, :, :], cls.unsqueeze(1).broadcast_to([1, GROUPS, D]))\
                          .then_inc(s_class, 16)
                if st.i == 2:
                    for b, n, r, t, m in TEXT_RUNS:
                        sp.dma_start(every[r:r + m, t, :, :], txt_seq[b, n:n + m, :, :]).then_inc(s_text, 16)
                if PT - 2 <= st.i <= PT:
                    load_rows(Step(st.i), 2 - PT)
                if st.i >= 2:
                    j = st.of(lambda i: i - 2)
                    wait_apart(sp, s_zrow, st, lambda i: i - 1)
                    sp.dma_start(z_dram[bass.ds(j * 128, 128), :], z_row[st.i % 2][:, :]).then_inc(s_zdma[st.i % 2], 16)

            sweep(sp, stage_a, PT + 2, 3, 4, 2)

            out_tile = out.rearrange("(t p) d -> p t d", p=TR)

            def stage_b(st):
                if st.i + 3 < GROUPS:
                    load_rows(st, 3)
                if st.i == 0:
                    sp.wait_ge(s_zeros, 3)
                    slots = slots_dram.rearrange("(k e t p) n -> e p k t n", k=TOPK, e=NEXP, p=XR)
                    for e in range(NEXP):
                        for k in range(TOPK):
                            sp.dma_start(slots[e, :, k, :, :], xg[1][:, :, :]).then_inc(s_fill, 16)
                g = st.of(lambda i: i)
                wait_apart(sp, s_h2, st, lambda i: i + 1)
                sp.dma_start(out_tile[:, bass.ds(g * TPG, TPG), :], h2[:, :, :]).then_inc(s_h2_out, 16)

            sweep(sp, stage_b, GROUPS, 1, 3, 2)

            def load_fc(e):
                sp.dma_start(raw_fc[:, :, :], c_fc[e].rearrange("o (k p) n -> p (o k) n", p=128)).then_inc(s_fcl, 16)

            def load_pj(e):
                sp.dma_start(raw_pj[:, :, :], c_proj[e].rearrange("o (k p) n -> p (o k) n", p=128)).then_inc(s_pjl, 16)

            bank, n = USE[("logit", GROUPS - 1, 0)]
            sp.wait_ge(s_full[bank], n)
            load_fc(slice(0, 1))
            load_pj(slice(0, 1))

            def stage_d(st):
                if st.i + 1 < NEXP:
                    nxt = st.of(lambda i: i + 1)
                    wait_apart(sp, s_fc_lo, st, lambda i: 4 * (i + 1))
                    load_fc(bass.ds(nxt, 1))
                    wait_apart(sp, s_pj_lo, st, lambda i: 4 * (i + 1))
                    load_pj(bass.ds(nxt, 1))

            sweep(sp, stage_d, NEXP, 1, 1, 2)
            sp.wait_ge(s_h2_out, 16 * GROUPS)
            sp.wait_ge(s_added, 16 * XT * NEXP)

        @block.gpsimd
        def _(pool):
            pool.memset(half[:, :], -0.5).then_inc(s_half, 1)
            pool.memset(pos_sb[:, :, :], 0.0).then_inc(s_zeros, 1)
            pool.memset(xg[1][:, :, :], 0.0).then_inc(s_zeros, 1)
            pool.wait_ge(s_zeros, 2)
            pool.memset(xg[1][:, :, D:D + 1].bitcast(I32), FAR).then_inc(s_zeros, 1)
            pool.memset(ones[:, :], 1.0).then_inc(s_masks, 1)
            pool.memset(tri[:, :], 1.0).then_inc(s_masks, 1)
            pool.memset(minus1[:, :], -1.0).then_inc(s_masks, 1)
            pool.wait_ge(s_masks, 3)
            pool.affine_select(out=tri[:, :], in_=tri[:, :], compare_op=ALU.is_gt, fill=0.0, base=0,
                               pattern=[[1, TR]], channel_multiplier=-1).then_inc(s_masks, 1)
            pool.iota(carry[:, :], pattern=[[NSLOT, TOPK], [CAP, NEXP]], base=0, channel_multiplier=0,
                      allow_small_or_imprecise_dtypes=True).then_inc(s_masks, 1)
            pool.iota(expert[:, :, :], pattern=[[0, TPG], [1, NEXP]], base=0, channel_multiplier=0,
                      allow_small_or_imprecise_dtypes=True).then_inc(s_masks, 1)
            pool.iota(limit[:, :, :, :], pattern=[[0, TPG], [NSLOT, TOPK], [CAP, NEXP]], base=CAP, channel_multiplier=0,
                      allow_small_or_imprecise_dtypes=True).then_inc(s_masks, 1)
            pool.iota(place_of[:, :, :], pattern=[[CAP, NEXP], [XR, XT]], base=0, channel_multiplier=1,
                      allow_small_or_imprecise_dtypes=True).then_inc(s_masks, 1)
            pool.iota(ids[:, :, :], pattern=[[TR, TILES], [0, 1]], base=0, channel_multiplier=1).then_inc(s_masks, 1)

            def root(rs, st, ready, f, done):
                wait(pool, ready, st, f)
                pool.tensor_tensor(rs, rs, half[0:rs.shape[0], 0:rs.shape[1]], ALU.pow).then_inc(done, 1)

            def add_positions(st, shift):
                g = st.of(lambda i: i + shift)
                wait(pool, s_rows[(st.i + shift) % 2], st, lambda i: 16 * len(PATCH_RUNS) * ((i + shift) // 2 + 1))
                r = rows[:, g * TPG:(g + 1) * TPG, 0:D] if st.k is None else rows[:, bass.ds(g * TPG, TPG), 0:D]
                pool.tensor_tensor(r, r, pos_sb[:, :, :], ALU.add).then_inc(s_h, 1)

            def root_patches(st, shift):
                root(a_rs[:, :], st, s_a_ln, lambda i: 3 * (i + shift + 1), s_a_rs)
                pool.tensor_tensor(a_nb[:, :], a_mv[:, 0:1], minus1[:, 0:1], ALU.mult).then_inc(s_a_nb, 1)
                wait(pool, s_a_nb, st, lambda i: 2 * (i + shift) + 1)
                wait(pool, s_a_rs, st, lambda i: i + shift + 1)
                pool.tensor_tensor(a_nb[:, :], a_nb[:, :], a_rs[:, :], ALU.mult).then_inc(s_a_nb, 1)

            def root_in(st, shift):
                root(n_rs[:, :], st, s_n_ln, lambda i: 3 * (i + shift + 1), s_n_rs)

            def stage_a(st):
                if st.i == PT - 1:
                    pool.wait_ge(s_pos, 16 * len(POS_RUNS))
                    pool.wait_ge(s_class, 16 * BPG)
                    pool.wait_ge(s_text, 16 * len(TEXT_RUNS))
                    add_positions(Step(0), 0)
                if st.i == PT:
                    root_in(Step(0), 0)
                if st.i + 1 < PT:
                    root_patches(st, 1)
                if st.i >= 2:
                    p = st.i % 2
                    wait(pool, s_zn, st, lambda i: i - 1)
                    pool.tensor_tensor(z_row[p][:, :], z_row[p][:, :], g2_sb[:, :], ALU.mult).then_inc(s_zmul, 1)
                    wait(pool, s_zmul, st, lambda i: i - 1)
                    pool.tensor_tensor(z_row[p][:, :], z_row[p][:, :], b2_sb[:, :], ALU.add).then_inc(s_zrow, 1)
                if 1 <= st.i <= PT:
                    root(z_rs[:, :], st, s_z_ln, lambda i: 3 * i, s_z_rs)
                if st.i in PIECES:
                    w = piece(st)
                    wait(pool, s_wq_hi, st, lambda i: i - 1)
                    pool.tensor_tensor(wq_lo[:, 0, w], wq_raw[:, 0, w], f32(wq_hi[:, 0, w]), ALU.subtract)\
                        .then_inc(s_wq_lo, 1)

            pool.wait_ge(s_half, 1)
            pool.wait_ge(s_masks, 3)
            root_patches(Step(0), 0)
            for _, n, r, t, m in POS_RUNS:
                pool.dma_start(pos_sb[r:r + m, t, :], pos[n:n + m, :]).then_inc(s_pos, 16)
            pool.wait_ge(s_small, 48)
            sweep(pool, stage_a, PT + 2, 3, 4, 2)

            def root_mid(st, shift):
                if st.i + shift >= 1:
                    wait_apart(pool, s_sent, st, lambda i: 16 * TOPK * TPG * (i + shift))
                root(m_rs[:, :], st, s_m_ln, lambda i: 3 * (i + shift + 1), s_m_rs)
                g = st.of(lambda i: i + shift)
                t = slice(g * TPG, (g + 1) * TPG) if st.k is None else bass.ds(g * TPG, TPG)
                pool.tensor_copy(sent[:, :, D:D + 1].bitcast(I32), ids[:, t, :]).then_inc(s_ids, 1)

            def weigh(st, shift):
                def before(n):
                    wait(pool, s_prob, st, lambda i: 6 * (i + shift) + n)

                wait(pool, s_pick, st, lambda i: PICKS * (i + shift + 1))
                pool.tensor_tensor(gap[:, :], best[:, 1, :], best[:, 0, :], ALU.subtract).then_inc(s_gap, 1)
                wait(pool, s_egap, st, lambda i: i + shift + 1)
                pool.tensor_tensor(denom[:, :], e_gap[:, :], minus1[0:TR, :], ALU.subtract).then_inc(s_prob, 1)
                before(1)
                pool.tensor_tensor(prob[:, 0, :], denom[:, :], minus1[0:TR, :], ALU.pow).then_inc(s_prob, 1)
                before(2)
                pool.tensor_tensor(prob[:, 1, :], prob[:, 0, :], e_gap[:, :], ALU.mult).then_inc(s_prob, 1)
                before(3)
                for k in range(TOPK):
                    pool.tensor_tensor(part[:, k, :, :], chosen[:, :, k, :],
                                       prob[:, k, :].unsqueeze(2).broadcast_to([TR, TPG, NEXP]), ALU.mult).then_inc(s_prob, 1)
                before(5)
                pool.tensor_tensor(sent[:, :, D + 1:], part[:, 0, :, :], part[:, 1, :, :], ALU.add).then_inc(s_prob, 1)

            def send(st, shift):
                wait(pool, s_prob, st, lambda i: 6 * (i + shift + 1))
                wait(pool, s_place, st, lambda i: PLACED * (i + shift + 1))
                wait(pool, s_ids, st, lambda i: i + shift + 1)
                wait(pool, s_x2, st, lambda i: i + shift + 1)
                if st.k is not None:
                    pool.nop(nofuse=True)
                for k in range(TOPK):
                    for t in range(TPG):
                        pool.indirect_dma_start(slots_dram,
                                                bass.IndirectOffsetOnAxis(ap=slot_ix[:, t, k:k + 1].bitcast(U32), axis=0),
                                                sent[:, t, :], None, bounds_check=TOPK * NSLOT - 1, oob_is_err=False)\
                            .then_inc(s_sent, 16)

            def stage_b(st):
                if st.i + 1 < GROUPS:
                    root_in(st, 1)
                if st.i >= 2:
                    send(st, -2)
                if st.i + 2 < GROUPS:
                    add_positions(st, 2)
                if st.i >= 1:
                    root_mid(st, -1)
                    weigh(st, -1)
                if st.i == 0:
                    pool.wait_ge(s_masks, 9)
                if st.i == 1:
                    pool.wait_ge(s_fill, 16 * TOPK * NEXP)

            add_positions(Step(0), 1)
            sweep(pool, stage_b, GROUPS, 2, 2, 2)
            send(Step(GROUPS), -2)
            root_mid(Step(GROUPS), -1)
            weigh(Step(GROUPS), -1)
            send(Step(GROUPS), -1)

            def fetch(st, shift):
                p = (st.i + shift) % 2
                wait_apart(pool, s_found_ix, st, lambda i: i + shift + 1)
                for t in range(XT):
                    pool.indirect_dma_start(xg[p][:, t, :], None, slots_dram,
                                            bass.IndirectOffsetOnAxis(ap=found_ix[p][:, t:t + 1].bitcast(U32), axis=0),
                                            bounds_check=TOPK * NSLOT - 1, oob_is_err=False).then_inc(s_xg[p], 16)

            pool.wait_ge(s_sent, 16 * TOPK * TILES)
            fetch(Step(0), 0)

            def stage_d(st):
                p = st.i % 2
                wait(pool, s_added, st, lambda i: 16 * XT * i)
                if st.i == 0:
                    pool.wait_ge(s_h2_out, 16 * GROUPS)
                if st.i + 1 < NEXP:
                    fetch(st, 1)
                for t in range(XT):
                    wait_apart(pool, s_yrow, st, lambda i: XT * i + t + 1)
                    pool.indirect_dma_start(out, bass.IndirectOffsetOnAxis(ap=xg[p][:, t, D:D + 1].bitcast(U32), axis=0),
                                            yrow[p][:, t, :], None, bounds_check=TOKENS - 1, oob_is_err=False,
                                            compute_op=ALU.add).then_inc(s_added, 16)

            sweep(pool, stage_d, NEXP, 1, 1, 2)

        @block.scalar
        def _(act):
            def norm_patches_end(st, shift):
                p = (st.i + shift) % 2
                wait(act, s_a_nb, st, lambda i: 2 * (i + shift + 1))
                act.activation(patch[p], patch[p], ACT.Identity, scale=a_rs[:, 0:1], bias=a_nb[:, 0:1]).then_inc(s_pn, 1)

            norm_patches_end(Step(0), 0)
            act.wait_ge(s_gain, 32)
            act.wait_ge(s_wp, 16)
            for k in range(KP):
                act.activation(wp_hi[:, k, :], wp_raw[:, k, :], ACT.Copy, scale=g1_sb[:, k:k + 1]).then_inc(s_wp_hi, 1)

            def stage_a(st):
                if st.i < PT:
                    p = st.i % 2
                    wait(act, s_pT, st, lambda i: i + 1)
                    wait(act, s_z, st, lambda i: i - 1)
                    for h in range(2):
                        act.activation(pT_hi[p][:, 3 * h:3 * h + 3, :],
                                       pair[p][:, h, 0:384].rearrange("p (k n) -> p k n", k=3), ACT.Copy)\
                            .then_inc(s_pT_hi, 1)
                if st.i in PIECES:
                    w = piece(st)
                    wait(act, s_wql[st.i % 2], st, lambda i: 16 * (i // 2))
                    act.activation(wq_hi[:, :, w], wq_raw[:, :, w], ACT.Copy).then_inc(s_wq_hi, 1)
                if st.i + 1 < PT:
                    norm_patches_end(st, 1)
                if st.i in (PT - 1, PT):
                    act.wait_ge(s_wll, 16)
                    w = slice((st.i - PT + 1) * 4, (st.i - PT + 2) * 4)
                    act.activation(wl_hi[:, w, :], wl_raw[:, w, :], ACT.Copy).then_inc(s_wl_hi, 1)

            sweep(act, stage_a, PT + 2, 3, 4, 2)

            def put_qkv(st, shift, c):
                bank, nth = use("qkv", st, shift, c)
                wait(act, s_full[bank], st, nth)
                act.activation(qkv[(st.i + shift) % 2][:, c, :], shared[bank][:, 0:GT], ACT.Identity,
                               bias=bq_sb[:, c:c + 1]).then_inc(s_free[bank], 1)

            def put_xT(st, shift):
                for c in range(KD):
                    bank, nth = use("xt", st, shift, c)
                    wait(act, s_full[bank], st, nth)
                    act.activation(xT_hi[:, c, :], shared[bank][:, 0:GT], ACT.Copy).then_inc(s_xT_hi, 1)

            def put_exp(st, u):
                wait(act, s_sub, st, lambda i: UNITS * i + u + 2)
                e = expo[(u + 1) % 2][:, :, :]
                act.activation(e, e, ACT.Exp, scale=SCALE).then_inc(s_exp, 1)

            def put_ctx(st, u):
                wait(act, s_ctx, st, lambda i: UNITS * i + u + 1)
                act.activation(ctx_hi[:, UP * (u % 2):UP * (u % 2 + 1), SEQ * (u // 2):SEQ * (u // 2 + 1)],
                               ct_ps[:, 0:UP * SEQ].rearrange("p (k n) -> p k n", k=UP), ACT.Copy)\
                    .then_inc(s_c_hi, 1)

            def put_y(st, shift):
                for c in range(KD):
                    bank, nth = use("proj", st, shift, c)
                    wait(act, s_full[bank], st, nth)
                    act.activation(yT[:, c, :], shared[bank][:, 0:GT], ACT.Identity,
                                   bias=bl_sb[:, c:c + 1]).then_inc(s_free[bank], 1)

            def put_gap(st, shift):
                wait(act, s_gap, st, lambda i: i + shift + 1)
                act.activation(e_gap[:, :], gap[:, :], ACT.Exp).then_inc(s_egap, 1)

            def put_x2T(st, shift):
                for c in range(KD):
                    bank, nth = use("x2t", st, shift, c)
                    wait(act, s_full[bank], st, nth)
                    act.activation(x2T[:, c, :], shared[bank][:, 0:GT], ACT.Copy).then_inc(s_free[bank], 1)

            act.wait_ge(s_const, 48)
            put_xT(Step(0), 0)
            act.wait_ge(s_wl_lo, 2)
            for n, c in enumerate(START):
                put_qkv(Step(0), 0, c)
                if n == 11:
                    put_exp(Step(-1), UNITS - 1)

            def stage_b(st):
                more, before = st.i + 1 < GROUPS, st.i >= 1
                for u in range(UNITS):
                    blocks = list(qkv_of(u)) if more else []
                    if u == 4 and before:
                        put_x2T(st, -1)
                    ahead = 3 if u == 1 else 2
                    for c in blocks[:-1][:ahead]:
                        put_qkv(st, 1, c)
                    if u == 0 and before:
                        put_y(st, -1)
                    if u == 0 and more:
                        put_xT(st, 1)
                    if u == UNITS - 1:
                        put_ctx(st, u)
                    if more or u + 1 < UNITS:
                        put_exp(st, u)
                    for c in blocks[:-1][ahead:]:
                        put_qkv(st, 1, c)
                    if u < UNITS - 1:
                        put_ctx(st, u)
                    for c in blocks[-1:]:
                        put_qkv(st, 1, c)
                    if u == 7 and before:
                        put_gap(st, -1)

            sweep(act, stage_b, GROUPS, 1, 1, 2)
            put_y(Step(GROUPS), -1)
            put_x2T(Step(GROUPS), -1)
            put_gap(Step(GROUPS), -1)

            def split_fc(st, shift, q):
                wait(act, s_fcl, st, lambda i: 16 * (i + shift + 1))
                wait(act, s_mid, st, lambda i: KF * (i + shift))
                w = slice(q * FF // 4, (q + 1) * FF // 4)
                act.activation(fc_hi[:, :, w], raw_fc[:, :, w], ACT.Copy).then_inc(s_fc_hi, 1)

            def split_pj(st, q):
                wait(act, s_pjl, st, lambda i: 16 * (i + 1))
                wait(act, s_y, st, lambda i: XT * i)
                w = slice(q * KF // 4, (q + 1) * KF // 4)
                act.activation(pj_hi[:, w, :], raw_pj[:, w, :], ACT.Copy).then_inc(s_pj_hi, 1)

            def put_xe(st, shift):
                for n in range(2 * KD):
                    c, h = n // 2, n % 2
                    wait(act, s_xe, st, lambda i: 2 * KD * (i + shift) + n + 1)
                    bank = (vt_ps, ct_ps)[h]
                    act.activation(xe_hi[:, c, h * 3 * XR:(h + 1) * 3 * XR], bank[:, 0:3 * XR], ACT.Copy)\
                        .then_inc(s_xe_hi, 1)

            for q in range(4):
                split_fc(Step(0), 0, q)
            put_xe(Step(0), 0)

            def stage_d(st):
                for f in range(KF):
                    wait(act, s_mid, st, lambda i: KF * i + f + 1)
                    wait(act, s_act_lo, st, lambda i: KF * i + f - 1)
                    for h, (a, b) in enumerate(HALVES):
                        gelu = act.activation(act_f[f % 2][:, a:b], pair[f % 2][:, h, 0:b - a], ACT.Gelu)
                    gelu.then_inc(s_gelu, 1)
                    if f < 4:
                        split_pj(st, f)
                if st.i + 1 < NEXP:
                    for q in range(4):
                        split_fc(st, 1, q)
                    put_xe(st, 1)

            sweep(act, stage_d, NEXP, 1, 1, 2)

        @block.vector
        def _(dve):
            def norm_patches(st, shift):
                p = (st.i + shift) % 2
                wait(dve, s_patch[p], st, lambda i: 16 * ((i + shift) // 2 + 1))
                x = patch[p]
                for h in range(2):
                    stats = dve.bn_stats(a_stat[:, h, :], x[:, h * 384:(h + 1) * 384])
                stats.then_inc(s_a_ln, 1)
                wait(dve, s_pn, st, lambda i: i + shift)
                wait_apart(dve, s_a_ln, st, lambda i: 3 * (i + shift) + 1)
                dve.bn_aggr(a_mv[:, :], a_stat[:, :, :].rearrange("p a b -> p (a b)")).then_inc(s_a_ln, 1)
                wait(dve, s_a_ln, st, lambda i: 3 * (i + shift) + 2)
                dve.tensor_scalar(a_rs[:, :], a_mv[:, 1:2], EPS, None, ALU.add).then_inc(s_a_ln, 1)

            def low_patches(st):
                p = st.i % 2
                for h in range(2):
                    wait(dve, s_pT_hi, st, lambda i: 2 * i + h + 1)
                    dve.tensor_tensor(pT_lo[p][:, 3 * h:3 * h + 3, :],
                                      pair[p][:, h, 0:384].rearrange("p (k n) -> p k n", k=3),
                                      f32(pT_hi[p][:, 3 * h:3 * h + 3, :]), ALU.subtract).then_inc(s_pT_lo, 1)

            def norm_z(st):
                p = (st.i - 1) % 2
                z = z_row[p][:, :]
                wait(dve, s_z, st, lambda i: i)
                wait(dve, s_zdma[p], st, lambda i: 16 * ((i - 1) // 2))
                dve.tensor_tensor(z, shared[p][:, 0:D], zb_sb[:, :], ALU.add).then_inc(s_z1, 1)
                wait(dve, s_z1, st, lambda i: i)
                dve.bn_stats(z_stat[:, :], z).then_inc(s_z_ln, 1)
                wait_apart(dve, s_z_ln, st, lambda i: 3 * (i - 1) + 1)
                dve.bn_aggr(z_mv[:, :], z_stat[:, :]).then_inc(s_z_ln, 1)
                wait(dve, s_z_ln, st, lambda i: 3 * (i - 1) + 2)
                dve.tensor_scalar(z_rs[:, :], z_mv[:, 1:2], EPS, None, ALU.add).then_inc(s_z_ln, 1)

            def norm_z_end(st):
                z = z_row[st.i % 2][:, :]
                wait(dve, s_z_rs, st, lambda i: i - 1)
                dve.tensor_scalar(z, z, z_mv[:, 0:1], z_rs[:, 0:1], ALU.subtract, ALU.mult).then_inc(s_zn, 1)

            def rows_of(st, shift):
                g = st.of(lambda i: i + shift)
                if st.k is None:
                    return [rows[:, g * TPG + t, 0:D] for t in range(TPG)]
                return [rows[:, bass.ds(g * TPG + t, 1), 0:D].rearrange("p o d -> p (o d)") for t in range(TPG)]

            def norm_in(st, shift):
                src = rows_of(st, shift)
                wait(dve, s_h, st, lambda i: i + shift + 1)
                for t in range(TPG):
                    stats = dve.bn_stats(n_stat[:, t, :], src[t])
                stats.then_inc(s_n_ln, 1)
                wait_apart(dve, s_n_ln, st, lambda i: 3 * (i + shift) + 1)
                for t in range(TPG):
                    stats = dve.bn_aggr(n_mv[:, t, :], n_stat[:, t, :])
                stats.then_inc(s_n_ln, 1)
                wait(dve, s_n_ln, st, lambda i: 3 * (i + shift) + 2)
                dve.tensor_scalar(n_rs[:, :], n_mv[:, :, 1], EPS, None, ALU.add).then_inc(s_n_ln, 1)

            def low_wl(h):
                dve.wait_ge(s_wl_hi, h + 1)
                w = slice(h * PAIRS // 2, (h + 1) * PAIRS // 2)
                dve.tensor_tensor(wl_lo[:, w, :], wl_raw[:, w, :], f32(wl_hi[:, w, :]), ALU.subtract).then_inc(s_wl_lo, 1)

            def norm_in_end(st, shift):
                src = rows_of(st, shift)
                wait(dve, s_n_rs, st, lambda i: i + shift + 1)
                for t in range(TPG):
                    done = dve.tensor_scalar(xn[:, t, :], src[t], n_mv[:, t, 0:1], n_rs[:, t:t + 1],
                                             ALU.subtract, ALU.mult)
                done.then_inc(s_xn, 1)

            norm_patches(Step(0), 0)
            dve.wait_ge(s_gain, 32)
            dve.tensor_copy(b1_wide, b1_sb[:, :].unsqueeze(2).broadcast_to([128, KP, 128])).then_inc(s_b1w, 1)
            for k in range(KP):
                dve.wait_ge(s_wp_hi, k + 1)
                dve.scalar_tensor_tensor(wp_lo[:, k, :], wp_raw[:, k, :], g1_sb[:, k:k + 1], f32(wp_hi[:, k, :]),
                                         ALU.mult, ALU.subtract).then_inc(s_wp_lo, 1)

            def stage_a(st):
                if st.i + 1 < PT:
                    norm_patches(st, 1)
                if st.i >= 2:
                    norm_z_end(st)
                if st.i < PT:
                    low_patches(st)
                if st.i == 1:
                    dve.wait_ge(s_bw, 1)
                    dve.wait_ge(s_small, 48)
                    dve.tensor_tensor(zb_sb[:, :], zb_sb[:, :], vt_ps[:, 0:D], ALU.add).then_inc(s_zb, 1)
                    dve.wait_ge(s_zb, 1)
                if 1 <= st.i <= PT:
                    norm_z(st)
                if st.i == PT - 1:
                    norm_in(Step(0), 0)
                if st.i == PT:
                    norm_in_end(Step(0), 0)
                if st.i in PIECES:
                    w = piece(st)
                    wait(dve, s_wq_hi, st, lambda i: i - 1)
                    dve.tensor_tensor(wq_lo[:, 1, w], wq_raw[:, 1, w], f32(wq_hi[:, 1, w]), ALU.subtract)\
                        .then_inc(s_wq_lo2, 1)
                if st.i == PT:
                    low_wl(0)

            sweep(dve, stage_a, PT + 2, 3, 4, 2)

            def low_xT(st, shift):
                for c in range(KD):
                    bank, nth = use("xt", st, shift, c)
                    wait(dve, s_xT_hi, st, lambda i: KD * (i + shift) + c + 1)
                    dve.tensor_tensor(xT_lo[:, c, :], shared[bank][:, 0:GT], f32(xT_hi[:, c, :]), ALU.subtract)\
                        .then_inc(s_xT_lo, 1)
                    dve.wait_ge(s_xT_lo, st.of(lambda i: KD * (i + shift) + c + 1))
                    dve.sem_inc(s_free[bank], 1)

            def take_max(st, u):
                sc = pair[u % 2][0:SEQ, :, 0:UP * SEQ].rearrange("s e (q k) -> s e q k", k=SEQ)
                tp = top[:, :].rearrange("s (e q) -> s e q", e=2)
                ex = expo[u % 2][:, :, :].rearrange("s (e q) k -> s e q k", e=2)
                wait(dve, s_score, st, lambda i: UNITS * i + u + 1)
                dve.tensor_reduce(tp, sc, AX, ALU.max).then_inc(s_top, 1)
                wait(dve, s_top, st, lambda i: UNITS * i + u + 1)
                wait(dve, s_ctx, st, lambda i: UNITS * i + u - 1)
                dve.tensor_tensor(ex, sc, tp.unsqueeze(3).broadcast_to([SEQ, 2, UP, SEQ]), ALU.subtract)\
                    .then_inc(s_sub, 1)

            def weigh_values(st, u):
                wait(dve, s_exp, st, lambda i: UNITS * i + u + 1)
                dve.tensor_reduce(zsum[:, :], expo[u % 2][:, :, :], AX, ALU.add).then_inc(s_zs, 1)
                wait(dve, s_zs, st, lambda i: UNITS * i + u + 1)
                dve.reciprocal(zinv[:, :], zsum[:, :]).then_inc(s_zi, 1)
                wait(dve, s_zi, st, lambda i: UNITS * i + u + 1)
                wait(dve, s_vt, st, lambda i: UNITS * i + u + 1)
                wait(dve, s_ctx, st, lambda i: UNITS * i + u - 1)
                zi = zinv[:, :].rearrange("s (e q) -> s q e", e=2).unsqueeze(3).broadcast_to([SEQ, UP, 2, HD])
                dve.tensor_tensor(vals[u % 2][:, :, :].rearrange("s (q e) d -> s q e d", e=2),
                                  vt_ps[0:SEQ, :].rearrange("s (q e d) -> s q e d", e=2, d=HD), zi, ALU.mult)\
                    .then_inc(s_val, 1)

            def low_ctx(st, u):
                at = (slice(None), slice(UP * (u % 2), UP * (u % 2 + 1)), slice(SEQ * (u // 2), SEQ * (u // 2 + 1)))
                wait(dve, s_c_hi, st, lambda i: UNITS * i + u + 1)
                dve.tensor_tensor(ctx_lo[at], ct_ps[:, 0:UP * SEQ].rearrange("p (k n) -> p k n", k=UP),
                                  f32(ctx_hi[at]), ALU.subtract).then_inc(s_c_lo, 1)

            def residual(st, shift):
                g = st.of(lambda i: i + shift)
                parts = ((0, 1), (1, TPG))
                for n, (a, b) in enumerate(parts):
                    bank, nth = use("ytr", st, shift, n)
                    wait(dve, s_full[bank], st, nth)
                    src = rows[:, g * TPG + a:g * TPG + b, 0:D] if st.k is None else rows[:, bass.ds(g * TPG + a, b - a), 0:D]
                    dve.tensor_tensor(h2[:, a:b, :], shared[bank][0:TR, 0:(b - a) * D].rearrange("p (t d) -> p t d", d=D),
                                      src, ALU.add).then_inc(s_free[bank], 1)

            def norm_mid(st, shift):
                for n in range(2):
                    bank, nth = use("ytr", st, shift, n)
                    wait(dve, s_free[bank], st, nth)
                dve.sem_inc(s_h2, 1)
                for t in range(TPG):
                    stats = dve.bn_stats(m_stat[:, t, :], h2[:, t, :])
                stats.then_inc(s_m_ln, 1)
                wait_apart(dve, s_m_ln, st, lambda i: 3 * (i + shift) + 1)
                for t in range(TPG):
                    stats = dve.bn_aggr(m_mv[:, t, :], m_stat[:, t, :])
                stats.then_inc(s_m_ln, 1)
                wait(dve, s_m_ln, st, lambda i: 3 * (i + shift) + 2)
                dve.tensor_scalar(m_rs[:, :], m_mv[:, :, 1], EPS, None, ALU.add).then_inc(s_m_ln, 1)

            def norm_mid_end(st, shift):
                wait(dve, s_m_rs, st, lambda i: i + shift + 1)
                for t in range(TPG):
                    done = dve.tensor_scalar(sent[:, t, 0:D], h2[:, t, :], m_mv[:, t, 0:1], m_rs[:, t:t + 1],
                                             ALU.subtract, ALU.mult)
                done.then_inc(s_x2, 1)

            def put_logits(st, shift):
                bank, nth = use("logit", st, shift, 0)
                wait(dve, s_h2_out, st, lambda i: 16 * (i + shift + 1))
                wait(dve, s_full[bank], st, nth)
                dve.tensor_copy(logits[:, :, :], shared[bank][0:TR, 0:TPG * NEXP].rearrange("p (t e) -> p t e", e=NEXP))\
                    .then_inc(s_free[bank], 1)

            def pick(st, shift, k):
                at = 6 * k
                src = (logits, rest)[k][:, :, :]

                def before(n):
                    wait(dve, s_pick, st, lambda i: PICKS * (i + shift) + n)

                def wide(ap):
                    return ap.unsqueeze(2).broadcast_to([TR, TPG, NEXP])

                if k == 0:
                    bank, nth = use("logit", st, shift, 0)
                    wait(dve, s_free[bank], st, nth)
                else:
                    before(at)
                dve.tensor_reduce(best[:, k, :], src, AX, ALU.max).then_inc(s_pick, 1)
                before(at + 1)
                dve.tensor_tensor(is_top[:, :, :], src, wide(best[:, k, :]), ALU.is_equal).then_inc(s_pick, 1)
                before(at + 2)
                dve.scalar_tensor_tensor(cand[:, :, :], is_top[:, :, :], -float(NEXP), expert[:, :, :], ALU.mult, ALU.add)\
                    .then_inc(s_pick, 1)
                before(at + 3)
                dve.tensor_reduce(first[:, k, :], cand[:, :, :], AX, ALU.min).then_inc(s_pick, 1)
                before(at + 4)
                dve.scalar_tensor_tensor(chosen[:, :, k, :], expert[:, :, :], -float(NEXP), wide(first[:, k, :]),
                                         ALU.add, ALU.is_equal).then_inc(s_pick, 1)
                before(at + 5)
                if k == 0:
                    dve.scalar_tensor_tensor(rest[:, :, :], chosen[:, :, 0, :], -3.0e38, logits[:, :, :], ALU.mult, ALU.add)\
                        .then_inc(s_pick, 1)
                else:
                    dve.tensor_copy(chosen_b[:, :, :], chosen[:, :, :, :].rearrange("p t k e -> p t (k e)"))\
                        .then_inc(s_chosen, 1)

            def place(st, shift):
                bank, nth = use("rank", st, shift, 0)
                flat = "p t k e -> p t (k e)"

                def before(n):
                    wait(dve, s_place, st, lambda i: PLACED * (i + shift) + n)

                wait(dve, s_full[bank], st, nth)
                dve.tensor_tensor(rank[:, :, :], shared[bank][0:TR, 0:TPG * CHOICES].rearrange("p (t c) -> p t c", c=CHOICES),
                                  carry[0:TR, :].unsqueeze(1).broadcast_to([TR, TPG, CHOICES]), ALU.add).then_inc(s_rank, 1)
                wait(dve, s_rank, st, lambda i: i + shift + 1)
                dve.tensor_tensor(carry[:, :], carry[:, :], shared[bank][0:XR, TPG * CHOICES:(TPG + 1) * CHOICES], ALU.add)\
                    .then_inc(s_free[bank], 1)
                dve.tensor_tensor(over[:, :, :], rank[:, :, :], limit[0:TR, :, :, :].rearrange(flat), ALU.is_ge).then_inc(s_place, 1)
                before(1)
                dve.scalar_tensor_tensor(over[:, :, :], over[:, :, :], float(FAR), rank[:, :, :], ALU.mult, ALU.add)\
                    .then_inc(s_place, 1)
                before(2)
                dve.tensor_tensor(over[:, :, :], over[:, :, :], chosen[:, :, :, :].rearrange(flat), ALU.mult).then_inc(s_place, 1)
                before(3)
                dve.tensor_reduce(slot_f[:, :, :], over[:, :, :].rearrange("p t (k e) -> p t k e", e=NEXP), AX, ALU.add)\
                    .then_inc(s_place, 1)
                before(4)
                wait(dve, s_m_rs, st, lambda i: i + shift + 1)
                dve.tensor_copy(slot_ix[:, :, :], slot_f[:, :, :]).then_inc(s_place, 1)
                wait(dve, s_free[bank], st, nth)

            low_xT(Step(0), 0)
            low_wl(1)
            take_max(Step(0), 0)

            def stage_b(st):
                more, before = st.i + 1 < GROUPS, st.i >= 1
                for u in range(UNITS):
                    if u == 0 and st.i == 0:
                        dve.wait_ge(s_masks, 9)
                    if u == 0 and more:
                        norm_in(st, 1)
                    if u == 2 and before:
                        residual(st, -1)
                    weigh_values(st, u)
                    if u == 0 and more:
                        norm_in_end(st, 1)
                    if u == 5 and before:
                        put_logits(st, -1)
                    if u == 7 and before:
                        place(st, -1)
                    if u == UNITS - 1:
                        low_ctx(st, u)
                    if u + 1 < UNITS:
                        take_max(st, u + 1)
                    elif more:
                        take_max(Step(st.i + 1, st.k, st.span), 0)
                    if u == 2 and before:
                        norm_mid(st, -1)
                    if u == 3 and before:
                        norm_mid_end(st, -1)
                    if u == 5 and before:
                        pick(st, -1, 0)
                    if u == 6 and before:
                        pick(st, -1, 1)
                    if u == 0 and more:
                        low_xT(st, 1)
                    if u < UNITS - 1:
                        low_ctx(st, u)

            sweep(dve, stage_b, GROUPS, 1, 1, 2)
            last = Step(GROUPS)
            residual(last, -1)
            norm_mid(last, -1)
            norm_mid_end(last, -1)
            put_logits(last, -1)
            pick(last, -1, 0)
            pick(last, -1, 1)
            place(last, -1)

            begin = carry[:, 0:NEXP].unsqueeze(2).broadcast_to([XR, NEXP, XT])
            dve.scalar_tensor_tensor(shift_by[:, :], limit[:, 0, 0, :], float(NSLOT - CAP), carry[:, 0:NEXP],
                                     ALU.add, ALU.subtract).then_inc(s_found, 1)
            dve.tensor_tensor(second[:, :, :], place_of[:, :, :], begin, ALU.is_ge).then_inc(s_found, 1)
            dve.wait_ge(s_found, 2)
            dve.tensor_tensor(second[:, :, :], second[:, :, :], shift_by[:, :].unsqueeze(2).broadcast_to([XR, NEXP, XT]),
                              ALU.mult).then_inc(s_found, 1)
            dve.wait_ge(s_found, 3)
            dve.tensor_tensor(found[:, :, :], second[:, :, :], place_of[:, :, :], ALU.add).then_inc(s_found, 1)
            dve.wait_ge(s_found, FOUND)

            def index(st, shift):
                e = st.of(lambda i: i + shift)
                src = found[:, e, :] if st.k is None else found[:, bass.ds(e, 1), :].rearrange("p o t -> p (o t)")
                dve.tensor_copy(found_ix[(st.i + shift) % 2][:, :], src).then_inc(s_found_ix, 1)

            index(Step(0), 0)

            def low_fc(st, shift, q):
                wait(dve, s_fc_hi, st, lambda i: 4 * (i + shift) + q + 1)
                w = slice(q * FF // 4, (q + 1) * FF // 4)
                dve.tensor_tensor(fc_lo[:, :, w], raw_fc[:, :, w], f32(fc_hi[:, :, w]), ALU.subtract).then_inc(s_fc_lo, 1)

            def low_pj(st, q):
                wait(dve, s_pj_hi, st, lambda i: 4 * i + q + 1)
                w = slice(q * KF // 4, (q + 1) * KF // 4)
                dve.tensor_tensor(pj_lo[:, w, :], raw_pj[:, w, :], f32(pj_hi[:, w, :]), ALU.subtract).then_inc(s_pj_lo, 1)

            def low_xe(st, shift, c):
                for h in range(2):
                    n = 2 * c + h
                    w = slice(h * 3 * XR, (h + 1) * 3 * XR)
                    wait(dve, s_xe_hi, st, lambda i: 2 * KD * (i + shift) + n + 1)
                    dve.tensor_tensor(xe_lo[:, c, w], (vt_ps, ct_ps)[h][:, 0:3 * XR], f32(xe_hi[:, c, w]), ALU.subtract)\
                        .then_inc(s_xe_lo, 1)

            for q in range(4):
                low_fc(Step(0), 0, q)
            for c in range(KD):
                low_xe(Step(0), 0, c)

            def stage_d(st):
                p = st.i % 2
                col = D + 1 + st.of(lambda i: i)
                if st.i + 1 < NEXP:
                    index(st, 1)

                def put_y(t):
                    wait(dve, s_y, st, lambda i: XT * i + t + 1)
                    w = xg[p][:, t, col:col + 1] if st.k is None else xg[p][:, t, bass.ds(col, 1)]
                    dve.tensor_scalar(yrow[p][:, t, :], y_banks[t][0:XR, 0:D], w, None, ALU.mult).then_inc(s_yrow, 1)

                for f in range(KF):
                    wait(dve, s_gelu, st, lambda i: KF * i + f + 1)
                    if f == 0:
                        wait(dve, s_y, st, lambda i: XT * i)
                    dve.tensor_copy(act_hi[:, f, :], act_f[f % 2][:, :]).then_inc(s_act_hi, 1)
                    wait(dve, s_act_hi, st, lambda i: KF * i + f + 1)
                    dve.tensor_tensor(act_lo[:, f, :], act_f[f % 2][:, :], f32(act_hi[:, f, :]), ALU.subtract)\
                        .then_inc(s_act_lo, 1)
                    if f < 4:
                        low_pj(st, f)
                more = st.i + 1 < NEXP
                for t in range(XT // 2):
                    if more:
                        low_fc(st, 1, t)
                    put_y(t)
                if more:
                    low_fc(st, 1, 3)
                    low_xe(st, 1, 0)
                put_y(3)
                if more:
                    low_xe(st, 1, 1)
                for t in range(4, XT):
                    put_y(t)
                wait(dve, s_added, st, lambda i: 16 * XT * i)
                if st.k is not None:
                    dve.nop(nofuse=True)

            sweep(dve, stage_d, NEXP, 1, 1, 2)

        @block.tensor
        def _(pe):
            def three(dst, terms, first=True, last=True):
                for n, (l_hi, l_lo, r_hi, r_lo) in enumerate(terms):
                    pe.matmul(dst, l_hi, r_hi, start=(first and n == 0), stop=False)
                    pe.matmul(dst, l_hi, r_lo, start=False, stop=False)
                    done = pe.matmul(dst, l_lo, r_hi, start=False, stop=(last and n == len(terms) - 1))
                return done

            def turn_patches(st, shift):
                p = (st.i + shift) % 2
                wait(pe, s_pn, st, lambda i: i + shift + 1)
                wait(pe, s_pT_lo, st, lambda i: 2 * (i + shift - 1))
                for k in range(KP):
                    done = pe.transpose(pair[p][:, k // 3, k % 3 * 128:(k % 3 + 1) * 128],
                                        patch[p][:, k * 128:(k + 1) * 128], ident[:, :])
                done.then_inc(s_pT, 1)

            def project(st):
                p = st.i % 2
                wait(pe, s_pT_lo, st, lambda i: 2 * (i + 1))
                wait(pe, s_z1, st, lambda i: i - 1)
                three(shared[p][:, 0:D], [(pT_hi[p][:, k, :], pT_lo[p][:, k, :], wp_hi[:, k, :], wp_lo[:, k, :])
                                          for k in range(KP)]).then_inc(s_z, 1)

            pe.wait_ge(s_ident, 16)
            turn_patches(Step(0), 0)
            pe.wait_ge(s_b1w, 1)
            pe.wait_ge(s_wp, 16)
            for k in range(KP):
                done = pe.matmul(vt_ps[:, 0:D], b1_wide[:, k, :], wp_raw[:, k, :], start=(k == 0), stop=(k == KP - 1))
            done.then_inc(s_bw, 1)
            pe.wait_ge(s_wp_lo, KP)

            def stage_a(st):
                if st.i + 1 < PT:
                    turn_patches(st, 1)
                if st.i < PT:
                    project(st)

            sweep(pe, stage_a, PT + 2, 3, 4, 2)

            def free(st, kind, shift, c):
                bank, nth = use(kind, st, shift, c)
                wait(pe, s_free[bank], st, lambda i: nth(i) - 1)
                return bank

            def taken(st, kind, shift, blocks):
                for bank in range(2):
                    mine = [c for c in blocks if USE[(kind, st.i + shift, c)][0] == bank]
                    if mine:
                        wait(pe, s_free[bank], st, lambda i: USE[(kind, i + shift, mine[-1])][1])

            def ready(st, kind, nxt, shift):
                if use(kind, st, shift, KD - 1)[0] != use(nxt, st, shift, 0)[0]:
                    taken(st, kind, shift, [KD - 1])

            def turn_x(st, shift, blocks=range(KD)):
                wait(pe, s_xn, st, lambda i: i + shift + 1)
                for c in blocks:
                    bank = free(st, "xt", shift, c)
                    for t in range(TPG):
                        done = pe.transpose(shared[bank][:, t * TR:(t + 1) * TR], xn[:, t, c * 128:(c + 1) * 128],
                                            ident[0:TR, 0:TR])
                    done.then_inc(s_full[bank], 1)

            def project_qkv(st, shift, c):
                if c == 0:
                    wait(pe, s_xT_lo, st, lambda i: KD * (i + shift + 1))
                bank = free(st, "qkv", shift, c)
                w = slice(c * 128, (c + 1) * 128)
                three(shared[bank][:, 0:GT], [(wq_hi[:, k, w], wq_lo[:, k, w], xT_hi[:, k, :], xT_lo[:, k, :])
                                              for k in range(KD)]).then_inc(s_full[bank], 1)

            def turn_values(st, u):
                b, h = u // 2, u % 2
                blocks = range(2 * PAIRS + UP * h, 2 * PAIRS + UP * (h + 1))
                taken(st, "qkv", 0, blocks)
                wait(pe, s_val, st, lambda i: UNITS * i + u)
                for q, c in enumerate(blocks):
                    done = pe.transpose(vt_ps[0:SEQ, q * 128:(q + 1) * 128],
                                        qkv[st.i % 2][:, c, b * SEQ:(b + 1) * SEQ], ident[:, :])
                done.then_inc(s_vt, 1)

            def score(st, u):
                b, h = u // 2, u % 2
                s = slice(b * SEQ, (b + 1) * SEQ)
                taken(st, "qkv", 0, range(2 * UP * h, 2 * UP * (h + 1)))
                wait(pe, s_sub, st, lambda i: UNITS * i + u - 1)
                for q in range(UP):
                    for e in range(2):
                        c, r = 2 * (UP * h + q), slice(HD * e, HD * (e + 1))
                        done = pe.matmul(pair[u % 2][0:SEQ, e, q * SEQ:(q + 1) * SEQ], qkv[st.i % 2][r, c + 1, s],
                                         qkv[st.i % 2][r, c, s], start=True, stop=True)
                done.then_inc(s_score, 1)

            def context(st, u):
                wait(pe, s_exp, st, lambda i: UNITS * i + u + 1)
                wait(pe, s_val, st, lambda i: UNITS * i + u + 1)
                wait(pe, s_c_lo, st, lambda i: UNITS * i + u)
                for q in range(UP):
                    for e in range(2):
                        done = pe.matmul(ct_ps[HD * e:HD * (e + 1), q * SEQ:(q + 1) * SEQ], vals[u % 2][:, 2 * q + e, :],
                                         expo[u % 2][:, UP * e + q, :], start=True, stop=True)
                done.then_inc(s_ctx, 1)

            def project_out(st, shift):
                wait(pe, s_c_lo, st, lambda i: UNITS * (i + shift + 1))
                for c in range(KD):
                    bank = free(st, "proj", shift, c)
                    w = slice(c * 128, (c + 1) * 128)
                    three(shared[bank][:, 0:GT], [(wl_hi[:, k, w], wl_lo[:, k, w], ctx_hi[:, k, :], ctx_lo[:, k, :])
                                                  for k in range(PAIRS)]).then_inc(s_full[bank], 1)

            def turn_y(st, shift):
                ready(st, "proj", "ytr", shift)
                for n, tiles in enumerate((range(1), range(1, TPG))):
                    bank = free(st, "ytr", shift, n)
                    for t in tiles:
                        for c in range(KD):
                            at = (t - tiles[0]) * D + c * 128
                            done = pe.transpose(shared[bank][0:TR, at:at + 128], yT[:, c, t * TR:(t + 1) * TR], ident[:, :])
                    done.then_inc(s_full[bank], 1)

            def turn_x2(st, shift):
                wait(pe, s_x2, st, lambda i: i + shift + 1)
                for c in range(KD):
                    bank = free(st, "x2t", shift, c)
                    for t in range(TPG):
                        done = pe.transpose(shared[bank][:, t * TR:(t + 1) * TR], sent[:, t, c * 128:(c + 1) * 128],
                                            ident[0:TR, 0:TR])
                    done.then_inc(s_full[bank], 1)

            def logit(st, shift):
                ready(st, "x2t", "logit", shift)
                bank = free(st, "logit", shift, 0)
                for t in range(TPG):
                    for c in range(KD):
                        done = pe.matmul(shared[bank][0:TR, t * NEXP:(t + 1) * NEXP], x2T[:, c, t * TR:(t + 1) * TR],
                                         wg_sb[:, c, :], start=(c == 0), stop=(c == KD - 1))
                done.then_inc(s_full[bank], 1)

            def count(st, shift):
                wait(pe, s_chosen, st, lambda i: i + shift + 1)
                bank = free(st, "rank", shift, 0)
                for t in range(TPG):
                    for b in range(t + 1):
                        pe.matmul(shared[bank][0:TR, t * CHOICES:(t + 1) * CHOICES], (tri[:, :] if b == t else ones[:, 0:TR]),
                                  chosen_b[:, b, :], start=(b == 0), stop=(b == t))
                for b in range(TPG):
                    done = pe.matmul(shared[bank][0:XR, TPG * CHOICES:(TPG + 1) * CHOICES], ones[:, :],
                                     chosen_b[:, b, :], start=(b == 0), stop=(b == TPG - 1))
                done.then_inc(s_full[bank], 1)

            pe.wait_ge(s_z1, PT)
            pe.wait_ge(s_zb, 1)
            turn_x(Step(0), 0)
            pe.wait_ge(s_wq_lo, len(PIECES))
            pe.wait_ge(s_wq_lo2, len(PIECES))
            for n, c in enumerate(START):
                project_qkv(Step(0), 0, c)
                if n == 9:
                    score(Step(0), 0)
            pe.wait_ge(s_const, 48)
            pe.wait_ge(s_wl_lo, 2)
            pe.wait_ge(s_masks, 5)

            def stage_b(st):
                more, before = st.i + 1 < GROUPS, st.i >= 1
                for u in range(UNITS):
                    if u == 2 and before:
                        turn_y(st, -1)
                    turn_values(st, u)
                    if u + 1 < UNITS:
                        score(st, u + 1)
                    elif more:
                        score(Step(st.i + 1, st.k, st.span), 0)
                    if u == 0 and before:
                        project_out(st, -1)
                    if u == 0 and more:
                        turn_x(st, 1, range(1))
                    if u == 4 and before:
                        turn_x2(st, -1)
                    if u == 5 and before:
                        logit(st, -1)
                    if u == 7 and before:
                        count(st, -1)
                    blocks = list(qkv_of(u)) if more else []
                    for c in blocks[:-1]:
                        project_qkv(st, 1, c)
                    context(st, u)
                    if u == 0 and more:
                        turn_x(st, 1, range(1, KD))
                    for c in blocks[-1:]:
                        project_qkv(st, 1, c)

            sweep(pe, stage_b, GROUPS, 1, 1, 2)
            last = Step(GROUPS)
            project_out(last, -1)
            turn_y(last, -1)
            turn_x2(last, -1)
            logit(last, -1)

            count(last, -1)

            def turn_slots(st, shift, c):
                p = (st.i + shift) % 2
                wait(pe, s_xg[p], st, lambda i: 16 * XT * ((i + shift) // 2 + 1))
                for h in range(2):
                    n = 2 * c + h
                    wait(pe, s_xe_lo, st, lambda i: 2 * KD * (i + shift) + n - 1)
                    for t in range(3):
                        done = pe.transpose((vt_ps, ct_ps)[h][:, t * XR:(t + 1) * XR],
                                            xg[p][:, 3 * h + t, c * 128:(c + 1) * 128], ident[0:XR, 0:XR])
                    done.then_inc(s_xe, 1)

            for c in range(KD):
                turn_slots(Step(0), 0, c)

            def multiply(st, t, blocks):
                r = slice(t * XR, (t + 1) * XR)
                return three(y_banks[t][0:XR, 0:D],
                             [(act_hi[:, f, r], act_lo[:, f, r], pj_hi[:, f, :], pj_lo[:, f, :]) for f in blocks],
                             first=blocks[0] == 0, last=blocks[-1] == KF - 1)

            def stage_d(st):
                wait(pe, s_xe_lo, st, lambda i: 2 * KD * (i + 1))
                wait(pe, s_fc_lo, st, lambda i: 4 * (i + 1))
                for f in range(KF):
                    wait(pe, s_gelu, st, lambda i: KF * i + f - 1)
                    if f == 0:
                        wait(pe, s_yrow, st, lambda i: XT * i - 2)
                    w = slice(f * 128, (f + 1) * 128)
                    for h, (a, b) in enumerate(HALVES):
                        done = three(pair[f % 2][:, h, 0:b - a],
                                     [(fc_hi[:, k, w], fc_lo[:, k, w], xe_hi[:, k, a:b], xe_lo[:, k, a:b]) for k in range(KD)])
                    done.then_inc(s_mid, 1)
                wait(pe, s_pj_lo, st, lambda i: 4 * (i + 1))
                for t in range(2):
                    wait(pe, s_yrow, st, lambda i: XT * i + t - 1)
                for f in range(KF):
                    wait(pe, s_act_lo, st, lambda i: KF * i + f + 1)
                    for t in range(2):
                        done = multiply(st, t, range(f, f + 1))
                        if f == KF - 1:
                            done.then_inc(s_y, 1)
                for t in range(2, XT):
                    if t in (3, 4) and st.i + 1 < NEXP:
                        turn_slots(st, 1, t - 3)
                    if t >= 4:
                        wait(pe, s_yrow, st, lambda i: XT * i + t - 3)
                    multiply(st, t, range(KF)).then_inc(s_y, 1)

            sweep(pe, stage_d, NEXP, 1, 1, 2)


def kernel(x, txt, L0_tok_ln1_g, L0_tok_ln1_b, L0_tok_W_proj, L0_tok_b_proj, L0_tok_ln2_g, L0_tok_ln2_b,
           L0_tok_cls_token, L0_tok_pos_emb, L0_attn_q_w, L0_attn_q_b, L0_attn_k_w, L0_attn_k_b,
           L0_attn_v_w, L0_attn_v_b, L0_attn_l_w, L0_attn_l_b, L0_ffn_w_g, L0_ffn_c_fc, L0_ffn_c_proj):
    import numpy as np
    import concourse.bacc as bacc
    from concourse.bass_utils import run_bass_kernel_spmd

    def blocks(w):
        return np.asarray(w).reshape(PAIRS, 128, -1)

    side = 96 // 16
    p = np.asarray(x).reshape(BATCH, 3, side, 16, side, 16).transpose(0, 2, 4, 3, 5, 1)
    p = p.reshape(PT, 128, PD)
    q, k, v = blocks(L0_attn_q_w), blocks(L0_attn_k_w), blocks(L0_attn_v_w)
    w_qkv = np.concatenate([np.stack([q, k], 1).reshape(2 * PAIRS, 128, D), v]).transpose(2, 0, 1).reshape(D, NQKV * 128)
    q, k, v = blocks(L0_attn_q_b), blocks(L0_attn_k_b), blocks(L0_attn_v_b)
    b_qkv = np.concatenate([np.stack([q, k], 1).reshape(2 * PAIRS, 128), v.reshape(PAIRS, 128)]).T
    inputs = dict(
        patches=p, txt=txt, ln1_g=np.asarray(L0_tok_ln1_g).reshape(KP, 128).T,
        ln1_b=np.asarray(L0_tok_ln1_b).reshape(KP, 128).T, w_proj=L0_tok_W_proj,
        b_proj=np.asarray(L0_tok_b_proj).reshape(1, D), ln2_g=np.asarray(L0_tok_ln2_g).reshape(1, D),
        ln2_b=np.asarray(L0_tok_ln2_b).reshape(1, D), cls=np.asarray(L0_tok_cls_token).reshape(1, D),
        pos=np.asarray(L0_tok_pos_emb).reshape(NPATCH + 1, D), w_qkv=w_qkv, b_qkv=b_qkv,
        w_l=np.asarray(L0_attn_l_w).T, b_l=np.asarray(L0_attn_l_b).reshape(KD, 128).T, w_g=L0_ffn_w_g,
        c_fc=L0_ffn_c_fc, c_proj=L0_ffn_c_proj, ident_in=np.eye(128, dtype=np.float32))
    nc = bacc.Bacc("TRN2", target_bir_lowering=False, num_devices=1)
    arrays, args = {}, {}
    for name, a in inputs.items():
        arrays[name] = np.ascontiguousarray(a)
        args[name] = nc.dram_tensor(name, arrays[name].shape, mybir.dt.from_np(arrays[name].dtype), kind="ExternalInput").ap()
    out = nc.dram_tensor("out", (TOKENS, D), F32, kind="ExternalOutput").ap()
    program(nc, **args, out=out)
    r = run_bass_kernel_spmd(nc, [arrays], core_ids=[0])
    return r.results[0]["out"].reshape(BATCH, SEQ, D)
```
